# Optimizing a Trainium2 kernel written in Bass

```python
import numpy as np
import jax
import jax.numpy as jnp

def _softmax(x, axis=-1):
    return jax.nn.softmax(x, axis=axis)

def _gelu(x):
    return jax.nn.gelu(x, approximate=True)

def _silu(x):
    return jax.nn.silu(x)

def _sigmoid(x):
    return jax.nn.sigmoid(x)

def _layernorm(x, axis=-1, eps=1e-05):
    m = jnp.mean(x, axis=axis, keepdims=True)
    v = jnp.var(x, axis=axis, keepdims=True)
    return (x - m) / jnp.sqrt(v + eps)

def _scatter_add(tgt, idx, src, axis=0):
    return tgt.at[idx].add(src)

def _segment_sum(src, seg, n):
    return jax.ops.segment_sum(src, seg, n)
kernel_name = 'mk_hybrid_d1_jaxref_r8_f6c144'

def setup_inputs(seed: int=0):
    np.random.seed(seed)
    _w = jnp.asarray

    def _L0_attn_a_setup():
        import jax, jax.numpy as jnp
        import numpy as np

        def apply_rope(x):
            b, h, n, d = x.shape
            half = d // 2
            freqs = jnp.arange(0, half, dtype=x.dtype) / half
            theta = 1.0 / 1250 ** freqs
            positions = jnp.arange(n, dtype=x.dtype)
            angles = positions[:, None] * theta[None, :]
            cos = jnp.cos(angles)[None, None, :, :]
            sin = jnp.sin(angles)[None, None, :, :]
            x1 = x[..., ::2]
            x2 = x[..., 1::2]
            r1 = x1 * cos - x2 * sin
            r2 = x1 * sin + x2 * cos
            return jnp.stack([r1, r2], axis=-1).reshape(b, h, n, d)
        key = jax.random.key(seed)
        ks = jax.random.split(key, 4)
        B, N, D = (2, 256, 128)
        x = jax.random.normal(ks[0], (B, N, D), dtype=jnp.float32)
        w_qkv = jax.random.normal(ks[1], (D, 3 * D), dtype=jnp.float32) * (1.0 / np.sqrt(D))
        b_qkv = jnp.zeros((3 * D,), dtype=jnp.float32)
        w_out = jax.random.normal(ks[2], (D, D), dtype=jnp.float32) * (1.0 / np.sqrt(D))
        b_out = jnp.zeros((D,), dtype=jnp.float32)
        return {'x': x, 'w_qkv': w_qkv, 'b_qkv': b_qkv, 'w_out': w_out, 'b_out': b_out}
    _L0_attn_a_in = _L0_attn_a_setup()

    def _L0_attn_b_setup():
        import jax, jax.numpy as jnp
        import numpy as np
        B, S, D, H = (2, 256, 128, 16)
        DEPTH = D // H
        EPS = 1e-06

        def _split_heads(t):
            b, s, _ = t.shape
            return t.reshape(b, s, H, DEPTH).transpose(0, 2, 1, 3)
        key = jax.random.key(seed)
        ks = jax.random.split(key, 6)
        glorot = lambda k: jax.random.uniform(k, (D, D), jnp.float32, -1.0, 1.0) * np.sqrt(6.0 / (D + D))
        return {'x': jax.random.normal(ks[0], (B, S, D), jnp.float32), 'Wq': glorot(ks[1]), 'bq': jnp.zeros((D,), jnp.float32), 'Wk': glorot(ks[2]), 'bk': jnp.zeros((D,), jnp.float32), 'Wv': glorot(ks[3]), 'bv': jnp.zeros((D,), jnp.float32), 'Wo': glorot(ks[4]), 'bo': jnp.zeros((D,), jnp.float32), 'gamma': jnp.ones((D,), jnp.float32), 'beta': jnp.zeros((D,), jnp.float32)}
    _L0_attn_b_in = _L0_attn_b_setup()

    def _L0_ffn_setup():
        import jax, jax.numpy as jnp
        import numpy as np
        DIM = 128
        N_EXPERTS = 16
        TOP_K = 4
        N_GROUP = 4
        TOPK_GROUP = 2
        MOE_INTER = 64
        SHARED_INTER = 256
        ROUTED_SCALE = 2.5

        def relu2(x):
            return jnp.square(jax.nn.relu(x))

        def _router(x2, gate_w, bias_e):
            T = x2.shape[0]
            logits = x2 @ gate_w.T
            scores = jax.nn.sigmoid(logits)
            sc = jax.lax.stop_gradient(scores + bias_e[None, :])
            grp = sc.reshape(T, N_GROUP, N_EXPERTS // N_GROUP)
            top2, _ = jax.lax.top_k(grp, 2)
            group_scores = top2.sum(-1)
            _, gidx = jax.lax.top_k(group_scores, TOPK_GROUP)
            rows = jnp.arange(T)[:, None]
            gmask = jnp.zeros((T, N_GROUP), dtype=sc.dtype).at[rows, gidx].set(1.0)
            smask = jnp.repeat(gmask, N_EXPERTS // N_GROUP, axis=1)
            masked = jnp.where(smask > 0, sc, 0.0)
            _, topk_idx = jax.lax.top_k(masked, TOP_K)
            topk_w = jnp.take_along_axis(scores, topk_idx, axis=1)
            topk_w = topk_w / (topk_w.sum(-1, keepdims=True) + 1e-20)
            topk_w = topk_w * ROUTED_SCALE
            return (topk_idx, topk_w)
        key = jax.random.key(seed)
        ks = jax.random.split(key, 6)
        hidden_states = jax.random.normal(ks[0], (2, 256, DIM), dtype=jnp.float32)
        gate_w = jax.random.normal(ks[1], (N_EXPERTS, DIM), dtype=jnp.float32) * 0.02
        bias_e = jnp.zeros((N_EXPERTS,), dtype=jnp.float32)
        up_w = jax.random.normal(ks[2], (N_EXPERTS, MOE_INTER, DIM), dtype=jnp.float32) * 0.02
        down_w = jax.random.normal(ks[3], (N_EXPERTS, DIM, MOE_INTER), dtype=jnp.float32) * 0.02
        shared_up = jax.random.normal(ks[4], (SHARED_INTER, DIM), dtype=jnp.float32) * 0.02
        shared_down = jax.random.normal(ks[5], (DIM, SHARED_INTER), dtype=jnp.float32) * 0.02
        return {'hidden_states': hidden_states, 'gate_w': gate_w, 'bias_e': bias_e, 'up_w': up_w, 'down_w': down_w, 'shared_up': shared_up, 'shared_down': shared_down}
    _L0_ffn_in = _L0_ffn_setup()
    _d = {'L0_attn_a_x': _L0_attn_a_in['x'], 'L0_attn_a_w_qkv': _L0_attn_a_in['w_qkv'], 'L0_attn_a_b_qkv': _L0_attn_a_in['b_qkv'], 'L0_attn_a_w_out': _L0_attn_a_in['w_out'], 'L0_attn_a_b_out': _L0_attn_a_in['b_out'], 'L0_attn_b_Wq': _L0_attn_b_in['Wq'], 'L0_attn_b_bq': _L0_attn_b_in['bq'], 'L0_attn_b_Wk': _L0_attn_b_in['Wk'], 'L0_attn_b_bk': _L0_attn_b_in['bk'], 'L0_attn_b_Wv': _L0_attn_b_in['Wv'], 'L0_attn_b_bv': _L0_attn_b_in['bv'], 'L0_attn_b_Wo': _L0_attn_b_in['Wo'], 'L0_attn_b_bo': _L0_attn_b_in['bo'], 'L0_attn_b_gamma': _L0_attn_b_in['gamma'], 'L0_attn_b_beta': _L0_attn_b_in['beta'], 'L0_ffn_gate_w': _L0_ffn_in['gate_w'], 'L0_ffn_bias_e': _L0_ffn_in['bias_e'], 'L0_ffn_up_w': _L0_ffn_in['up_w'], 'L0_ffn_down_w': _L0_ffn_in['down_w'], 'L0_ffn_shared_up': _L0_ffn_in['shared_up'], 'L0_ffn_shared_down': _L0_ffn_in['shared_down']}
    _x0 = _d['L0_attn_a_x']
    _d['L0_attn_a_x'] = jax.random.normal(jax.random.fold_in(jax.random.key(seed), 1), (4, 1024, 128), dtype=_x0.dtype)
    del _x0
    return _d

def reference(L0_attn_a_x, L0_attn_a_w_qkv, L0_attn_a_b_qkv, L0_attn_a_w_out, L0_attn_a_b_out, L0_attn_b_Wq, L0_attn_b_bq, L0_attn_b_Wk, L0_attn_b_bk, L0_attn_b_Wv, L0_attn_b_bv, L0_attn_b_Wo, L0_attn_b_bo, L0_attn_b_gamma, L0_attn_b_beta, L0_ffn_gate_w, L0_ffn_bias_e, L0_ffn_up_w, L0_ffn_down_w, L0_ffn_shared_up, L0_ffn_shared_down):

    def _L0_attn_a_ref(x, w_qkv, b_qkv, w_out, b_out):
        import jax, jax.numpy as jnp
        import numpy as np

        def apply_rope(x):
            b, h, n, d = x.shape
            half = d // 2
            freqs = jnp.arange(0, half, dtype=x.dtype) / half
            theta = 1.0 / 1250 ** freqs
            positions = jnp.arange(n, dtype=x.dtype)
            angles = positions[:, None] * theta[None, :]
            cos = jnp.cos(angles)[None, None, :, :]
            sin = jnp.sin(angles)[None, None, :, :]
            x1 = x[..., ::2]
            x2 = x[..., 1::2]
            r1 = x1 * cos - x2 * sin
            r2 = x1 * sin + x2 * cos
            return jnp.stack([r1, r2], axis=-1).reshape(b, h, n, d)
        B, N, D = x.shape
        H = 16
        hd = D // H
        qkv = x @ w_qkv + b_qkv
        q, k, v = jnp.split(qkv, 3, axis=-1)
        to_heads = lambda t: t.reshape(B, N, H, hd).transpose(0, 2, 1, 3)
        q, k, v = (to_heads(q), to_heads(k), to_heads(v))
        q = jax.nn.elu(q) + 1
        k = jax.nn.elu(k) + 1
        rot_q = apply_rope(q)
        rot_k = apply_rope(k)
        attn_num = jnp.einsum('bhid,bhjd->bhij', rot_q, rot_k)
        attn_denom = jnp.einsum('bhid,bhjd->bhij', q, k)
        attn_weights = attn_num / attn_denom
        out = jnp.einsum('bhij,bhjd->bhid', attn_weights, v)
        out = out.transpose(0, 2, 1, 3).reshape(B, N, D)
        return out @ w_out + b_out

    def _L0_attn_b_ref(x, Wq, bq, Wk, bk, Wv, bv, Wo, bo, gamma, beta):
        import jax, jax.numpy as jnp
        import numpy as np
        B, S, D, H = (2, 256, 128, 16)
        DEPTH = D // H
        EPS = 1e-06

        def _split_heads(t):
            b, s, _ = t.shape
            return t.reshape(b, s, H, DEPTH).transpose(0, 2, 1, 3)
        b, s, d = x.shape
        q = _split_heads(x @ Wq + bq)
        k = _split_heads(x @ Wk + bk)
        v = _split_heads(x @ Wv + bv)
        q = jax.nn.elu(q) + 1.0
        k = jax.nn.elu(k) + 1.0
        k = k / jnp.sqrt(jnp.sum(k * k, axis=-1, keepdims=True) + EPS)
        scores = jnp.einsum('bhqd,bhkd->bhqk', q, k)
        attn = jnp.einsum('bhqk,bhkd->bhqd', scores, v)
        attn = attn.transpose(0, 2, 1, 3).reshape(b, s, d)
        out = attn @ Wo + bo
        y = x + out
        mu = jnp.mean(y, axis=-1, keepdims=True)
        var = jnp.mean(jnp.square(y - mu), axis=-1, keepdims=True)
        return (y - mu) / jnp.sqrt(var + EPS) * gamma + beta

    def _L0_ffn_ref(hidden_states, gate_w, bias_e, up_w, down_w, shared_up, shared_down):
        import jax, jax.numpy as jnp
        import numpy as np
        DIM = 128
        N_EXPERTS = 16
        TOP_K = 4
        N_GROUP = 4
        TOPK_GROUP = 2
        MOE_INTER = 64
        SHARED_INTER = 256
        ROUTED_SCALE = 2.5

        def relu2(x):
            return jnp.square(jax.nn.relu(x))

        def _router(x2, gate_w, bias_e):
            T = x2.shape[0]
            logits = x2 @ gate_w.T
            scores = jax.nn.sigmoid(logits)
            sc = jax.lax.stop_gradient(scores + bias_e[None, :])
            grp = sc.reshape(T, N_GROUP, N_EXPERTS // N_GROUP)
            top2, _ = jax.lax.top_k(grp, 2)
            group_scores = top2.sum(-1)
            _, gidx = jax.lax.top_k(group_scores, TOPK_GROUP)
            rows = jnp.arange(T)[:, None]
            gmask = jnp.zeros((T, N_GROUP), dtype=sc.dtype).at[rows, gidx].set(1.0)
            smask = jnp.repeat(gmask, N_EXPERTS // N_GROUP, axis=1)
            masked = jnp.where(smask > 0, sc, 0.0)
            _, topk_idx = jax.lax.top_k(masked, TOP_K)
            topk_w = jnp.take_along_axis(scores, topk_idx, axis=1)
            topk_w = topk_w / (topk_w.sum(-1, keepdims=True) + 1e-20)
            topk_w = topk_w * ROUTED_SCALE
            return (topk_idx, topk_w)
        B, S, D = hidden_states.shape
        x2 = hidden_states.reshape(-1, D)
        T = x2.shape[0]
        topk_idx, topk_w = _router(x2, gate_w, bias_e)
        rows = jnp.arange(T)[:, None]
        combine = jnp.zeros((T, N_EXPERTS), dtype=topk_w.dtype).at[rows, topk_idx].add(topk_w)

        def body(acc, inp):
            wu, wd, cw = inp
            y = relu2(x2 @ wu.T) @ wd.T
            return (acc + cw[:, None] * y, None)
        routed, _ = jax.lax.scan(body, jnp.zeros_like(x2), (up_w, down_w, combine.T))
        shared = relu2(x2 @ shared_up.T) @ shared_down.T
        out = routed + shared
        return out.reshape(B, S, D)
    x = L0_attn_a_x
    x = x + _L0_attn_a_ref(_layernorm(x, axis=-1), L0_attn_a_w_qkv, L0_attn_a_b_qkv, L0_attn_a_w_out, L0_attn_a_b_out)
    x = x + _L0_ffn_ref(_layernorm(x, axis=-1), L0_ffn_gate_w, L0_ffn_bias_e, L0_ffn_up_w, L0_ffn_down_w, L0_ffn_shared_up, L0_ffn_shared_down)
    x = x + _L0_attn_b_ref(_layernorm(x, axis=-1), L0_attn_b_Wq, L0_attn_b_bq, L0_attn_b_Wk, L0_attn_b_bk, L0_attn_b_Wv, L0_attn_b_bv, L0_attn_b_Wo, L0_attn_b_bo, L0_attn_b_gamma, L0_attn_b_beta)
    x = x + _L0_ffn_ref(_layernorm(x, axis=-1), L0_ffn_gate_w, L0_ffn_bias_e, L0_ffn_up_w, L0_ffn_down_w, L0_ffn_shared_up, L0_ffn_shared_down)
    return x

_drawn_inputs = setup_inputs


def setup_inputs(seed=0):
    import zlib

    import numpy as np

    out = dict(_drawn_inputs(seed))
    spreads = {'L0_attn_a_b_qkv': (0.0, 0.1),
     'L0_attn_a_b_out': (0.0, 0.8),
     'L0_attn_b_bq': (0.0, 0.8),
     'L0_attn_b_bk': (0.0, 0.8),
     'L0_attn_b_bv': (0.0, 0.283),
     'L0_attn_b_bo': (0.0, 0.8),
     'L0_attn_b_gamma': (1.0, 0.6),
     'L0_attn_b_beta': (0.0, 0.8),
     'L0_ffn_bias_e': (0.0, 0.8)}
    factors = {'L0_attn_b_Wq': 3.462,
     'L0_attn_b_Wk': 5.014,
     'L0_ffn_gate_w': 8.0,
     'L0_ffn_up_w': 8.0,
     'L0_ffn_down_w': 8.0,
     'L0_ffn_shared_up': 8.0,
     'L0_ffn_shared_down': 8.0}
    for name, (base, spread) in spreads.items():
        noise = np.random.default_rng([zlib.crc32(name.encode()), seed]).standard_normal(out[name].shape)
        drawn = base * np.exp(spread * noise) if base else spread * noise
        out[name] = jnp.asarray(drawn.astype(out[name].dtype))
    for name, factor in factors.items():
        out[name] = (out[name] * factor).astype(out[name].dtype)
    return out
```

```python
from contextlib import ExitStack

import concourse.bass as bass
from concourse import mybir

ALU = mybir.AluOpType
ACT = mybir.ActivationFunctionType
F32 = mybir.dt.float32
BF16 = mybir.dt.bfloat16
AX_X = mybir.AxisListType.X

P = 128
BATCH, SEQ, D = 4, 1024, 128
TILES = BATCH * SEQ // P
SEQ_TILES = SEQ // P
HEADS = 16
HD = D // HEADS
BLK = 512
BT = BLK // P
BLOCKS = BATCH * SEQ // BLK
LN_EPS = 1e-5
B_EPS = 1e-6
ACT_TABLES = "natural_log_exp_and_others"

PARTS = 3
STACK = PARTS * PARTS * HD
STACK_K = 96
PAIRS = BATCH * HEADS // 2
HALVES = SEQ // BLK
KV = HD * HD

EXPERTS, GROUPS, TOP_K, TOP_GROUPS = 16, 4, 4, 2
PER_GROUP = EXPERTS // GROUPS
INTER, SHARED = 64, 256
ROUTED = EXPERTS * INTER // P
CHUNKS = ROUTED + SHARED // P
ROUTED_SCALE = 2.5
GATE_COLS = 128


class Steps:

    def __init__(self, eng, sem, base=0):
        self.eng, self.sem, self.base, self.n = eng, sem, base, 0

    def then_wait(self, ins):
        self.n += 1
        ins.then_inc(self.sem, 1)
        self.eng.wait_ge(self.sem, self.base + self.n)

    def mark(self, ins):
        self.n += 1
        ins.then_inc(self.sem, 1)

    def wait_apart(self):
        self.eng.wait_ge(self.sem, self.base + self.n)
        self.n += 1
        self.eng.sem_inc(self.sem, 1)


def bc(ap, axis, shape):
    return ap.unsqueeze(axis).to_broadcast(shape)


def row_to_all(ap):
    return ap.unsqueeze(0).to_broadcast([P, ap.shape[0]])


VEC_TILES = {0: (2, 5), 1: (3,)}
ACT_CHUNKS = [(u, j) for u in range(HALVES) for j in range(SEQ_TILES) if j not in VEC_TILES[u]]
VEC_CHUNKS = [(u, j) for u in range(HALVES) for j in VEC_TILES[u]]
NA, NV = len(ACT_CHUNKS), len(VEC_CHUNKS)
S_SLOTS = 2
V_SLOTS = 2


def pair_order():
    act, vec = 1.85, 3.65
    steps = []
    for n in range(NA):
        steps.append((act * n + 0.95, 0, "score_act", n + S_SLOTS))
        steps.append((act * (n + 1), 1, "use_act", n))
    for t in range(2 * NV):
        steps.append((vec * (t + 1), 0, "score_vec", t + V_SLOTS))
        if t % 2:
            steps.append((vec * (t + 1), 2, "use_vec", t // 2))
    steps.append((vec * (2 * NV - 1) + 1.2, 3, "project", 0))
    steps.append((100.0, 3, "project", 1))
    steps.sort()
    return [(kind, n) for _, _, kind, n in steps]


def hybrid_kernel(nc, x_in, w_qkv, b_qkv, w_out, b_out, Wq, bq, Wk, bk, Wv, bv, Wo, bo, gamma, beta,
                  gate_t, bias_e, up_t, down_t, ident_in, cos_in, sin_in, earlier_in, pick_in,
                  heads_in, out):
    x_dram = x_in.rearrange("b (t p) d -> p (b t) d", p=P)
    out_dram = out.rearrange("b (t p) d -> p (b t) d", p=P)
    q_scr = nc.dram_tensor("q_scr", [BATCH, HEADS, PARTS * PARTS, HD, SEQ], BF16).ap()
    k_scr = nc.dram_tensor("k_scr", [BATCH, HEADS, PARTS, HD, SEQ], BF16).ap()
    rq_scr = nc.dram_tensor("rq_scr", [BATCH, D, SEQ], F32).ap()

    with ExitStack() as whole:
        x = whole.enter_context(nc.sbuf_tensor("x", [P, TILES, D], F32))
        ident = whole.enter_context(nc.sbuf_tensor("ident", [P, P], F32))
        eps = whole.enter_context(nc.sbuf_tensor("eps", [P, 2], F32))
        with ExitStack() as both:
            rk = both.enter_context(nc.sbuf_tensor("rk", [P, BATCH, HEADS // 2, SEQ_TILES, 2 * HD], F32))
            v = both.enter_context(nc.sbuf_tensor("v", [P, BATCH, HEADS // 2, SEQ_TILES, 2 * HD], F32))
            project_a(nc, x_dram, w_qkv, b_qkv, b_out, ident_in, cos_in, sin_in, x, ident, eps, rk, v,
                      q_scr, k_scr, rq_scr)
            attend_a(nc, w_out, x, rk, v, q_scr, k_scr, rq_scr)
        experts(nc, "f1", gate_t, bias_e, up_t, down_t, earlier_in, pick_in, x, ident, eps)
        attend_b(nc, Wq, bq, Wk, bk, Wv, bv, Wo, bo, gamma, beta, heads_in, x, ident, eps)
        experts(nc, "f2", gate_t, bias_e, up_t, down_t, earlier_in, pick_in, x, ident, eps)
        with ExitStack() as ctx:
            stored = ctx.enter_context(nc.semaphore("stored"))
            block = ctx.enter_context(nc.Block())

            @block.sync
            def _(sp):
                for b in range(BATCH):
                    tiles = slice(b * SEQ_TILES, (b + 1) * SEQ_TILES)
                    sp.dma_start(out_dram[:, tiles, :], x[:, tiles, :]).then_inc(stored, 16)
                sp.wait_ge(stored, 16 * BATCH)


def project_a(nc, x_dram, w_qkv, b_qkv, b_out, ident_in, cos_in, sin_in, x, ident, eps, rk, v,
              q_scr, k_scr, rq_scr):
    with ExitStack() as ctx:
        def sb(name, shape, dt=F32):
            return ctx.enter_context(nc.sbuf_tensor(name, shape, dt))

        def sem(name):
            return ctx.enter_context(nc.semaphore(name))

        w = sb("w", [P, 3 * D])
        bias = sb("bias", [P, 3 * D])
        bias_out = sb("bias_out", [P, D])
        cos = sb("cos", [P, SEQ_TILES, HD])
        sin = sb("sin", [P, SEQ_TILES, HD])
        ln = LayerNorm("ln", sb, sem, eps[:, 0:1])
        xn = sb("xn", [P, 2, BT, D])
        xnT = sb("xnT", [P, 2, BLK])
        qk = sb("qk", [P, 2, BT, 2 * D])
        e = sb("e", [P, 2, BT, 2 * D])
        m = sb("m", [P, BT, 2 * D])
        el = sb("el", [P, 2, BT, 2 * D])
        ra = sb("ra", [P, BT, 2 * D])
        rb = sb("rb", [P, 2, BT, 2 * D])
        rq = sb("rq", [P, 2, BT, D])
        rqT = sb("rqT", [P, 2, BLK])
        rest = sb("rest", [P, 2, 2, BLK])
        parts = sb("parts", [P, 2, PARTS, 2, BLK], BF16)

        ps_xT = ctx.enter_context(nc.psum_tensor("ps_xT", [P, BLK], F32))
        ps_qkv = ctx.enter_context(nc.psum_tensor("ps_qkv", [P, BT, 512], F32))
        ps_T = ctx.enter_context(nc.psum_tensor("ps_T", [P, 3, BLK], F32))

        x_loaded, w_loaded = sem("x_loaded"), sem("w_loaded")
        set_up = sem("set_up")
        vec_steps, pool_steps, xn_ready = sem("vec_steps"), sem("pool_steps"), sem("xn_ready")
        xnT_ps, xnT_ready, qkv_ps, qk_ready = sem("xnT_ps"), sem("xnT_ready"), sem("qkv_ps"), sem("qk_ready")
        e_ready, el_ready, rb_ready, rot_ready = sem("e_ready"), sem("el_ready"), sem("rb_ready"), sem("rot_ready")
        T_ps, rqT_ready, part0_ready, parts_ready = sem("T_ps"), sem("rqT_ready"), sem("part0_ready"), sem("parts_ready")
        scratch_written = [sem("scratch_written0"), sem("scratch_written1")]
        WRITES = PARTS * PARTS + PARTS + 1

        block = ctx.enter_context(nc.Block())

        @block.sync
        def _(sp):
            for b in range(BATCH):
                tiles = slice(b * SEQ_TILES, (b + 1) * SEQ_TILES)
                sp.dma_start(x[:, tiles, :], x_dram[:, tiles, :]).then_inc(x_loaded, 16)
            for dst, src in ((ident[:], ident_in), (w[:], w_qkv), (bias[:], row_to_all(b_qkv)),
                             (bias_out[:], row_to_all(b_out)), (cos[:], cos_in), (sin[:], sin_in)):
                sp.dma_start(dst, src).then_inc(w_loaded, 16)
            for g in range(2):
                sp.sem_inc(scratch_written[g], 16)
            with sp.Fori(0, BLOCKS // 2) as b:
                for g in range(2):
                    sp.wait_ge(parts_ready, 2 * b + g + 1)
                    sp.wait_ge(rqT_ready, 2 * b + g + 1)
                    tok = slice(g * BLK, (g + 1) * BLK)
                    for r in range(PARTS):
                        for s in range(PARTS):
                            sp.dma_start(q_scr[b, :, r * PARTS + s, :, tok],
                                         parts[:, g, (r + s) % PARTS, 0, :]).then_inc(scratch_written[g], 16)
                    for s in range(PARTS):
                        sp.dma_start(k_scr[b, :, s, :, tok], parts[:, g, s, 1, :]).then_inc(scratch_written[g], 16)
                    sp.dma_start(rq_scr[b, :, tok], rqT[:, g, :]).then_inc(scratch_written[g], 16)
            for g in range(2):
                sp.wait_ge(scratch_written[g], 16 * WRITES * BLOCKS // 2 + 16)

        @block.vector
        def _(dve):
            nc.vector.memset(eps[:, 0:1], LN_EPS)
            nc.vector.memset(eps[:, 1:2], B_EPS).then_inc(set_up, 1)
            dve.wait_ge(x_loaded, 16 * BATCH)
            dve.wait_ge(w_loaded, 16 * 6)
            STEPS = LayerNorm.STEPS + 4
            with dve.Fori(0, BLOCKS // 2) as b:
                for g in range(2):
                    t0 = (2 * b + g) * BT
                    n = 2 * b + g
                    steps = Steps(dve, vec_steps, n * STEPS)
                    tile = lambda t: x[:, t0 + t, :]
                    ln.statistics(nc, dve, steps, n, g, tile)
                    ln.normalize(nc, dve, steps, n, g, lambda t: xn[:, g, t, :], tile).then_inc(xn_ready, 1)
                    dve.wait_ge(qkv_ps, n + 1)
                    steps.mark(nc.vector.tensor_tensor(
                        v[:, b, :, g * BT:(g + 1) * BT, :].rearrange("p h t f -> p t h f"),
                        ps_qkv[:, :, 2 * D:3 * D].rearrange("p t (h f) -> p t h f", f=2 * HD),
                        bc(bias[:, 2 * D:3 * D].rearrange("p (h f) -> p h f", f=2 * HD), 1,
                           [P, BT, HEADS // 2, 2 * HD]), ALU.add))
                    nc.vector.tensor_tensor(qk[:, g, :, :], ps_qkv[:, :, 0:2 * D],
                                            bc(bias[:, 0:2 * D], 1, [P, BT, 2 * D]), ALU.add).then_inc(qk_ready, 1)
                    dve.wait_ge(qk_ready, n + 1)
                    steps.then_wait(nc.vector.tensor_scalar(m[:], qk[:, g, :, :], 0.0, None, ALU.max))
                    dve.wait_ge(e_ready, n + 1)
                    flat = "p t f -> p (t f)"
                    nc.vector.scalar_tensor_tensor(
                        out=el[:, g, :, :].rearrange(flat), in0=e[:, g, :, :].rearrange(flat), scalar=1.0,
                        in1=m[:].rearrange(flat), op0=ALU.min, op1=ALU.add).then_inc(el_ready, 1)
                    dve.wait_ge(el_ready, n + 1)
                    ev = el[:, g, :, :].rearrange("p t (h f two) -> p t h f two", two=2, f=HD // 2)
                    rv = rb[:, g, :, :].rearrange("p t (h f two) -> p t h f two", two=2, f=HD // 2)
                    sv = sin[:, g * BT:(g + 1) * BT, :].rearrange("p t (f two) -> p t f two", two=2)
                    for a in range(2):
                        last = nc.vector.tensor_tensor(
                            rv[:, :, :, :, a], ev[:, :, :, :, 1 - a],
                            bc(sv[:, :, :, a], 2, [P, BT, 2 * HEADS, HD // 2]), ALU.mult)
                    last.then_inc(rb_ready, 1)
                    dve.wait_ge(part0_ready, n + 1)
                    steps.then_wait(nc.vector.tensor_tensor(rest[:, g, :, :], ps_T[:, 0:2, :],
                                                            parts[:, g, 0, :, :], ALU.subtract))
                    steps.then_wait(nc.vector.tensor_copy(parts[:, g, 1, :, :], rest[:, g, :, :]))
                    nc.vector.tensor_tensor(parts[:, g, 2, :, :], rest[:, g, :, :], parts[:, g, 1, :, :],
                                            ALU.subtract).then_inc(parts_ready, 1)
                    assert steps.n == STEPS

        @block.scalar
        def _(act):
            nc.scalar.preload_act_table_set(ACT_TABLES)
            act.wait_ge(set_up, 1)
            with act.Fori(0, BLOCKS // 2) as b:
                for g in range(2):
                    n = 2 * b + g
                    ln.scale(nc, act, n, g)
                    act.wait_ge(xnT_ps, n + 1)
                    nc.scalar.copy(xnT[:, g, :], ps_xT[:]).then_inc(xnT_ready, 1)
                    act.wait_ge(qk_ready, n + 1)
                    nc.scalar.activation(e[:, g, :, :], qk[:, g, :, :], ACT.Exp).then_inc(e_ready, 1)
                    act.wait_ge(T_ps, n + 1)
                    act.wait_ge(scratch_written[g], 16 * WRITES * b + 16)
                    nc.scalar.copy(parts[:, g, 0, :, :], ps_T[:, 0:2, :]).then_inc(part0_ready, 1)
                    act.wait_ge(part0_ready, n + 1)
                    nc.scalar.copy(rqT[:, g, :], ps_T[:, 2, :]).then_inc(rqT_ready, 1)

        @block.gpsimd
        def _(pool):
            pool.wait_ge(w_loaded, 16 * 6)
            with pool.Fori(0, BLOCKS // 2) as b:
                for g in range(2):
                    n = 2 * b + g
                    t0 = n * BT
                    pool.wait_ge(xn_ready, n + 1)
                    nc.gpsimd.tensor_tensor(x[:, bass.ds(t0, BT), :], x[:, bass.ds(t0, BT), :],
                                            bc(bias_out[:], 1, [P, BT, D]), ALU.add)
                    pool.wait_ge(el_ready, n + 1)
                    nc.gpsimd.tensor_tensor(
                        ra[:].rearrange("p t (h f) -> p t h f", f=HD),
                        el[:, g, :, :].rearrange("p t (h f) -> p t h f", f=HD),
                        bc(cos[:, g * BT:(g + 1) * BT, :], 2, [P, BT, 2 * HEADS, HD]),
                        ALU.mult).then_inc(pool_steps, 1)
                    pool.wait_ge(pool_steps, n + 1)
                    pool.wait_ge(rb_ready, n + 1)
                    nc.gpsimd.tensor_tensor(
                        rk[:, b, :, g * BT:(g + 1) * BT, :].rearrange("p h t f -> p t h f"),
                        ra[:, :, D:2 * D].rearrange("p t (h f) -> p t h f", f=2 * HD),
                        rb[:, g, :, D:2 * D].rearrange("p t (h f) -> p t h f", f=2 * HD), ALU.add)
                    nc.gpsimd.tensor_tensor(rq[:, g, :, :], ra[:, :, 0:D], rb[:, g, :, 0:D],
                                            ALU.add).then_inc(rot_ready, 1)
                    pool.wait_ge(rot_ready, n + 1)

        @block.tensor
        def _(pe):
            pe.wait_ge(w_loaded, 16 * 6)
            with pe.Fori(0, BLOCKS // 2) as b:
                for g in range(2):
                    n = 2 * b + g
                    pe.wait_ge(xn_ready, n + 1)
                    for t in range(BT):
                        last = nc.tensor.transpose(ps_xT[:, t * P:(t + 1) * P], xn[:, g, t, :], ident[:])
                    last.then_inc(xnT_ps, 1)
                    pe.wait_ge(xnT_ready, n + 1)
                    for t in range(BT):
                        last = nc.tensor.matmul(ps_qkv[:, t, 0:3 * D], xnT[:, g, t * P:(t + 1) * P], w[:],
                                                start=True, stop=True)
                    last.then_inc(qkv_ps, 1)
                    pe.wait_ge(el_ready, n + 1)
                    for a in range(2):
                        for t in range(BT):
                            nc.tensor.transpose(ps_T[:, a, t * P:(t + 1) * P], el[:, g, t, a * D:(a + 1) * D], ident[:])
                    pe.wait_ge(rot_ready, n + 1)
                    for t in range(BT):
                        last = nc.tensor.transpose(ps_T[:, 2, t * P:(t + 1) * P], rq[:, g, t, :], ident[:])
                    last.then_inc(T_ps, 1)
                    pe.wait_ge(parts_ready, n + 1)
                    pe.wait_ge(rqT_ready, n + 1)


def attend_a(nc, w_out, x, rk, v, q_scr, k_scr, rq_scr):
    with ExitStack() as ctx:
        def sb(name, shape, dt=F32):
            return ctx.enter_context(nc.sbuf_tensor(name, shape, dt))

        def sem(name):
            return ctx.enter_context(nc.semaphore(name))

        q_st = sb("q_st", [P, 2, 2, SEQ], BF16)
        k_st = sb("k_st", [P, 2, 2, SEQ], BF16)
        rq_rep = sb("rq_rep", [P, 2, SEQ])
        wo = sb("wo", [P, HEADS // 2, D])
        kv = sb("kv", [P, 2, 2, SEQ_TILES, KV])
        r_act = sb("r_act", [P, NA, 2, BLK])
        r_vec = sb("r_vec", [P, 2 * NV, BLK])
        gq = sb("gq", [P, HALVES, BLK])

        ps_act = ctx.enter_context(nc.psum_tensor("ps_act", [P, S_SLOTS, 2, BLK], F32))
        ps_vec = ctx.enter_context(nc.psum_tensor("ps_vec", [P, V_SLOTS, BLK], F32))
        ps_g = ctx.enter_context(nc.psum_tensor("ps_g", [P, HALVES, BLK], F32))

        wo_loaded, zeroed = sem("wo_loaded"), sem("zeroed")
        loaded = [sem("loaded0"), sem("loaded1")]
        act_scores, ln_done, act_ready = sem("act_scores"), sem("ln_done"), sem("act_ready")
        vec_scores, vec_ready = sem("vec_scores"), sem("vec_ready")
        kv_ready = sem("kv_ready")
        g_ready, gq_ready, y_ready, x_added = sem("g_ready"), sem("gq_ready"), sem("y_ready"), sem("x_added")
        LOADS = 16 * 9

        block = ctx.enter_context(nc.Block())

        @block.sync
        def _(sp):
            for h in range(HEADS):
                sp.dma_start(wo[(h % 2) * KV:(h % 2 + 1) * KV, h // 2, :],
                             bc(w_out[h * HD:(h + 1) * HD, :], 0, [HD, HD, D])).then_inc(wo_loaded, 16)

            def load(n, s):
                b, hp = n // (HEADS // 2), n % (HEADS // 2)
                for a in range(2):
                    sp.dma_start(q_st[0:STACK, s, a, :],
                                 q_scr[b, 2 * hp + a].rearrange("s d n -> (s d) n")).then_inc(loaded[s], 16)
                    for r in range(PARTS):
                        sp.dma_start(k_st[r * PARTS * HD:(r + 1) * PARTS * HD, s, a, :],
                                     k_scr[b, 2 * hp + a].rearrange("s d n -> (s d) n")).then_inc(loaded[s], 16)
                sp.dma_start(rq_rep[:, s, :], bc(rq_scr[b, bass.ds(hp * 2 * HD, 2 * HD), :], 1, [2 * HD, HD, SEQ])
                             ).then_inc(loaded[s], 16)

            sp.wait_ge(zeroed, 1)
            for s in range(2):
                load(s, s)
            with sp.Fori(0, PAIRS // 2 - 1) as i:
                for s in range(2):
                    sp.wait_ge(gq_ready, HALVES * (2 * i + s + 1))
                    load(2 * i + s + 2, s)

        @block.gpsimd
        def _(pool):
            def products(n, s):
                b, hp = n // (HEADS // 2), n % (HEADS // 2)
                for a in range(2):
                    last = nc.gpsimd.tensor_tensor(
                        kv[:, s, a, :, :].rearrange("p t (c d) -> p t c d", d=HD),
                        bc(rk[:, b, hp, :, a * HD:(a + 1) * HD], 3, [P, SEQ_TILES, HD, HD]),
                        bc(v[:, b, hp, :, a * HD:(a + 1) * HD], 2, [P, SEQ_TILES, HD, HD]), ALU.mult)
                last.then_inc(kv_ready, 1)

            for s in range(2):
                products(s, s)
            with pool.Fori(0, PAIRS // 2 - 1) as i:
                for s in range(2):
                    pool.wait_ge(g_ready, HALVES * (2 * i + s + 1))
                    products(2 * i + s + 2, s)

        @block.tensor
        def _(pe):
            def scores(out, s, a, u, j):
                return nc.tensor.matmul(out, k_st[0:STACK_K, s, a, j * P:(j + 1) * P],
                                        q_st[0:STACK_K, s, a, u * BLK:(u + 1) * BLK], start=True, stop=True)

            def score_act(i, s, n, first=False):
                s, n = s + n // NA, n % NA
                u, j = ACT_CHUNKS[n]
                count = (2 * i + s) * NA + n
                s = s % 2
                if not first:
                    pe.wait_ge(ln_done, count - S_SLOTS + 1)
                for a in range(2):
                    last = scores(ps_act[:, (s * NA + n) % S_SLOTS, a, :], s, a, u, j)
                last.then_inc(act_scores, 1)

            def score_vec(i, s, t, first=False):
                s, t = s + t // (2 * NV), t % (2 * NV)
                u, j = VEC_CHUNKS[t // 2]
                count = (2 * i + s) * 2 * NV + t
                s = s % 2
                if not first:
                    pe.wait_ge(vec_ready, count - V_SLOTS + 1)
                scores(ps_vec[:, t % V_SLOTS, :], s, t % 2, u, j).then_inc(vec_scores, 1)

            def pair(i, s, last_pair):
                n = 2 * i + s
                opened, left = set(), {u: SEQ_TILES for u in range(HALVES)}
                next_loaded = False
                pe.wait_ge(kv_ready, n + 1)
                for kind, c in ORDER:
                    if kind in ("score_act", "score_vec"):
                        own = c < (NA if kind == "score_act" else 2 * NV)
                        if not own and last_pair:
                            continue
                        if not own and not next_loaded:
                            pe.wait_ge(loaded[(s + 1) % 2], LOADS * (i + 1 + (s + 1) // 2))
                            next_loaded = True
                        (score_act if kind == "score_act" else score_vec)(i, s, c)
                        continue
                    if kind == "project":
                        project(n, c)
                        continue
                    if kind == "use_act":
                        u, j = ACT_CHUNKS[c]
                        pe.wait_ge(act_ready, n * NA + c + 1)
                    else:
                        u, j = VEC_CHUNKS[c]
                        pe.wait_ge(vec_ready, 2 * NV * n + 2 * c + 2)
                    if u not in opened:
                        pe.wait_ge(x_added, HALVES * n + u + 1)
                    for a in range(2):
                        r = r_act[:, c, a, :] if kind == "use_act" else r_vec[:, 2 * c + a, :]
                        last = nc.tensor.matmul(ps_g[a * KV:(a + 1) * KV, u, :], kv[:, s, a, j, :], r,
                                                start=u not in opened, stop=left[u] == 1)
                    opened.add(u)
                    left[u] -= 1
                    if left[u] == 0:
                        last.then_inc(g_ready, 1)

            def project(n, u):
                pe.wait_ge(gq_ready, HALVES * n + u + 1)
                for t in range(BT):
                    last = nc.tensor.matmul(ps_g[:, u, t * P:(t + 1) * P], gq[:, u, t * P:(t + 1) * P],
                                            wo[:, n % (HEADS // 2), :], start=True, stop=True)
                last.then_inc(y_ready, 1)

            ORDER = pair_order()
            pe.wait_ge(wo_loaded, 16 * HEADS)
            pe.wait_ge(loaded[0], LOADS)
            for c in range(S_SLOTS):
                score_act(0, 0, c, first=True)
            for c in range(V_SLOTS):
                score_vec(0, 0, c, first=True)
            with pe.Fori(0, PAIRS // 2 - 1) as i:
                for s in range(2):
                    pair(i, s, False)
            pair(PAIRS // 2 - 1, 0, False)
            pair(PAIRS // 2 - 1, 1, True)

        @block.scalar
        def _(act):
            nc.scalar.preload_act_table_set(ACT_TABLES)
            with act.Fori(0, PAIRS // 2) as i:
                for s in range(2):
                    for c in range(NA):
                        n = (2 * i + s) * NA + c
                        act.wait_ge(act_scores, n + 1)
                        nc.scalar.activation(r_act[:, c, :, :], ps_act[:, (s * NA + c) % S_SLOTS, :, :],
                                             ACT.Ln).then_inc(ln_done, 1)
                        act.wait_ge(ln_done, n + 1)
                        nc.scalar.activation(r_act[:, c, :, :], r_act[:, c, :, :], ACT.Exp,
                                             scale=-1.0).then_inc(act_ready, 1)

        @block.vector
        def _(dve):
            nc.vector.memset(q_st[64:STACK_K, :, :, :], 0.0)
            nc.vector.memset(k_st[64:STACK_K, :, :, :], 0.0).then_inc(zeroed, 1)
            dve.sem_inc(x_added, HALVES)

            def rotate(n, s, u):
                dve.wait_ge(g_ready, HALVES * n + u + 1)
                nc.vector.tensor_tensor(gq[:, u, :], ps_g[:, u, :], rq_rep[:, s, u * BLK:(u + 1) * BLK],
                                        ALU.mult).then_inc(gq_ready, 1)

            def add(n, u):
                dve.wait_ge(y_ready, HALVES * n + u + 1)
                tiles = x[:, bass.ds((n // (HEADS // 2)) * SEQ_TILES + u * BT, BT), :]
                nc.vector.tensor_tensor(tiles, ps_g[:, u, :].rearrange("p (t d) -> p t d", d=D), tiles,
                                        ALU.add).then_inc(x_added, 1)

            with dve.Fori(0, PAIRS // 2) as i:
                for s in range(2):
                    n = 2 * i + s
                    for t in range(2 * NV):
                        dve.wait_ge(vec_scores, 2 * NV * n + t + 1)
                        nc.vector.reciprocal(r_vec[:, t, :], ps_vec[:, t % V_SLOTS, :]).then_inc(vec_ready, 1)
                        if t == 2 * NV - 2:
                            rotate(n, s, 0)
                        if t == 2 * NV - 1:
                            add(n, 0)
                    rotate(n, s, 1)
                    add(n, 1)


class LayerNorm:

    STEPS = BT + 6

    def __init__(self, name, sb, sem, eps, eps_value=LN_EPS):
        self.stats = sb(name + "_stats", [P, BT, 6])
        self.mv = sb(name + "_mv", [P, 2, BT, 2])
        self.lnv = sb(name + "_lnv", [P, 2, BT])
        self.rstd = sb(name + "_rstd", [P, 2, BT])
        self.newton = sb(name + "_newton", [P, 3, BT])
        self.eps, self.eps_value = eps, eps_value
        self.stats_ready, self.ln_ready, self.rstd_ready = (
            sem(name + "_stats_ready"), sem(name + "_ln_ready"), sem(name + "_rstd_ready"))

    def statistics(self, nc, dve, steps, n, g, tile):
        for t in range(BT):
            steps.mark(nc.vector.bn_stats(self.stats[:, t, :], tile(t)))
        steps.wait_apart()
        for t in range(BT):
            last = nc.vector.bn_aggr(self.mv[:, g, t, :], self.stats[:, t, :])
        last.then_inc(self.stats_ready, 1)
        dve.wait_ge(self.stats_ready, n + 1)

    def scale(self, nc, act, n, g):
        act.wait_ge(self.stats_ready, n + 1)
        nc.scalar.activation(self.lnv[:, g, :], self.mv[:, g, :, 1], ACT.Ln, bias=self.eps).then_inc(self.ln_ready, 1)
        act.wait_ge(self.ln_ready, n + 1)
        nc.scalar.activation(self.rstd[:, g, :], self.lnv[:, g, :], ACT.Exp, scale=-0.5).then_inc(self.rstd_ready, 1)

    def normalize(self, nc, dve, steps, n, g, dst, tile):
        V, (half, t1, r), r0 = nc.vector, (self.newton[:, a, :] for a in range(3)), self.rstd[:, g, :]
        steps.then_wait(V.tensor_scalar(half, self.mv[:, g, :, 1], self.eps_value, -0.5, ALU.add, ALU.mult))
        dve.wait_ge(self.rstd_ready, n + 1)
        steps.then_wait(V.tensor_tensor(t1, half, r0, ALU.mult))
        steps.then_wait(V.tensor_tensor(half, t1, r0, ALU.mult))
        steps.then_wait(V.tensor_scalar(t1, half, 1.5, None, ALU.add))
        steps.then_wait(V.tensor_tensor(r, t1, r0, ALU.mult))
        for t in range(BT):
            last = V.tensor_scalar(dst(t), tile(t), self.mv[:, g, t, 0:1], self.newton[:, 2, t:t + 1],
                                   ALU.subtract, ALU.mult)
        return last


def experts(nc, name, gate_t, bias_e, up_t, down_t, earlier_in, pick_in, x, ident, eps):
    with ExitStack() as ctx:
        def sb(n, shape, dt=F32):
            return ctx.enter_context(nc.sbuf_tensor(f"{name}_{n}", shape, dt))

        def sem(n):
            return ctx.enter_context(nc.semaphore(f"{name}_{n}"))

        def ps(n, shape, dt=F32):
            return ctx.enter_context(nc.psum_tensor(f"{name}_{n}", shape, dt))

        E, G, RANKED = EXPERTS, GROUPS, STACK_K
        gate = sb("gate", [P, GATE_COLS])
        up = sb("up", [P, CHUNKS, P])
        down = sb("down", [P, CHUNKS, D])
        bias = sb("bias", [P, E])
        earlier = sb("earlier", [P, E, E], BF16)
        pick = sb("pick", [P, ROUTED, P], BF16)
        identb = sb("identb", [P, P], BF16)
        ln = LayerNorm(name + "_ln", lambda n, shape: sb(n, shape), sem, eps[:, 0:1])
        xn = sb("xn", [P, BT, D])
        xnT = sb("xnT", [P, 2, BLK])
        ex = sb("ex", [P, BT, E])
        one_ex = sb("one_ex", [P, BT, E])
        score = sb("score", [P, BT, E])
        biased = sb("biased", [P, BT, E])
        sums = sb("sums", [P, BT * G, 6])
        group = sb("group", [P, BT, G])
        g_more = sb("g_more", [P, BT, G, G], BF16)
        g_same = sb("g_same", [P, BT, G, G], BF16)
        g_rank = sb("g_rank", [P, BT, G])
        g_in = sb("g_in", [P, BT * G])
        masked = sb("masked", [P, BT, E])
        more = sb("more", [P, BT, E, E], BF16)
        same = sb("same", [P, BT, E, E], BF16)
        rank = sb("rank", [P, BT * E])
        wsel = sb("wsel", [P, BT * E])
        total = sb("total", [P, BT])
        inv = sb("inv", [P, BT])
        weight = sb("weight", [P, BT, E])
        wrest = sb("wrest", [P, BT, E])
        wparts = sb("wparts", [P, BT, RANKED], BF16)
        wT = sb("wT", [P, BLK], BF16)
        r = sb("r", [P, 3, BLK])
        rw = sb("rw", [P, 2, BLK])
        h = sb("h", [P, 2, CHUNKS, BLK])

        ps_xT = ps("ps_xT", [P, BLK])
        ps_gate = ps("ps_gate", [P, BT, GATE_COLS])
        ps_wT = ps("ps_wT", [P, 2 * BLK], BF16)
        ps_u = ps("ps_u", [P, 2, BLK])
        ps_w = ps("ps_w", [P, 2, BLK])
        ps_y = ps("ps_y", [P, BT, D])

        loaded, set_up = sem("loaded"), sem("set_up")
        vec_steps = sem("vec_steps")
        xn_ready, xT_ps, xnT_ready = sem("xn_ready"), sem("xT_ps"), sem("xnT_ready")
        gate_ps, ex_ready, wparts_ready, wT_ps, wT_ready = (
            sem("gate_ps"), sem("ex_ready"), sem("wparts_ready"), sem("wT_ps"), sem("wT_ready"))
        u_ps, w_ps, r_ready, rw_ready, h_ready = sem("u_ps"), sem("w_ps"), sem("r_ready"), sem("rw_ready"), sem("h_ready")
        y_ready = sem("y_ready")
        LOADS = 7

        def blocks(eng, front, main):
            front(0, 0)
            with eng.Fori(0, BLOCKS // 2 - 1) as i:
                for g in range(2):
                    main(2 * i + g, g, True)
            main(BLOCKS - 2, 0, True)
            main(BLOCKS - 1, 1, False)

        block = ctx.enter_context(nc.Block())

        @block.sync
        def _(sp):
            for dst, src in ((gate[:, 0:E], gate_t), (up[:], up_t.rearrange("d (c i) -> d c i", i=P)),
                             (down[:], down_t.rearrange("(c i) d -> i c d", i=P)), (bias[:], row_to_all(bias_e)),
                             (earlier[:], earlier_in), (pick[:], pick_in[:, 0:ROUTED, :]), (identb[:], pick_in[:, ROUTED, :])):
                sp.dma_start(dst, src).then_inc(loaded, 16)

        @block.vector
        def _(dve):
            nc.vector.memset(gate[:, E:GATE_COLS], 0.0)
            nc.vector.memset(wparts[:], 0.0).then_inc(set_up, 1)
            dve.wait_ge(set_up, 1)
            dve.wait_ge(loaded, 16 * LOADS)
            t3, t4 = "p t e -> p (t e)", "p (t g) e -> p t g e"
            ROUTE_STEPS = 28
            STEPS = LayerNorm.STEPS + ROUTE_STEPS

            def normalize(n, g):
                steps = Steps(dve, vec_steps, n * STEPS)
                tile = lambda t: x[:, n * BT + t, :]
                ln.statistics(nc, dve, steps, n, g, tile)
                ln.normalize(nc, dve, steps, n, g, lambda t: xn[:, t, :], tile).then_inc(xn_ready, 1)

            def route(n):
                s = Steps(dve, vec_steps, n * STEPS + LayerNorm.STEPS)
                V = nc.vector
                dve.wait_ge(ex_ready, n + 1)
                s.then_wait(V.tensor_scalar(one_ex[:], ex[:], 1.0, None, ALU.add))
                s.then_wait(V.reciprocal(score[:], one_ex[:]))
                s.then_wait(V.tensor_tensor(biased[:], score[:], bc(bias[:], 1, [P, BT, E]), ALU.add))
                yield
                four = biased[:].rearrange("p t (g e) -> p (t g) e", e=PER_GROUP)
                s.mark(V.tensor_tensor(sums[:, :, 0:3], four[:, :, 0:3], four[:, :, 1:4], ALU.add))
                s.mark(V.tensor_tensor(sums[:, :, 3:5], four[:, :, 0:2], four[:, :, 2:4], ALU.add))
                s.then_wait(V.tensor_tensor(sums[:, :, 5:6], four[:, :, 0:1], four[:, :, 3:4], ALU.add))
                s.then_wait(V.tensor_reduce(group[:].rearrange("p t g -> p (t g)"), sums[:], AX_X, ALU.max))
                yield
                sh = [P, BT, G, G]
                s.mark(V.tensor_tensor(g_more[:], bc(group[:], 2, sh), bc(group[:], 3, sh), ALU.is_gt))
                s.then_wait(V.tensor_tensor(g_same[:], bc(group[:], 2, sh), bc(group[:], 3, sh), ALU.is_equal))
                s.then_wait(V.tensor_tensor(g_same[:], g_same[:], bc(earlier[:, 0:G, 0:G], 1, sh), ALU.mult))
                s.then_wait(V.tensor_tensor(g_more[:], g_more[:], g_same[:], ALU.add))
                yield
                s.then_wait(V.tensor_reduce(g_rank[:], g_more[:], AX_X, ALU.add))
                s.then_wait(V.tensor_scalar(g_in[:], g_rank[:].rearrange("p t g -> p (t g)"), float(TOP_GROUPS), None,
                                            ALU.is_lt))
                s.then_wait(V.tensor_tensor(masked[:].rearrange("p t (g e) -> p (t g) e", e=PER_GROUP), four,
                                            bc(g_in[:], 2, [P, BT * G, PER_GROUP]), ALU.mult))
                yield
                sh = [P, BT, E, E]
                s.mark(V.tensor_tensor(more[:], bc(masked[:], 2, sh), bc(masked[:], 3, sh), ALU.is_gt))
                s.then_wait(V.tensor_tensor(same[:], bc(masked[:], 2, sh), bc(masked[:], 3, sh), ALU.is_equal))
                yield
                s.then_wait(V.tensor_tensor(same[:], same[:], bc(earlier[:], 1, sh), ALU.mult))
                s.then_wait(V.tensor_tensor(more[:], more[:], same[:], ALU.add))
                yield
                s.then_wait(V.tensor_reduce(rank[:].rearrange("p (t e) -> p t e", e=E), more[:], AX_X, ALU.add))
                s.then_wait(V.scalar_tensor_tensor(out=wsel[:], in0=rank[:], scalar=float(TOP_K),
                                                   in1=score[:].rearrange(t3), op0=ALU.is_lt, op1=ALU.mult))
                chosen = wsel[:].rearrange("p (t e) -> p t e", e=E)
                s.then_wait(V.tensor_reduce(total[:], chosen, AX_X, ALU.add))
                yield
                s.then_wait(V.tensor_scalar(inv[:], total[:], 1e-20, None, ALU.add))
                s.then_wait(V.reciprocal(total[:], inv[:]))
                s.then_wait(V.tensor_scalar(inv[:], total[:], ROUTED_SCALE, None, ALU.mult))
                s.then_wait(V.tensor_tensor(weight[:], chosen, bc(inv[:], 2, [P, BT, E]), ALU.mult))
                s.then_wait(V.tensor_copy(wparts[:, :, 0:E], weight[:]))
                yield
                s.then_wait(V.tensor_tensor(wrest[:], weight[:], wparts[:, :, 0:E], ALU.subtract))
                s.then_wait(V.tensor_copy(wparts[:, :, E:2 * E], wrest[:]))
                V.tensor_tensor(wparts[:, :, 2 * E:3 * E], wrest[:], wparts[:, :, E:2 * E],
                                ALU.subtract).then_inc(wparts_ready, 1)
                assert s.n == ROUTE_STEPS, s.n
                yield

            def front(n, g):
                normalize(n, g)
                for _ in route(n):
                    pass

            def main(n, g, prepare):
                routing = iter(())
                for c in range(ROUTED):
                    dve.wait_ge(r_ready, CHUNKS * n + c + 1)
                    dve.wait_ge(w_ps, ROUTED * n + c + 1)
                    if c >= 2:
                        dve.wait_ge(h_ready, CHUNKS * n + c - 1)
                    nc.vector.tensor_tensor(rw[:, c % 2, :], r[:, c % 3, :], ps_w[:, c % 2, :],
                                            ALU.mult).then_inc(rw_ready, 1)
                    if prepare and c == 0:
                        normalize(n + 1, 1 - g)
                    if prepare and c == 4:
                        routing = route(n + 1)
                    next(routing, None)
                    if c > 4:
                        next(routing, None)
                for _ in routing:
                    pass
                dve.wait_ge(y_ready, n + 1)
                tiles = x[:, bass.ds(n * BT, BT), :]
                nc.vector.tensor_tensor(tiles, ps_y[:], tiles, ALU.add)

            blocks(dve, front, main)

        @block.scalar
        def _(act):
            nc.scalar.preload_act_table_set(ACT_TABLES)

            def turn(n, g):
                act.wait_ge(xT_ps, n + 1)
                nc.scalar.copy(xnT[:, g, :], ps_xT[:]).then_inc(xnT_ready, 1)

            def exp_gate(n):
                act.wait_ge(gate_ps, n + 1)
                nc.scalar.activation(ex[:], ps_gate[:, :, 0:E], ACT.Exp, scale=-1.0).then_inc(ex_ready, 1)

            def turn_weights(n):
                act.wait_ge(wT_ps, n + 1)
                nc.scalar.copy(wT[0:RANKED, :], ps_wT[0:RANKED, 0:BLK]).then_inc(wT_ready, 1)

            def front(n, g):
                ln.scale(nc, act, n, g)
                turn(n, g)
                exp_gate(n)
                turn_weights(n)

            def main(n, g, prepare):
                for c in range(CHUNKS):
                    act.wait_ge(u_ps, CHUNKS * n + c + 1)
                    if c >= 3:
                        act.wait_ge(h_ready, CHUNKS * n + c - 2)
                    nc.scalar.activation(r[:, c % 3, :], ps_u[:, c % 2, :], ACT.Relu).then_inc(r_ready, 1)
                    if prepare and c == 0:
                        ln.scale(nc, act, n + 1, 1 - g)
                    if prepare and c == 2:
                        turn(n + 1, 1 - g)
                    if prepare and c == 3:
                        exp_gate(n + 1)
                if prepare:
                    turn_weights(n + 1)

            blocks(act, front, main)

        @block.gpsimd
        def _(pool):
            def main(n, g, prepare):
                for c in range(CHUNKS):
                    if c < ROUTED:
                        pool.wait_ge(rw_ready, ROUTED * n + c + 1)
                        other = rw[:, c % 2, :]
                    else:
                        pool.wait_ge(r_ready, CHUNKS * n + c + 1)
                        other = r[:, c % 3, :]
                    nc.gpsimd.tensor_tensor(h[:, g, c, :], r[:, c % 3, :], other, ALU.mult).then_inc(h_ready, 1)

            blocks(pool, lambda n, g: None, main)

        @block.tensor
        def _(pe):
            pe.wait_ge(loaded, 16 * LOADS)
            pe.wait_ge(set_up, 1)

            def turn(n, g):
                pe.wait_ge(xn_ready, n + 1)
                for t in range(BT):
                    last = nc.tensor.transpose(ps_xT[:, t * P:(t + 1) * P], xn[:, t, :], ident[:])
                last.then_inc(xT_ps, 1)

            def gates(n, g):
                pe.wait_ge(xnT_ready, n + 1)
                for t in range(BT):
                    last = nc.tensor.matmul(ps_gate[:, t, :], xnT[:, g, t * P:(t + 1) * P], gate[:],
                                            start=True, stop=True)
                last.then_inc(gate_ps, 1)

            def turn_weights(n):
                pe.wait_ge(wparts_ready, n + 1)
                for t in range(BT):
                    last = nc.tensor.transpose(ps_wT[0:RANKED, t * P:(t + 1) * P], wparts[:, t, :], identb[:])
                last.then_inc(wT_ps, 1)

            def front(n, g):
                turn(n, g)
                gates(n, g)
                turn_weights(n)

            def main(n, g, prepare):
                def into_y(c):
                    pe.wait_ge(h_ready, CHUNKS * n + c + 1)
                    for t in range(BT):
                        last = nc.tensor.matmul(ps_y[:, t, :], h[:, g, c, t * P:(t + 1) * P], down[:, c, :],
                                                start=(c == 0 and t == 0), stop=(c == CHUNKS - 1),
                                                skip_group_check=True)
                    return last

                pe.wait_ge(wT_ready, n + 1)
                for c in range(CHUNKS):
                    if c >= 2:
                        pe.wait_ge(r_ready, CHUNKS * n + c - 1)
                    nc.tensor.matmul(ps_u[:, c % 2, :], up[:, c, :], xnT[:, g, :],
                                     start=True, stop=True).then_inc(u_ps, 1)
                    if c < ROUTED:
                        if c >= 2:
                            pe.wait_ge(rw_ready, ROUTED * n + c - 1)
                        nc.tensor.matmul(ps_w[:, c % 2, :], pick[0:RANKED, c, :], wT[0:RANKED, :],
                                         start=True, stop=True).then_inc(w_ps, 1)
                    if prepare and c == 2:
                        turn(n + 1, 1 - g)
                    if prepare and c == 3:
                        gates(n + 1, 1 - g)
                    if c >= 3:
                        into_y(c - 3)
                for c in range(CHUNKS - 3, CHUNKS):
                    last = into_y(c)
                last.then_inc(y_ready, 1)
                if prepare:
                    turn_weights(n + 1)

            blocks(pe, front, main)


def attend_b(nc, Wq, bq, Wk, bk, Wv, bv, Wo, bo, gamma, beta, heads_in, x, ident, eps):
    with ExitStack() as ctx:
        def sb(n, shape, dt=F32):
            return ctx.enter_context(nc.sbuf_tensor("b_" + n, shape, dt))

        def sem(n):
            return ctx.enter_context(nc.semaphore("b_" + n))

        def ps(n, shape, dt=F32):
            return ctx.enter_context(nc.psum_tensor("b_" + n, shape, dt))

        w = sb("w", [P, 3, D])
        wo = sb("wo", [P, D])
        bias = sb("bias", [P, 3, D])
        rows = sb("rows", [P, 3, D])
        heads = sb("heads", [P, D])
        ln1 = LayerNorm("ln1", lambda n, shape: sb(n, shape), sem, eps[:, 0:1])
        ln2 = LayerNorm("ln2", lambda n, shape: sb(n, shape), sem, eps[:, 1:2], B_EPS)
        z = sb("z", [P, 2, BT, D])
        zb = sb("zb", [P, 2, BT, D])
        zT = sb("zT", [P, 2, BLK])
        qk = sb("qk", [P, 2, BT, 2, D])
        v = sb("v", [P, 2, BT, D])
        e = sb("e", [P, 2, BT, 2 * D])
        m = sb("m", [P, BT, 2 * D])
        el = sb("el", [P, 2, BT, 2, D])
        sq = sb("sq", [P, 2, BT, D])
        norm = sb("norm", [P, 2, BT, HEADS])
        lnn = sb("lnn", [P, 2, BT, HEADS])
        rnorm = sb("rnorm", [P, 2, BT, HEADS])
        kn = sb("kn", [P, 2, BT, D])
        qT = sb("qT", [P, 2, BLK])
        vk = sb("vk", [P, D])
        vko = sb("vko", [P, D])
        y = sb("y", [P, 2, BT, D])
        yn = sb("yn", [P, 2, BT, D])

        ps_T = ps("ps_T", [P, BLK])
        ps_qkv = ps("ps_qkv", [P, BT, 512])
        ps_vk = ps("ps_vk", [P, 512])
        ps_o = ps("ps_o", [P, 2, BT, D])

        loaded = sem("loaded")
        vec_steps = sem("vec_steps")
        z_ready, zb_ready, T_ps, zT_ready, qkv_ps, qk_ready, e_ready, el_ready, qT_ready = (
            sem(n) for n in ("z_ready", "zb_ready", "T_ps", "zT_ready", "qkv_ps", "qk_ready", "e_ready", "el_ready",
                             "qT_ready"))
        sq_ready, norm_ready, lnn_ready, rnorm_ready, kn_ready, vk_ps, vk_ready, vko_ps, vko_ready = (
            sem(n) for n in ("sq_ready", "norm_ready", "lnn_ready", "rnorm_ready", "kn_ready", "vk_ps", "vk_ready",
                             "vko_ps", "vko_ready"))
        o_ps, y_ready, yn_ready, scaled, x_done = (sem(n) for n in ("o_ps", "y_ready", "yn_ready", "scaled", "x_done"))
        LOADS = 11

        block = ctx.enter_context(nc.Block())

        @block.sync
        def _(sp):
            for a, (weight, vector) in enumerate(((Wq, bq), (Wk, bk), (Wv, bv))):
                sp.dma_start(w[:, a, :], weight).then_inc(loaded, 16)
                sp.dma_start(bias[:, a, :], row_to_all(vector)).then_inc(loaded, 16)
            for a, vector in enumerate((bo, gamma, beta)):
                sp.dma_start(rows[:, a, :], row_to_all(vector)).then_inc(loaded, 16)
            sp.dma_start(wo[:], Wo).then_inc(loaded, 16)
            sp.dma_start(heads[:], heads_in).then_inc(loaded, 16)

        @block.vector
        def _(dve):
            dve.wait_ge(loaded, 16 * LOADS)
            PER_HALF = 2 * LayerNorm.STEPS + 2
            with dve.Fori(0, BATCH) as b:
                flat = "p t f -> p (t f)"
                steps = Steps(dve, vec_steps, b * 2 * PER_HALF)
                for g in range(2):
                    n = 2 * b + g
                    tile = lambda t: x[:, n * BT + t, :]
                    ln1.statistics(nc, dve, steps, n, g, tile)
                    ln1.normalize(nc, dve, steps, n, g, lambda t: z[:, g, t, :], tile).then_inc(z_ready, 1)
                for g in range(2):
                    n = 2 * b + g
                    dve.wait_ge(qkv_ps, n + 1)
                    steps.mark(nc.vector.tensor_tensor(v[:, g, :, :], ps_qkv[:, :, 2 * D:3 * D],
                                                       bc(bias[:, 2, :], 1, [P, BT, D]), ALU.add))
                    nc.vector.tensor_tensor(qk[:, g, :, :, :].rearrange("p t a d -> p t (a d)"), ps_qkv[:, :, 0:2 * D],
                                            bc(bias[:, 0:2, :].rearrange("p a d -> p (a d)"), 1, [P, BT, 2 * D]),
                                            ALU.add).then_inc(qk_ready, 1)
                    dve.wait_ge(qk_ready, n + 1)
                    steps.then_wait(nc.vector.tensor_scalar(
                        m[:], qk[:, g, :, :, :].rearrange("p t a d -> p t (a d)"), 0.0, None, ALU.max))
                    dve.wait_ge(e_ready, n + 1)
                    nc.vector.scalar_tensor_tensor(
                        out=el[:, g, :, :, :].rearrange("p t a d -> p (t a d)"), in0=e[:, g, :, :].rearrange(flat),
                        scalar=1.0, in1=m[:].rearrange(flat), op0=ALU.min, op1=ALU.add).then_inc(el_ready, 1)
                    dve.wait_ge(sq_ready, n + 1)
                    nc.vector.tensor_reduce(norm[:, g, :, :].rearrange("p t h -> p (t h)"),
                                            sq[:, g, :, :].rearrange("p t (h f) -> p (t h) f", f=HD),
                                            AX_X, ALU.add).then_inc(norm_ready, 1)
                    dve.wait_ge(rnorm_ready, n + 1)
                    nc.vector.tensor_tensor(kn[:, g, :, :].rearrange("p t (h f) -> p (t h) f", f=HD),
                                            el[:, g, :, 1, :].rearrange("p t (h f) -> p t h f", f=HD),
                                            bc(rnorm[:, g, :, :].rearrange("p t h -> p (t h)"), 2, [P, BT * HEADS, HD]),
                                            ALU.mult).then_inc(kn_ready, 1)
                dve.wait_ge(vk_ps, b + 1)
                nc.vector.tensor_tensor(vk[:], ps_vk[:, 0:D], heads[:], ALU.mult).then_inc(vk_ready, 1)
                for g in range(2):
                    n = 2 * b + g
                    dve.wait_ge(o_ps, n + 1)
                    dve.wait_ge(zb_ready, n + 1)
                    nc.vector.tensor_tensor(y[:, g, :, :], ps_o[:, g, :, :], zb[:, g, :, :], ALU.add).then_inc(y_ready, 1)
                    dve.wait_ge(y_ready, n + 1)
                    tile = lambda t: y[:, g, t, :]
                    ln2.statistics(nc, dve, steps, n, g, tile)
                    ln2.normalize(nc, dve, steps, n, g, lambda t: yn[:, g, t, :], tile).then_inc(yn_ready, 1)
                for g in range(2):
                    n = 2 * b + g
                    tiles = x[:, bass.ds(n * BT, BT), :]
                    dve.wait_ge(x_done, n + 1)
                    dve.wait_ge(scaled, n + 1)
                    nc.vector.tensor_tensor(tiles, tiles, yn[:, g, :, :], ALU.add)
                assert steps.n == 2 * PER_HALF, steps.n

        @block.scalar
        def _(act):
            nc.scalar.preload_act_table_set(ACT_TABLES)
            act.wait_ge(loaded, 16 * LOADS)
            with act.Fori(0, BATCH) as b:
                for g in range(2):
                    ln1.scale(nc, act, 2 * b + g, g)
                for g in range(2):
                    n = 2 * b + g
                    act.wait_ge(T_ps, 2 * n + 1)
                    nc.scalar.copy(zT[:, g, :], ps_T[:]).then_inc(zT_ready, 1)
                    act.wait_ge(qk_ready, n + 1)
                    nc.scalar.activation(e[:, g, :, :], qk[:, g, :, :, :].rearrange("p t a d -> p t (a d)"),
                                         ACT.Exp).then_inc(e_ready, 1)
                    act.wait_ge(T_ps, 2 * n + 2)
                    nc.scalar.copy(qT[:, g, :], ps_T[:]).then_inc(qT_ready, 1)
                    act.wait_ge(norm_ready, n + 1)
                    nc.scalar.activation(lnn[:, g, :, :], norm[:, g, :, :], ACT.Ln, bias=eps[:, 1:2]).then_inc(lnn_ready, 1)
                    act.wait_ge(lnn_ready, n + 1)
                    nc.scalar.activation(rnorm[:, g, :, :], lnn[:, g, :, :], ACT.Exp, scale=-0.5).then_inc(rnorm_ready, 1)
                act.wait_ge(vko_ps, b + 1)
                nc.scalar.copy(vko[:], ps_vk[:, D:2 * D]).then_inc(vko_ready, 1)
                for g in range(2):
                    ln2.scale(nc, act, 2 * b + g, g)

        @block.gpsimd
        def _(pool):
            pool.wait_ge(loaded, 16 * LOADS)
            with pool.Fori(0, BATCH) as b:
                for g in range(2):
                    n = 2 * b + g
                    tiles = x[:, bass.ds(n * BT, BT), :]
                    pool.wait_ge(z_ready, n + 1)
                    nc.gpsimd.tensor_tensor(zb[:, g, :, :], z[:, g, :, :], bc(rows[:, 0, :], 1, [P, BT, D]),
                                            ALU.add).then_inc(zb_ready, 1)
                    nc.gpsimd.tensor_tensor(tiles, tiles, bc(rows[:, 2, :], 1, [P, BT, D]), ALU.add).then_inc(x_done, 1)
                for g in range(2):
                    n = 2 * b + g
                    pool.wait_ge(el_ready, n + 1)
                    nc.gpsimd.tensor_tensor(sq[:, g, :, :], el[:, g, :, 1, :], el[:, g, :, 1, :],
                                            ALU.mult).then_inc(sq_ready, 1)
                for g in range(2):
                    n = 2 * b + g
                    pool.wait_ge(yn_ready, n + 1)
                    nc.gpsimd.tensor_tensor(yn[:, g, :, :], yn[:, g, :, :], bc(rows[:, 1, :], 1, [P, BT, D]),
                                            ALU.mult).then_inc(scaled, 1)

        @block.tensor
        def _(pe):
            pe.wait_ge(loaded, 16 * LOADS)
            with pe.Fori(0, BATCH) as b:
                for g in range(2):
                    n = 2 * b + g
                    pe.wait_ge(z_ready, n + 1)
                    if g == 1:
                        pe.wait_ge(qT_ready, n)
                    for t in range(BT):
                        last = nc.tensor.transpose(ps_T[:, t * P:(t + 1) * P], z[:, g, t, :], ident[:])
                    last.then_inc(T_ps, 1)
                    pe.wait_ge(zT_ready, n + 1)
                    for t in range(BT):
                        last = nc.tensor.matmul(ps_qkv[:, t, 0:3 * D], zT[:, g, t * P:(t + 1) * P],
                                                w[:].rearrange("p a d -> p (a d)"), start=True, stop=True)
                    last.then_inc(qkv_ps, 1)
                    pe.wait_ge(el_ready, n + 1)
                    for t in range(BT):
                        last = nc.tensor.transpose(ps_T[:, t * P:(t + 1) * P], el[:, g, t, 0, :], ident[:])
                    last.then_inc(T_ps, 1)
                for g in range(2):
                    pe.wait_ge(kn_ready, 2 * b + g + 1)
                    for t in range(BT):
                        last = nc.tensor.matmul(ps_vk[:, 0:D], v[:, g, t, :], kn[:, g, t, :],
                                                start=(g == 0 and t == 0), stop=(g == 1 and t == BT - 1))
                last.then_inc(vk_ps, 1)
                pe.wait_ge(vk_ready, b + 1)
                nc.tensor.matmul(ps_vk[:, D:2 * D], vk[:], wo[:], start=True, stop=True).then_inc(vko_ps, 1)
                pe.wait_ge(vko_ready, b + 1)
                for g in range(2):
                    pe.wait_ge(qT_ready, 2 * b + g + 1)
                    for t in range(BT):
                        last = nc.tensor.matmul(ps_o[:, g, t, :], qT[:, g, t * P:(t + 1) * P], vko[:],
                                                start=True, stop=True)
                    last.then_inc(o_ps, 1)


def constants():
    import numpy as np

    f32 = np.float32
    half = HD // 2
    theta = (f32(1.0) / np.power(f32(1250), np.arange(half, dtype=f32) / f32(half))).astype(f32)
    angles = (np.arange(SEQ, dtype=f32)[:, None] * theta[None, :]).astype(f32)
    cos, sin = np.cos(angles).astype(f32), np.sin(angles).astype(f32)

    def table(even, odd):
        pairs = np.stack([even, odd], axis=-1).reshape(SEQ_TILES, P, HD)
        return np.ascontiguousarray(pairs.transpose(1, 0, 2))

    before = np.tril(np.ones((EXPERTS, EXPERTS), f32), -1)
    pick = np.zeros((P, ROUTED + 1, P), f32)
    for c in range(ROUTED):
        for part in range(PARTS):
            for a in range(2):
                pick[part * EXPERTS + 2 * c + a, c, a * INTER:(a + 1) * INTER] = 1
    pick[:, ROUTED, :] = np.eye(P)
    head = np.arange(D) // HD
    bf16 = mybir.dt.np(BF16)
    return {"earlier": np.ascontiguousarray(np.broadcast_to(before, (P, EXPERTS, EXPERTS))).astype(bf16),
            "pick": pick.astype(bf16), "heads": (head[:, None] == head[None, :]).astype(f32),
            "ident": np.eye(P, dtype=f32), "cos": table(cos, cos), "sin": table(-sin, sin)}


def kernel(**inputs):
    import concourse.bacc as bacc
    import numpy as np
    from concourse.bass_utils import run_bass_kernel_spmd as run

    a = {name.split("_", 1)[1]: np.asarray(array) for name, array in inputs.items()}
    c = constants()
    arrays = {
        "x_in": a["attn_a_x"], "w_qkv": a["attn_a_w_qkv"], "b_qkv": a["attn_a_b_qkv"],
        "w_out": a["attn_a_w_out"], "b_out": a["attn_a_b_out"],
        "Wq": a["attn_b_Wq"], "bq": a["attn_b_bq"], "Wk": a["attn_b_Wk"], "bk": a["attn_b_bk"],
        "Wv": a["attn_b_Wv"], "bv": a["attn_b_bv"], "Wo": a["attn_b_Wo"], "bo": a["attn_b_bo"],
        "gamma": a["attn_b_gamma"], "beta": a["attn_b_beta"],
        "gate_t": a["ffn_gate_w"].T, "bias_e": a["ffn_bias_e"],
        "up_t": np.concatenate([a["ffn_up_w"].reshape(EXPERTS * INTER, D), a["ffn_shared_up"]]).T,
        "down_t": np.concatenate([a["ffn_down_w"].transpose(0, 2, 1).reshape(EXPERTS * INTER, D),
                                  a["ffn_shared_down"].T]),
        "ident_in": c["ident"], "cos_in": c["cos"], "sin_in": c["sin"],
        "earlier_in": c["earlier"], "pick_in": c["pick"], "heads_in": c["heads"],
    }
    arrays = {name: np.ascontiguousarray(array) for name, array in arrays.items()}
    nc = bacc.Bacc("TRN2", target_bir_lowering=False, num_devices=1)
    args = {name: nc.dram_tensor(f"in_{name}_dram", array.shape, mybir.dt.from_np(array.dtype),
                                 kind="ExternalInput").ap() for name, array in arrays.items()}
    out = nc.dram_tensor("out_0_dram", (BATCH, SEQ, D), F32, kind="ExternalOutput").ap()
    hybrid_kernel(nc, out=out, **args)
    r = run(nc, [{f"in_{name}_dram": array for name, array in arrays.items()}], core_ids=[0])
    return r.results[0]["out_0_dram"]
```

```python
from contextlib import ExitStack

import concourse.bass as bass
from concourse import mybir

ALU = mybir.AluOpType
ACT = mybir.ActivationFunctionType
F32 = mybir.dt.float32
BF16 = mybir.dt.bfloat16
AX_X = mybir.AxisListType.X

P = 128
BATCH, SEQ, D = 4, 1024, 128
TILES = BATCH * SEQ // P
SEQ_TILES = SEQ // P
HEADS = 16
HD = D // HEADS
BLK = 512
BT = BLK // P
BLOCKS = BATCH * SEQ // BLK
LN_EPS = 1e-5
B_EPS = 1e-6
ACT_TABLES = "natural_log_exp_and_others"

PARTS = 3
STACK = PARTS * PARTS * HD
STACK_K = 96
PAIRS = BATCH * HEADS // 2
HALVES = SEQ // BLK
KV = HD * HD

EXPERTS, GROUPS, TOP_K, TOP_GROUPS = 16, 4, 4, 2
PER_GROUP = EXPERTS // GROUPS
INTER, SHARED = 64, 256
ROUTED = EXPERTS * INTER // P
CHUNKS = ROUTED + SHARED // P
ROUTED_SCALE = 2.5
GATE_COLS = 128


class Steps:

    def __init__(self, eng, sem, base=0):
        self.eng, self.sem, self.base, self.n = eng, sem, base, 0

    def then_wait(self, ins):
        self.n += 1
        ins.then_inc(self.sem, 1)
        self.eng.wait_ge(self.sem, self.base + self.n)

    def mark(self, ins):
        self.n += 1
        ins.then_inc(self.sem, 1)

    def wait_apart(self):
        self.eng.wait_ge(self.sem, self.base + self.n)
        self.n += 1
        self.eng.sem_inc(self.sem, 1)


def bc(ap, axis, shape):
    return ap.unsqueeze(axis).to_broadcast(shape)


def row_to_all(ap):
    return ap.unsqueeze(0).to_broadcast([P, ap.shape[0]])


VEC_TILES = {0: (2, 5), 1: (3,)}
ACT_CHUNKS = [(u, j) for u in range(HALVES) for j in range(SEQ_TILES) if j not in VEC_TILES[u]]
VEC_CHUNKS = [(u, j) for u in range(HALVES) for j in VEC_TILES[u]]
NA, NV = len(ACT_CHUNKS), len(VEC_CHUNKS)
S_SLOTS = 2
V_SLOTS = 2


def pair_order():
    act, vec = 1.85, 3.65
    steps = []
    for n in range(NA):
        steps.append((act * n + 0.95, 0, "score_act", n + S_SLOTS))
        steps.append((act * (n + 1), 1, "use_act", n))
    for t in range(2 * NV):
        steps.append((vec * (t + 1), 0, "score_vec", t + V_SLOTS))
        if t % 2:
            steps.append((vec * (t + 1), 2, "use_vec", t // 2))
    steps.append((vec * (2 * NV - 1) + 1.2, 3, "project", 0))
    steps.append((100.0, 3, "project", 1))
    steps.sort()
    return [(kind, n) for _, _, kind, n in steps]


def hybrid_kernel(nc, x_in, w_qkv, b_qkv, w_out, b_out, Wq, bq, Wk, bk, Wv, bv, Wo, bo, gamma, beta,
                  gate_t, bias_e, up_t, down_t, ident_in, cos_in, sin_in, earlier_in, pick_in,
                  heads_in, out):
    x_dram = x_in.rearrange("b (t p) d -> p (b t) d", p=P)
    out_dram = out.rearrange("b (t p) d -> p (b t) d", p=P)
    scratch = (nc.dram_tensor("qk_scr", [BATCH, PARTS, 2, D, SEQ], BF16).ap(),
               nc.dram_tensor("rq_scr", [BATCH, D, SEQ], F32).ap())

    with ExitStack() as whole:
        def sb(name, shape, dt=F32):
            return whole.enter_context(nc.sbuf_tensor(name, shape, dt))

        x = sb("x", [P, TILES, D])
        ident = sb("ident", [P, P])
        eps = sb("eps", [P, 2])
        ffn = {"gate": sb("gate", [P, GATE_COLS]), "up": sb("up", [P, CHUNKS, P]), "down": sb("down", [P, CHUNKS, D]),
               "bias": sb("bias_e", [P, EXPERTS]),
               "earlier": sb("earlier", [P, EXPERTS, EXPERTS], BF16),
               "pick": sb("pick", [P, ROUTED, P], BF16),
               "identb": sb("identb", [P, P], BF16)}
        att_b = {"w": sb("w_b", [P, 3, D]), "wo": sb("wo_b", [P, D]), "bias": sb("bias_b", [P, 3, D]),
                 "rows": sb("rows_b", [P, 3, D]),
                 "heads": sb("heads", [P, D])}
        later = [(ffn["gate"][:, 0:EXPERTS], gate_t), (ffn["up"][:], up_t.rearrange("d (c i) -> d c i", i=P)),
                 (ffn["down"][:], down_t.rearrange("(c i) d -> i c d", i=P)), (ffn["bias"][:], row_to_all(bias_e)),
                 (ffn["earlier"][:], earlier_in), (ffn["pick"][:], pick_in[:, 0:ROUTED, :]),
                 (ffn["identb"][:], pick_in[:, ROUTED, :]), (att_b["wo"][:], Wo), (att_b["heads"][:], heads_in)]
        for a, (weight, vector) in enumerate(((Wq, bq), (Wk, bk), (Wv, bv))):
            later += [(att_b["w"][:, a, :], weight), (att_b["bias"][:, a, :], row_to_all(vector))]
        for a, vector in enumerate((bo, gamma, beta)):
            later.append((att_b["rows"][:, a, :], row_to_all(vector)))

        with ExitStack() as both:
            rk = both.enter_context(nc.sbuf_tensor("rk", [P, BATCH, HEADS // 2, SEQ_TILES, 2 * HD], F32))
            v = both.enter_context(nc.sbuf_tensor("v", [P, BATCH, HEADS // 2, SEQ_TILES, 2 * HD], F32))
            wo = both.enter_context(nc.sbuf_tensor("wo", [P, HEADS // 2, D], F32))
            stacks = Stacks(nc, both, scratch)
            for h in range(HEADS):
                later.append((wo[(h % 2) * KV:(h % 2 + 1) * KV, h // 2, :],
                              bc(w_out[h * HD:(h + 1) * HD, :], 0, [HD, HD, D])))
            project_a(nc, x_dram, w_qkv, b_qkv, b_out, ident_in, cos_in, sin_in, later, x, ident, eps, rk, v,
                      scratch, stacks, ffn["gate"])
            attend_a(nc, wo, x, rk, v, stacks)
        experts(nc, "f1", ffn, x, ident, eps)
        attend_b(nc, att_b, x, ident, eps)
        experts(nc, "f2", ffn, x, ident, eps, out_dram)


class Stacks:

    LOADS = 16 * (2 * 2 * PARTS + 1)

    def __init__(self, nc, ctx, scratch):
        self.scratch = scratch
        self.q = ctx.enter_context(nc.sbuf_tensor("q_st", [P, 2, 2, SEQ], BF16))
        self.k = ctx.enter_context(nc.sbuf_tensor("k_st", [P, 2, 2, SEQ], BF16))
        self.rq = ctx.enter_context(nc.sbuf_tensor("rq_rep", [P, 2, SEQ], F32))
        self.loaded = [ctx.enter_context(nc.semaphore(f"loaded{s}")) for s in range(2)]

    def load(self, sp, n, s):
        qk_scr, rq_scr = self.scratch
        b, hp = n // (HEADS // 2), n % (HEADS // 2)
        for a in range(2):
            head = bass.ds((2 * hp + a) * HD, HD)
            for r in range(PARTS):
                rows = slice(r * PARTS * HD, (r + 1) * PARTS * HD)
                sp.dma_start(self.q[rows, s, a, :], bc(qk_scr[b, r, 0, head, :], 0, [PARTS, HD, SEQ])
                             ).then_inc(self.loaded[s], 16)
                sp.dma_start(self.k[rows, s, a, :], qk_scr[b, :, 1, head, :]).then_inc(self.loaded[s], 16)
        sp.dma_start(self.rq[:, s, :], bc(rq_scr[b, bass.ds(hp * 2 * HD, 2 * HD), :], 1, [2 * HD, HD, SEQ])
                     ).then_inc(self.loaded[s], 16)


def project_a(nc, x_dram, w_qkv, b_qkv, b_out, ident_in, cos_in, sin_in, later, x, ident, eps, rk, v,
              scratch, stacks, gate):
    qk_scr, rq_scr = scratch
    with ExitStack() as ctx:
        def sb(name, shape, dt=F32):
            return ctx.enter_context(nc.sbuf_tensor(name, shape, dt))

        def sem(name):
            return ctx.enter_context(nc.semaphore(name))

        w = sb("w", [P, 3 * D])
        bias = sb("bias", [P, 3 * D])
        bias_out = sb("bias_out", [P, D])
        cos = sb("cos", [P, SEQ_TILES, HD])
        sin = sb("sin", [P, SEQ_TILES, HD])
        ln = LayerNorm("ln", sb, sem, eps[:, 0:1])
        xn = sb("xn", [P, 2, BT, D])
        xnT = sb("xnT", [P, 2, BLK])
        qk = sb("qk", [P, 2, BT, 2 * D])
        e = sb("e", [P, 2, BT, 2 * D])
        m = sb("m", [P, 2, BT, 2 * D])
        el = sb("el", [P, 2, BT, 2 * D])
        ra = sb("ra", [P, BT, 2 * D])
        rb = sb("rb", [P, 2, BT, 2 * D])
        rq = sb("rq", [P, 2, BT, D])
        rqT = sb("rqT", [P, 2, BLK])
        rest = sb("rest", [P, 2, BLK])
        parts = sb("parts", [P, 2, PARTS, 2, BLK], BF16)

        ps_xT = ctx.enter_context(nc.psum_tensor("ps_xT", [P, BLK], F32))
        ps_qkv = ctx.enter_context(nc.psum_tensor("ps_qkv", [P, BT, 512], F32))
        ps_T = ctx.enter_context(nc.psum_tensor("ps_T", [P, 3, BLK], F32))

        x_loaded = [sem(f"x_loaded{b}") for b in range(BATCH)]
        w_loaded, later_loaded, set_up = sem("w_loaded"), sem("later_loaded"), sem("set_up")
        ln_steps, pool_steps, xn_ready = sem("ln_steps"), sem("pool_steps"), sem("xn_ready")
        xnT_ps, xnT_ready, qkv_ps, qk_ready = sem("xnT_ps"), sem("xnT_ready"), sem("qkv_ps"), sem("qk_ready")
        em_ready, el_ready, rb_ready = sem("em_ready"), sem("el_ready"), sem("rb_ready")
        rot_ready = sem("rot_ready")
        qkT_ps, rqT_ps, rqT_ready = sem("qkT_ps"), sem("rqT_ps"), sem("rqT_ready")
        part0_ready, rest_ready, part1_ready, parts_ready = (
            sem("part0_ready"), sem("rest_ready"), sem("part1_ready"), sem("parts_ready"))
        scratch_written = [sem("scratch_written0"), sem("scratch_written1")]
        WRITES = 16 * 2

        def turns(eng, turn):
            turn(-1, 0, (1,))
            turn(-1, 1, (1, 2))
            with eng.Fori(0, BLOCKS // 2 - 1) as b:
                for g in range(2):
                    turn(b, g, (1, 2, 3))
            turn(BLOCKS // 2 - 1, 0, (2, 3))
            turn(BLOCKS // 2 - 1, 1, (3,))

        block = ctx.enter_context(nc.Block())

        @block.sync
        def _(sp):
            for b in range(BATCH):
                tiles = slice(b * SEQ_TILES, (b + 1) * SEQ_TILES)
                sp.dma_start(x[:, tiles, :], x_dram[:, tiles, :]).then_inc(x_loaded[b], 16)
                if b == 0:
                    for dst, src in ((ident[:], ident_in), (w[:], w_qkv), (bias[:], row_to_all(b_qkv)),
                                     (bias_out[:], row_to_all(b_out)), (cos[:], cos_in), (sin[:], sin_in)):
                        sp.dma_start(dst, src).then_inc(w_loaded, 16)
            for dst, src in later:
                sp.dma_start(dst, src).then_inc(later_loaded, 16)
            for g in range(2):
                sp.sem_inc(scratch_written[g], 16)

            def write(b):
                for g in range(2):
                    sp.wait_ge(parts_ready, 2 * b + g + 1)
                    sp.wait_ge(rqT_ready, 2 * b + g + 1)
                    tok = slice(g * BLK, (g + 1) * BLK)
                    sp.dma_start(qk_scr[b, :, :, :, tok].rearrange("s a d n -> d (s a) n"),
                                 parts[:, g, :, :, :].rearrange("d s a n -> d (s a) n")).then_inc(scratch_written[g], 16)
                    sp.dma_start(rq_scr[b, :, tok], rqT[:, g, :]).then_inc(scratch_written[g], 16)

            with sp.Fori(0, BATCH - 1) as b:
                write(b)
            for g in range(2):
                sp.wait_ge(scratch_written[g], WRITES * (BATCH - 1) + 16)
            sp.wait_ge(set_up, 1)
            for s in range(2):
                stacks.load(sp, s, s)
            write(BATCH - 1)
            for g in range(2):
                sp.wait_ge(scratch_written[g], WRITES * BATCH + 16)
            sp.wait_ge(later_loaded, 16 * len(later))

        @block.vector
        def _(dve):
            nc.vector.memset(eps[:, 0:1], LN_EPS)
            nc.vector.memset(eps[:, 1:2], B_EPS)
            nc.vector.memset(gate[:, EXPERTS:GATE_COLS], 0.0)
            nc.vector.memset(stacks.q[64:STACK_K, :, :, :], 0.0)
            nc.vector.memset(stacks.k[64:STACK_K, :, :, :], 0.0).then_inc(set_up, 1)
            dve.sem_inc(rest_ready, 1)
            flat = "p t f -> p (t f)"

            def bias_qkv(b, g):
                n = 2 * b + g
                dve.wait_ge(qkv_ps, n + 1)
                nc.vector.tensor_tensor(
                    v[:, b, :, g * BT:(g + 1) * BT, :].rearrange("p h t f -> p t h f"),
                    ps_qkv[:, :, 2 * D:3 * D].rearrange("p t (h f) -> p t h f", f=2 * HD),
                    bc(bias[:, 2 * D:3 * D].rearrange("p (h f) -> p h f", f=2 * HD), 1,
                       [P, BT, HEADS // 2, 2 * HD]), ALU.add)
                nc.vector.tensor_tensor(qk[:, g, :, :], ps_qkv[:, :, 0:2 * D],
                                        bc(bias[:, 0:2 * D], 1, [P, BT, 2 * D]), ALU.add).then_inc(qk_ready, 1)

            def elu_and_sines(b, g):
                n = 2 * b + g
                dve.wait_ge(em_ready, n + 1)
                nc.vector.scalar_tensor_tensor(
                    out=el[:, g, :, :].rearrange(flat), in0=e[:, g, :, :].rearrange(flat), scalar=1.0,
                    in1=m[:, g, :, :].rearrange(flat), op0=ALU.min, op1=ALU.add).then_inc(el_ready, 1)
                dve.wait_ge(el_ready, n + 1)
                ev = el[:, g, :, :].rearrange("p t (h f two) -> p t h f two", two=2, f=HD // 2)
                rv = rb[:, g, :, :].rearrange("p t (h f two) -> p t h f two", two=2, f=HD // 2)
                sv = sin[:, g * BT:(g + 1) * BT, :].rearrange("p t (f two) -> p t f two", two=2)
                for a in range(2):
                    last = nc.vector.tensor_tensor(
                        rv[:, :, :, :, a], ev[:, :, :, :, 1 - a],
                        bc(sv[:, :, :, a], 2, [P, BT, 2 * HEADS, HD // 2]), ALU.mult)
                last.then_inc(rb_ready, 1)

            def split(b, g):
                n = 2 * b + g
                dve.wait_ge(part0_ready, n + 1)
                nc.vector.tensor_tensor(rest[:], ps_T[:, 0:2, :], parts[:, g, 0, :, :],
                                        ALU.subtract).then_inc(rest_ready, 1)
                dve.wait_ge(rest_ready, n + 2)
                nc.vector.tensor_copy(parts[:, g, 1, :, :], rest[:]).then_inc(part1_ready, 1)
                dve.wait_ge(part1_ready, n + 1)
                nc.vector.tensor_tensor(parts[:, g, 2, :, :], rest[:], parts[:, g, 1, :, :],
                                        ALU.subtract).then_inc(parts_ready, 1)

            def turn(b, g, stages):
                if 1 in stages:
                    n = 2 * b + 2 + g
                    steps = Steps(dve, ln_steps, n * LayerNorm.STEPS)
                    tile = lambda t: x[:, n * BT + t, :]
                    ln.statistics(nc, dve, steps, n, g, tile)
                if 3 in stages:
                    elu_and_sines(b, g)
                if 1 in stages:
                    ln.normalize(nc, dve, steps, n, g, lambda t: xn[:, g, t, :], tile).then_inc(xn_ready, 1)
                if 2 in stages:
                    if g:
                        bias_qkv(b + 1, 0)
                    else:
                        bias_qkv(b, 1)
                if 3 in stages:
                    split(b, g)

            for b in range(BATCH):
                dve.wait_ge(x_loaded[b], 16)
            dve.wait_ge(w_loaded, 16 * 6)
            turns(dve, turn)

        @block.scalar
        def _(act):
            nc.scalar.preload_act_table_set(ACT_TABLES)
            act.wait_ge(set_up, 1)

            def turn(b, g, stages):
                if 2 in stages:
                    n, o = 2 * b + g + 1, 1 - g
                    act.wait_ge(xnT_ps, n + 1)
                    nc.scalar.copy(xnT[:, o, :], ps_xT[:]).then_inc(xnT_ready, 1)
                if 1 in stages:
                    ln.scale(nc, act, 2 * b + g + 2, g)
                if 3 in stages:
                    n = 2 * b + g
                    act.wait_ge(qkT_ps, n + 1)
                    act.wait_ge(scratch_written[g], WRITES * b + 16)
                    nc.scalar.copy(parts[:, g, 0, :, :], ps_T[:, 0:2, :]).then_inc(part0_ready, 1)
                if 2 in stages:
                    n, o = 2 * b + g + 1, 1 - g
                    act.wait_ge(qk_ready, n + 1)
                    nc.scalar.activation(e[:, o, :, :], qk[:, o, :, :], ACT.Exp)
                    nc.scalar.activation(m[:, o, :, :], qk[:, o, :, :], ACT.Relu).then_inc(em_ready, 1)
                if 3 in stages:
                    n = 2 * b + g
                    act.wait_ge(rqT_ps, n + 1)
                    nc.scalar.copy(rqT[:, g, :], ps_T[:, 2, :]).then_inc(rqT_ready, 1)

            turns(act, turn)

        @block.gpsimd
        def _(pool):
            pool.wait_ge(w_loaded, 16 * 6)

            def turn(b, g, stages):
                if 3 in stages:
                    n = 2 * b + g
                    pool.wait_ge(el_ready, n + 1)
                    nc.gpsimd.tensor_tensor(
                        ra[:].rearrange("p t (h f) -> p t h f", f=HD),
                        el[:, g, :, :].rearrange("p t (h f) -> p t h f", f=HD),
                        bc(cos[:, g * BT:(g + 1) * BT, :], 2, [P, BT, 2 * HEADS, HD]),
                        ALU.mult).then_inc(pool_steps, 1)
                    pool.wait_ge(pool_steps, n + 1)
                    pool.wait_ge(rb_ready, n + 1)
                    nc.gpsimd.tensor_tensor(
                        rk[:, b, :, g * BT:(g + 1) * BT, :].rearrange("p h t f -> p t h f"),
                        ra[:, :, D:2 * D].rearrange("p t (h f) -> p t h f", f=2 * HD),
                        rb[:, g, :, D:2 * D].rearrange("p t (h f) -> p t h f", f=2 * HD),
                        ALU.add)
                    nc.gpsimd.tensor_tensor(rq[:, g, :, :], ra[:, :, 0:D], rb[:, g, :, 0:D],
                                            ALU.add).then_inc(rot_ready, 1)
                    pool.wait_ge(rot_ready, n + 1)
                if 1 in stages:
                    n = 2 * b + g + 2
                    pool.wait_ge(xn_ready, n + 1)
                    nc.gpsimd.tensor_tensor(x[:, bass.ds(n * BT, BT), :], x[:, bass.ds(n * BT, BT), :],
                                            bc(bias_out[:], 1, [P, BT, D]), ALU.add)

            turns(pool, turn)

        @block.tensor
        def _(pe):
            pe.wait_ge(w_loaded, 16 * 6)

            def turn(b, g, stages):
                if 2 in stages:
                    n, o = 2 * b + g + 1, 1 - g
                    pe.wait_ge(xn_ready, n + 1)
                    for t in range(BT):
                        last = nc.tensor.transpose(ps_xT[:, t * P:(t + 1) * P], xn[:, o, t, :], ident[:])
                    last.then_inc(xnT_ps, 1)
                if 2 in stages:
                    n, o = 2 * b + g + 1, 1 - g
                    pe.wait_ge(xnT_ready, n + 1)
                    if 3 in stages:
                        pe.wait_ge(qk_ready, n)
                    for t in range(BT):
                        last = nc.tensor.matmul(ps_qkv[:, t, 0:3 * D], xnT[:, o, t * P:(t + 1) * P], w[:],
                                                start=True, stop=True)
                    last.then_inc(qkv_ps, 1)
                if 3 in stages:
                    n = 2 * b + g
                    pe.wait_ge(el_ready, n + 1)
                    pe.wait_ge(rest_ready, n + 1)
                    for a in range(2):
                        for t in range(BT):
                            last = nc.tensor.transpose(ps_T[:, a, t * P:(t + 1) * P], el[:, g, t, a * D:(a + 1) * D],
                                                       ident[:])
                    last.then_inc(qkT_ps, 1)
                if 3 in stages:
                    if 2 not in stages:
                        pe.wait_ge(rqT_ready, 2 * b + g)
                    pe.wait_ge(rot_ready, 2 * b + g + 1)
                    for t in range(BT):
                        last = nc.tensor.transpose(ps_T[:, 2, t * P:(t + 1) * P], rq[:, g, t, :], ident[:])
                    last.then_inc(rqT_ps, 1)

            turns(pe, turn)


def attend_a(nc, wo, x, rk, v, stacks):
    with ExitStack() as ctx:
        def sb(name, shape, dt=F32):
            return ctx.enter_context(nc.sbuf_tensor(name, shape, dt))

        def sem(name):
            return ctx.enter_context(nc.semaphore(name))

        q_st, k_st, rq_rep, loaded, LOADS = stacks.q, stacks.k, stacks.rq, stacks.loaded, Stacks.LOADS
        kv = sb("kv", [P, 2, 2, SEQ_TILES, KV])
        r_act = sb("r_act", [P, NA, 2, BLK])
        r_vec = sb("r_vec", [P, 2 * NV, BLK])
        gq = sb("gq", [P, HALVES, BLK])

        ps_act = ctx.enter_context(nc.psum_tensor("ps_act", [P, S_SLOTS, 2, BLK], F32))
        ps_vec = ctx.enter_context(nc.psum_tensor("ps_vec", [P, V_SLOTS, BLK], F32))
        ps_g = ctx.enter_context(nc.psum_tensor("ps_g", [P, HALVES, BLK], F32))

        act_scores, ln_done, act_ready = sem("act_scores"), sem("ln_done"), sem("act_ready")
        vec_scores, vec_ready = sem("vec_scores"), sem("vec_ready")
        kv_ready = sem("kv_ready")
        g_ready, gq_ready, y_ready, x_added = sem("g_ready"), sem("gq_ready"), sem("y_ready"), sem("x_added")

        block = ctx.enter_context(nc.Block())

        @block.sync
        def _(sp):
            with sp.Fori(0, PAIRS // 2 - 1) as i:
                for s in range(2):
                    sp.wait_ge(gq_ready, HALVES * (2 * i + s + 1))
                    stacks.load(sp, 2 * i + s + 2, s)

        @block.gpsimd
        def _(pool):
            def products(n, s):
                b, hp = n // (HEADS // 2), n % (HEADS // 2)
                for a in range(2):
                    last = nc.gpsimd.tensor_tensor(
                        kv[:, s, a, :, :].rearrange("p t (c d) -> p t c d", d=HD),
                        bc(rk[:, b, hp, :, a * HD:(a + 1) * HD], 3, [P, SEQ_TILES, HD, HD]),
                        bc(v[:, b, hp, :, a * HD:(a + 1) * HD], 2, [P, SEQ_TILES, HD, HD]), ALU.mult)
                last.then_inc(kv_ready, 1)

            for s in range(2):
                products(s, s)
            with pool.Fori(0, PAIRS // 2 - 1) as i:
                for s in range(2):
                    pool.wait_ge(g_ready, HALVES * (2 * i + s + 1))
                    products(2 * i + s + 2, s)

        @block.tensor
        def _(pe):
            def scores(out, s, a, u, j):
                return nc.tensor.matmul(out, k_st[0:STACK_K, s, a, j * P:(j + 1) * P],
                                        q_st[0:STACK_K, s, a, u * BLK:(u + 1) * BLK], start=True, stop=True)

            def score_act(i, s, n, first=False):
                s, n = s + n // NA, n % NA
                u, j = ACT_CHUNKS[n]
                count = (2 * i + s) * NA + n
                s = s % 2
                if not first:
                    pe.wait_ge(ln_done, count - S_SLOTS + 1)
                for a in range(2):
                    last = scores(ps_act[:, (s * NA + n) % S_SLOTS, a, :], s, a, u, j)
                last.then_inc(act_scores, 1)

            def score_vec(i, s, t, first=False):
                s, t = s + t // (2 * NV), t % (2 * NV)
                u, j = VEC_CHUNKS[t // 2]
                count = (2 * i + s) * 2 * NV + t
                s = s % 2
                if not first:
                    pe.wait_ge(vec_ready, count - V_SLOTS + 1)
                scores(ps_vec[:, t % V_SLOTS, :], s, t % 2, u, j).then_inc(vec_scores, 1)

            def pair(i, s, last_pair):
                n = 2 * i + s
                opened, left = set(), {u: SEQ_TILES for u in range(HALVES)}
                next_loaded = False
                pe.wait_ge(kv_ready, n + 1)
                for kind, c in ORDER:
                    if kind in ("score_act", "score_vec"):
                        own = c < (NA if kind == "score_act" else 2 * NV)
                        if not own and last_pair:
                            continue
                        if not own and not next_loaded:
                            pe.wait_ge(loaded[(s + 1) % 2], LOADS * (i + 1 + (s + 1) // 2))
                            next_loaded = True
                        (score_act if kind == "score_act" else score_vec)(i, s, c)
                        continue
                    if kind == "project":
                        project(n, c)
                        continue
                    if kind == "use_act":
                        u, j = ACT_CHUNKS[c]
                        pe.wait_ge(act_ready, n * NA + c + 1)
                    else:
                        u, j = VEC_CHUNKS[c]
                        pe.wait_ge(vec_ready, 2 * NV * n + 2 * c + 2)
                    if u not in opened:
                        pe.wait_ge(x_added, HALVES * n + u + 1)
                    for a in range(2):
                        r = r_act[:, c, a, :] if kind == "use_act" else r_vec[:, 2 * c + a, :]
                        last = nc.tensor.matmul(ps_g[a * KV:(a + 1) * KV, u, :], kv[:, s, a, j, :], r,
                                                start=u not in opened, stop=left[u] == 1)
                    opened.add(u)
                    left[u] -= 1
                    if left[u] == 0:
                        last.then_inc(g_ready, 1)

            def project(n, u):
                pe.wait_ge(gq_ready, HALVES * n + u + 1)
                for t in range(BT):
                    last = nc.tensor.matmul(ps_g[:, u, t * P:(t + 1) * P], gq[:, u, t * P:(t + 1) * P],
                                            wo[:, n % (HEADS // 2), :], start=True, stop=True)
                last.then_inc(y_ready, 1)

            ORDER = pair_order()
            pe.wait_ge(loaded[0], LOADS)
            for c in range(S_SLOTS):
                score_act(0, 0, c, first=True)
            for c in range(V_SLOTS):
                score_vec(0, 0, c, first=True)
            with pe.Fori(0, PAIRS // 2 - 1) as i:
                for s in range(2):
                    pair(i, s, False)
            pair(PAIRS // 2 - 1, 0, False)
            pair(PAIRS // 2 - 1, 1, True)

        @block.scalar
        def _(act):
            nc.scalar.preload_act_table_set(ACT_TABLES)
            with act.Fori(0, PAIRS // 2) as i:
                for s in range(2):
                    for c in range(NA):
                        n = (2 * i + s) * NA + c
                        act.wait_ge(act_scores, n + 1)
                        nc.scalar.activation(r_act[:, c, :, :], ps_act[:, (s * NA + c) % S_SLOTS, :, :],
                                             ACT.Ln).then_inc(ln_done, 1)
                        act.wait_ge(ln_done, n + 1)
                        nc.scalar.activation(r_act[:, c, :, :], r_act[:, c, :, :], ACT.Exp,
                                             scale=-1.0).then_inc(act_ready, 1)

        @block.vector
        def _(dve):
            dve.sem_inc(x_added, HALVES)

            def rotate(n, s, u):
                dve.wait_ge(g_ready, HALVES * n + u + 1)
                nc.vector.tensor_tensor(gq[:, u, :], ps_g[:, u, :], rq_rep[:, s, u * BLK:(u + 1) * BLK],
                                        ALU.mult).then_inc(gq_ready, 1)

            def add(n, u):
                dve.wait_ge(y_ready, HALVES * n + u + 1)
                tiles = x[:, bass.ds((n // (HEADS // 2)) * SEQ_TILES + u * BT, BT), :]
                nc.vector.tensor_tensor(tiles, ps_g[:, u, :].rearrange("p (t d) -> p t d", d=D), tiles,
                                        ALU.add).then_inc(x_added, 1)

            with dve.Fori(0, PAIRS // 2) as i:
                for s in range(2):
                    n = 2 * i + s
                    for t in range(2 * NV):
                        dve.wait_ge(vec_scores, 2 * NV * n + t + 1)
                        nc.vector.reciprocal(r_vec[:, t, :], ps_vec[:, t % V_SLOTS, :]).then_inc(vec_ready, 1)
                        if t == 2 * NV - 2:
                            rotate(n, s, 0)
                        if t == 2 * NV - 1:
                            add(n, 0)
                    rotate(n, s, 1)
                    add(n, 1)


class LayerNorm:

    STEPS = BT + 6

    def __init__(self, name, sb, sem, eps, eps_value=LN_EPS):
        self.stats = sb(name + "_stats", [P, BT, 6])
        self.mv = sb(name + "_mv", [P, 2, BT, 2])
        self.lnv = sb(name + "_lnv", [P, 2, BT])
        self.rstd = sb(name + "_rstd", [P, 2, BT])
        self.newton = sb(name + "_newton", [P, 3, BT])
        self.eps, self.eps_value = eps, eps_value
        self.stats_ready, self.ln_ready, self.rstd_ready = (
            sem(name + "_stats_ready"), sem(name + "_ln_ready"), sem(name + "_rstd_ready"))

    def statistics(self, nc, dve, steps, n, g, tile):
        for t in range(BT):
            steps.mark(nc.vector.bn_stats(self.stats[:, t, :], tile(t)))
        steps.wait_apart()
        for t in range(BT):
            last = nc.vector.bn_aggr(self.mv[:, g, t, :], self.stats[:, t, :])
        last.then_inc(self.stats_ready, 1)
        dve.wait_ge(self.stats_ready, n + 1)

    def scale(self, nc, act, n, g):
        act.wait_ge(self.stats_ready, n + 1)
        nc.scalar.activation(self.lnv[:, g, :], self.mv[:, g, :, 1], ACT.Ln, bias=self.eps).then_inc(self.ln_ready, 1)
        act.wait_ge(self.ln_ready, n + 1)
        nc.scalar.activation(self.rstd[:, g, :], self.lnv[:, g, :], ACT.Exp, scale=-0.5).then_inc(self.rstd_ready, 1)

    def normalize(self, nc, dve, steps, n, g, dst, tile):
        V, (half, t1, r), r0 = nc.vector, (self.newton[:, a, :] for a in range(3)), self.rstd[:, g, :]
        steps.then_wait(V.tensor_scalar(half, self.mv[:, g, :, 1], self.eps_value, -0.5, ALU.add, ALU.mult))
        dve.wait_ge(self.rstd_ready, n + 1)
        steps.then_wait(V.tensor_tensor(t1, half, r0, ALU.mult))
        steps.then_wait(V.tensor_tensor(half, t1, r0, ALU.mult))
        steps.then_wait(V.tensor_scalar(t1, half, 1.5, None, ALU.add))
        steps.then_wait(V.tensor_tensor(r, t1, r0, ALU.mult))
        for t in range(BT):
            last = V.tensor_scalar(dst(t), tile(t), self.mv[:, g, t, 0:1], self.newton[:, 2, t:t + 1],
                                   ALU.subtract, ALU.mult)
        return last


def experts(nc, name, weights, x, ident, eps, out_dram=None):
    with ExitStack() as ctx:
        def sb(n, shape, dt=F32):
            return ctx.enter_context(nc.sbuf_tensor(f"{name}_{n}", shape, dt))

        def sem(n):
            return ctx.enter_context(nc.semaphore(f"{name}_{n}"))

        def ps(n, shape, dt=F32):
            return ctx.enter_context(nc.psum_tensor(f"{name}_{n}", shape, dt))

        E, G, RANKED = EXPERTS, GROUPS, STACK_K
        gate, up, down, bias, earlier, pick, identb = (
            weights[n] for n in ("gate", "up", "down", "bias", "earlier", "pick", "identb"))
        ln = LayerNorm(name + "_ln", lambda n, shape: sb(n, shape), sem, eps[:, 0:1])
        xn = sb("xn", [P, BT, D])
        xnT = sb("xnT", [P, 2, BLK])
        ex = sb("ex", [P, BT, E])
        one_ex = sb("one_ex", [P, BT, E])
        score = sb("score", [P, BT, E])
        biased = sb("biased", [P, BT, E])
        sums = sb("sums", [P, BT * G, 6])
        group = sb("group", [P, BT, G])
        g_more = sb("g_more", [P, BT, G, G], BF16)
        g_same = sb("g_same", [P, BT, G, G], BF16)
        g_rank = sb("g_rank", [P, BT, G])
        g_in = sb("g_in", [P, BT * G])
        masked = sb("masked", [P, BT, E])
        more = sb("more", [P, BT, E, E], BF16)
        same = sb("same", [P, BT, E, E], BF16)
        rank = sb("rank", [P, BT * E])
        wsel = sb("wsel", [P, BT * E])
        total = sb("total", [P, BT])
        inv = sb("inv", [P, BT])
        weight = sb("weight", [P, BT, E])
        wrest = sb("wrest", [P, BT, E])
        wparts = sb("wparts", [P, BT, RANKED], BF16)
        wT = sb("wT", [P, BLK], BF16)
        r = sb("r", [P, 3, BLK])
        rw = sb("rw", [P, 2, BLK])
        h = sb("h", [P, 2, CHUNKS, BLK])

        ps_xT = ps("ps_xT", [P, BLK])
        ps_gate = ps("ps_gate", [P, BT, GATE_COLS])
        ps_wT = ps("ps_wT", [P, 2 * BLK], BF16)
        ps_u = ps("ps_u", [P, 2, BLK])
        ps_w = ps("ps_w", [P, 2, BLK])
        ps_y = ps("ps_y", [P, BT, D])

        set_up = sem("set_up")
        vec_steps = sem("vec_steps")
        xn_ready, xT_ps, xnT_ready = sem("xn_ready"), sem("xT_ps"), sem("xnT_ready")
        gate_ps, ex_ready, wparts_ready, wT_ps, wT_ready = (
            sem("gate_ps"), sem("ex_ready"), sem("wparts_ready"), sem("wT_ps"), sem("wT_ready"))
        u_ps, w_ps, r_ready, rw_ready, h_ready = sem("u_ps"), sem("w_ps"), sem("r_ready"), sem("rw_ready"), sem("h_ready")
        y_ready, x_ready, stored = sem("y_ready"), sem("x_ready"), sem("stored")

        def blocks(eng, front, main):
            front(0, 0)
            with eng.Fori(0, BLOCKS // 2 - 1) as i:
                for g in range(2):
                    main(2 * i + g, g, True)
            main(BLOCKS - 2, 0, True)
            main(BLOCKS - 1, 1, False)

        block = ctx.enter_context(nc.Block())

        @block.sync
        def _(sp):
            if out_dram is not None:
                with sp.Fori(0, BLOCKS) as n:
                    sp.wait_ge(x_ready, n + 1)
                    sp.dma_start(out_dram[:, bass.ds(n * BT, BT), :],
                                 x[:, bass.ds(n * BT, BT), :]).then_inc(stored, 16)
                sp.wait_ge(stored, 16 * BLOCKS)

        @block.vector
        def _(dve):
            nc.vector.memset(wparts[:], 0.0).then_inc(set_up, 1)
            dve.wait_ge(set_up, 1)
            t3, t4 = "p t e -> p (t e)", "p (t g) e -> p t g e"
            ROUTE_STEPS = 28
            STEPS = LayerNorm.STEPS + ROUTE_STEPS

            def normalize(n, g):
                steps = Steps(dve, vec_steps, n * STEPS)
                tile = lambda t: x[:, n * BT + t, :]
                ln.statistics(nc, dve, steps, n, g, tile)
                ln.normalize(nc, dve, steps, n, g, lambda t: xn[:, t, :], tile).then_inc(xn_ready, 1)

            def route(n):
                s = Steps(dve, vec_steps, n * STEPS + LayerNorm.STEPS)
                V = nc.vector
                dve.wait_ge(ex_ready, n + 1)
                s.then_wait(V.tensor_scalar(one_ex[:], ex[:], 1.0, None, ALU.add))
                s.then_wait(V.reciprocal(score[:], one_ex[:]))
                s.then_wait(V.tensor_tensor(biased[:], score[:], bc(bias[:], 1, [P, BT, E]), ALU.add))
                yield
                four = biased[:].rearrange("p t (g e) -> p (t g) e", e=PER_GROUP)
                s.mark(V.tensor_tensor(sums[:, :, 0:3], four[:, :, 0:3], four[:, :, 1:4], ALU.add))
                s.mark(V.tensor_tensor(sums[:, :, 3:5], four[:, :, 0:2], four[:, :, 2:4], ALU.add))
                s.then_wait(V.tensor_tensor(sums[:, :, 5:6], four[:, :, 0:1], four[:, :, 3:4], ALU.add))
                s.then_wait(V.tensor_reduce(group[:].rearrange("p t g -> p (t g)"), sums[:], AX_X, ALU.max))
                yield
                sh = [P, BT, G, G]
                s.mark(V.tensor_tensor(g_more[:], bc(group[:], 2, sh), bc(group[:], 3, sh), ALU.is_gt))
                s.then_wait(V.tensor_tensor(g_same[:], bc(group[:], 2, sh), bc(group[:], 3, sh), ALU.is_equal))
                s.then_wait(V.tensor_tensor(g_same[:], g_same[:], bc(earlier[:, 0:G, 0:G], 1, sh), ALU.mult))
                s.then_wait(V.tensor_tensor(g_more[:], g_more[:], g_same[:], ALU.add))
                yield
                s.then_wait(V.tensor_reduce(g_rank[:], g_more[:], AX_X, ALU.add))
                s.then_wait(V.tensor_scalar(g_in[:], g_rank[:].rearrange("p t g -> p (t g)"), float(TOP_GROUPS), None,
                                            ALU.is_lt))
                s.then_wait(V.tensor_tensor(masked[:].rearrange("p t (g e) -> p (t g) e", e=PER_GROUP), four,
                                            bc(g_in[:], 2, [P, BT * G, PER_GROUP]), ALU.mult))
                yield
                sh = [P, BT, E, E]
                s.mark(V.tensor_tensor(more[:], bc(masked[:], 2, sh), bc(masked[:], 3, sh), ALU.is_gt))
                s.then_wait(V.tensor_tensor(same[:], bc(masked[:], 2, sh), bc(masked[:], 3, sh), ALU.is_equal))
                yield
                s.then_wait(V.tensor_tensor(same[:], same[:], bc(earlier[:], 1, sh), ALU.mult))
                s.then_wait(V.tensor_tensor(more[:], more[:], same[:], ALU.add))
                yield
                s.then_wait(V.tensor_reduce(rank[:].rearrange("p (t e) -> p t e", e=E), more[:], AX_X, ALU.add))
                s.then_wait(V.scalar_tensor_tensor(out=wsel[:], in0=rank[:], scalar=float(TOP_K),
                                                   in1=score[:].rearrange(t3), op0=ALU.is_lt, op1=ALU.mult))
                chosen = wsel[:].rearrange("p (t e) -> p t e", e=E)
                s.then_wait(V.tensor_reduce(total[:], chosen, AX_X, ALU.add))
                yield
                s.then_wait(V.tensor_scalar(inv[:], total[:], 1e-20, None, ALU.add))
                s.then_wait(V.reciprocal(total[:], inv[:]))
                s.then_wait(V.tensor_scalar(inv[:], total[:], ROUTED_SCALE, None, ALU.mult))
                s.then_wait(V.tensor_tensor(weight[:], chosen, bc(inv[:], 2, [P, BT, E]), ALU.mult))
                s.then_wait(V.tensor_copy(wparts[:, :, 0:E], weight[:]))
                yield
                s.then_wait(V.tensor_tensor(wrest[:], weight[:], wparts[:, :, 0:E], ALU.subtract))
                s.then_wait(V.tensor_copy(wparts[:, :, E:2 * E], wrest[:]))
                V.tensor_tensor(wparts[:, :, 2 * E:3 * E], wrest[:], wparts[:, :, E:2 * E],
                                ALU.subtract).then_inc(wparts_ready, 1)
                assert s.n == ROUTE_STEPS, s.n
                yield

            def front(n, g):
                normalize(n, g)
                for _ in route(n):
                    pass

            def main(n, g, prepare):
                routing = iter(())
                for c in range(ROUTED):
                    dve.wait_ge(r_ready, CHUNKS * n + c + 1)
                    dve.wait_ge(w_ps, ROUTED * n + c + 1)
                    if c >= 2:
                        dve.wait_ge(h_ready, CHUNKS * n + c - 1)
                    nc.vector.tensor_tensor(rw[:, c % 2, :], r[:, c % 3, :], ps_w[:, c % 2, :],
                                            ALU.mult).then_inc(rw_ready, 1)
                    if prepare and c == 0:
                        normalize(n + 1, 1 - g)
                    if prepare and c == 4:
                        routing = route(n + 1)
                    next(routing, None)
                    if c > 4:
                        next(routing, None)
                for _ in routing:
                    pass
                dve.wait_ge(y_ready, n + 1)
                tiles = x[:, bass.ds(n * BT, BT), :]
                nc.vector.tensor_tensor(tiles, ps_y[:], tiles, ALU.add).then_inc(x_ready, 1)

            blocks(dve, front, main)

        @block.scalar
        def _(act):
            nc.scalar.preload_act_table_set(ACT_TABLES)

            def turn(n, g):
                act.wait_ge(xT_ps, n + 1)
                nc.scalar.copy(xnT[:, g, :], ps_xT[:]).then_inc(xnT_ready, 1)

            def exp_gate(n):
                act.wait_ge(gate_ps, n + 1)
                nc.scalar.activation(ex[:], ps_gate[:, :, 0:E], ACT.Exp, scale=-1.0).then_inc(ex_ready, 1)

            def turn_weights(n):
                act.wait_ge(wT_ps, n + 1)
                nc.scalar.copy(wT[0:RANKED, :], ps_wT[0:RANKED, 0:BLK]).then_inc(wT_ready, 1)

            def front(n, g):
                ln.scale(nc, act, n, g)
                turn(n, g)
                exp_gate(n)
                turn_weights(n)

            def main(n, g, prepare):
                for c in range(CHUNKS):
                    act.wait_ge(u_ps, CHUNKS * n + c + 1)
                    if c >= 3:
                        act.wait_ge(h_ready, CHUNKS * n + c - 2)
                    nc.scalar.activation(r[:, c % 3, :], ps_u[:, c % 2, :], ACT.Relu).then_inc(r_ready, 1)
                    if prepare and c == 0:
                        ln.scale(nc, act, n + 1, 1 - g)
                    if prepare and c == 2:
                        turn(n + 1, 1 - g)
                    if prepare and c == 3:
                        exp_gate(n + 1)
                if prepare:
                    turn_weights(n + 1)

            blocks(act, front, main)

        @block.gpsimd
        def _(pool):
            def main(n, g, prepare):
                for c in range(CHUNKS):
                    if c < ROUTED:
                        pool.wait_ge(rw_ready, ROUTED * n + c + 1)
                        other = rw[:, c % 2, :]
                    else:
                        pool.wait_ge(r_ready, CHUNKS * n + c + 1)
                        other = r[:, c % 3, :]
                    nc.gpsimd.tensor_tensor(h[:, g, c, :], r[:, c % 3, :], other, ALU.mult).then_inc(h_ready, 1)

            blocks(pool, lambda n, g: None, main)

        @block.tensor
        def _(pe):
            pe.wait_ge(set_up, 1)

            def turn(n, g):
                pe.wait_ge(xn_ready, n + 1)
                for t in range(BT):
                    last = nc.tensor.transpose(ps_xT[:, t * P:(t + 1) * P], xn[:, t, :], ident[:])
                last.then_inc(xT_ps, 1)

            def gates(n, g):
                pe.wait_ge(xnT_ready, n + 1)
                for t in range(BT):
                    last = nc.tensor.matmul(ps_gate[:, t, :], xnT[:, g, t * P:(t + 1) * P], gate[:],
                                            start=True, stop=True)
                last.then_inc(gate_ps, 1)

            def turn_weights(n):
                pe.wait_ge(wparts_ready, n + 1)
                for t in range(BT):
                    last = nc.tensor.transpose(ps_wT[0:RANKED, t * P:(t + 1) * P], wparts[:, t, :], identb[:])
                last.then_inc(wT_ps, 1)

            def front(n, g):
                turn(n, g)
                gates(n, g)
                turn_weights(n)

            def main(n, g, prepare):
                def into_y(c):
                    pe.wait_ge(h_ready, CHUNKS * n + c + 1)
                    for t in range(BT):
                        last = nc.tensor.matmul(ps_y[:, t, :], h[:, g, c, t * P:(t + 1) * P], down[:, c, :],
                                                start=(c == 0 and t == 0), stop=(c == CHUNKS - 1),
                                                skip_group_check=True)
                    return last

                pe.wait_ge(wT_ready, n + 1)
                for c in range(CHUNKS):
                    if c >= 2:
                        pe.wait_ge(r_ready, CHUNKS * n + c - 1)
                    nc.tensor.matmul(ps_u[:, c % 2, :], up[:, c, :], xnT[:, g, :],
                                     start=True, stop=True).then_inc(u_ps, 1)
                    if c < ROUTED:
                        if c >= 2:
                            pe.wait_ge(rw_ready, ROUTED * n + c - 1)
                        nc.tensor.matmul(ps_w[:, c % 2, :], pick[0:RANKED, c, :], wT[0:RANKED, :],
                                         start=True, stop=True).then_inc(w_ps, 1)
                    if prepare and c == 2:
                        turn(n + 1, 1 - g)
                    if prepare and c == 3:
                        gates(n + 1, 1 - g)
                    if c >= 3:
                        into_y(c - 3)
                for c in range(CHUNKS - 3, CHUNKS):
                    last = into_y(c)
                last.then_inc(y_ready, 1)
                if prepare:
                    turn_weights(n + 1)

            blocks(pe, front, main)


def attend_b(nc, weights, x, ident, eps):
    with ExitStack() as ctx:
        def sb(n, shape, dt=F32):
            return ctx.enter_context(nc.sbuf_tensor("b_" + n, shape, dt))

        def sem(n):
            return ctx.enter_context(nc.semaphore("b_" + n))

        def ps(n, shape, dt=F32):
            return ctx.enter_context(nc.psum_tensor("b_" + n, shape, dt))

        w, wo, bias, rows, heads = (weights[n] for n in ("w", "wo", "bias", "rows", "heads"))
        ln1 = LayerNorm("ln1", lambda n, shape: sb(n, shape), sem, eps[:, 0:1])
        ln2 = LayerNorm("ln2", lambda n, shape: sb(n, shape), sem, eps[:, 1:2], B_EPS)
        z = sb("z", [P, 2, BT, D])
        zb = sb("zb", [P, TILES, D])
        zT = sb("zT", [P, 2, BLK])
        qk = sb("qk", [P, 2, BT, 2 * D])
        v = sb("v", [P, 2, BT, D])
        e = sb("e", [P, 2, BT, 2 * D])
        m = sb("m", [P, 2, BT, 2 * D])
        el = sb("el", [P, 2, BT, 2, D])
        sq = sb("sq", [P, 2, BT, D])
        norm = sb("norm", [P, 2, BT, HEADS])
        lnn = sb("lnn", [P, 2, BT, HEADS])
        rnorm = sb("rnorm", [P, 2, BT, HEADS])
        kn = sb("kn", [P, 2, BT, D])
        qT = sb("qT", [P, 2, BLK])
        vk = sb("vk", [P, D])
        vko = sb("vko", [P, D])
        y = sb("y", [P, 2, BT, D])
        yn = sb("yn", [P, 2, BT, D])

        ps_zT = ps("ps_zT", [P, BLK])
        ps_qT = ps("ps_qT", [P, BLK])
        ps_qkv = ps("ps_qkv", [P, BT, 512])
        ps_vk = ps("ps_vk", [P, 512])
        ps_o = ps("ps_o", [P, BT, D])

        ln1_steps, ln2_steps = sem("ln1_steps"), sem("ln2_steps")
        z_ready, zb_ready, zT_ps, zT_ready, qkv_ps, qk_ready, em_ready, el_ready, qT_ps, qT_ready = (
            sem(n) for n in ("z_ready", "zb_ready", "zT_ps", "zT_ready", "qkv_ps", "qk_ready", "em_ready",
                             "el_ready", "qT_ps", "qT_ready"))
        sq_ready, norm_ready, lnn_ready, rnorm_ready, kn_ready, vk_ps, vk_ready, vko_ps, vko_ready = (
            sem(n) for n in ("sq_ready", "norm_ready", "lnn_ready", "rnorm_ready", "kn_ready", "vk_ps", "vk_ready",
                             "vko_ps", "vko_ready"))
        o_ps, y_ready, yn_ready, beta_added, scaled, x_done = (
            sem(n) for n in ("o_ps", "y_ready", "yn_ready", "beta_added", "scaled", "x_done"))

        def turns(eng, turn):
            turn(-1, 0, (1,))
            turn(-1, 1, (1, 2))
            turn(0, 0, (1, 2, 3))
            turn(0, 1, (1, 2, 3))
            with eng.Fori(1, BATCH - 1) as b:
                for g in range(2):
                    turn(b, g, (1, 2, 3, 4))
            turn(BATCH - 1, 0, (2, 3, 4))
            turn(BATCH - 1, 1, (3, 4))
            turn(BATCH, 0, (4,))
            turn(BATCH, 1, (4,))

        def per_head(ap):
            return ap.rearrange("p t (h f) -> p (t h) f", f=HD)

        block = ctx.enter_context(nc.Block())

        @block.vector
        def _(dve):
            flat = "p t f -> p (t f)"

            def turn(b, g, stages):
                n = 2 * b + g
                nxt, o = n + 1, 1 - g
                if 1 in stages:
                    k1 = n + 2
                    steps1 = Steps(dve, ln1_steps, k1 * LayerNorm.STEPS)
                    xt = lambda t: x[:, k1 * BT + t, :]
                    ln1.statistics(nc, dve, steps1, k1, g, xt)
                if 3 in stages:
                    dve.wait_ge(em_ready, n + 1)
                    nc.vector.scalar_tensor_tensor(
                        out=el[:, g, :, :, :].rearrange("p t a d -> p (t a d)"), in0=e[:, g, :, :].rearrange(flat),
                        scalar=1.0, in1=m[:, g, :, :].rearrange(flat), op0=ALU.min,
                        op1=ALU.add).then_inc(el_ready, 1)
                if 4 in stages and g == 0:
                    dve.wait_ge(vk_ps, b)
                    nc.vector.tensor_tensor(vk[:], ps_vk[:, 0:D], heads[:], ALU.mult).then_inc(vk_ready, 1)
                if 1 in stages:
                    if 3 in stages:
                        dve.wait_ge(zb_ready, n + 1)
                    ln1.normalize(nc, dve, steps1, k1, g, lambda t: z[:, g, t, :], xt).then_inc(z_ready, 1)
                if 4 in stages:
                    k4 = n - 2
                    dve.wait_ge(o_ps, k4 + 1)
                    dve.wait_ge(zb_ready, k4 + 1)
                    nc.vector.tensor_tensor(y[:, g, :, :], zb[:, bass.ds(k4 * BT, BT), :], ps_o[:],
                                            ALU.add).then_inc(y_ready, 1)
                    dve.wait_ge(y_ready, k4 + 1)
                    steps2 = Steps(dve, ln2_steps, k4 * LayerNorm.STEPS)
                    yt = lambda t: y[:, g, t, :]
                    ln2.statistics(nc, dve, steps2, k4, g, yt)
                if 3 in stages:
                    dve.wait_ge(sq_ready, n + 1)
                    nc.vector.tensor_reduce(norm[:, g, :, :].rearrange("p t h -> p (t h)"), per_head(sq[:, g, :, :]),
                                            AX_X, ALU.add).then_inc(norm_ready, 1)
                if 2 in stages:
                    dve.wait_ge(qkv_ps, nxt + 1)
                    nc.vector.tensor_tensor(v[:, o, :, :], ps_qkv[:, :, 2 * D:3 * D],
                                            bc(bias[:, 2, :], 1, [P, BT, D]), ALU.add)
                    nc.vector.tensor_tensor(qk[:, o, :, :], ps_qkv[:, :, 0:2 * D],
                                            bc(bias[:, 0:2, :].rearrange("p a d -> p (a d)"), 1, [P, BT, 2 * D]),
                                            ALU.add).then_inc(qk_ready, 1)
                if 4 in stages:
                    if 3 not in stages:
                        dve.wait_ge(x_done, k4 - 1)
                    ln2.normalize(nc, dve, steps2, k4, g, lambda t: yn[:, g, t, :], yt).then_inc(yn_ready, 1)
                if 3 in stages:
                    dve.wait_ge(rnorm_ready, n + 1)
                    nc.vector.tensor_tensor(kn[:, g, :, :].rearrange("p t (h f) -> p (t h) f", f=HD),
                                            el[:, g, :, 1, :].rearrange("p t (h f) -> p t h f", f=HD),
                                            bc(rnorm[:, g, :, :].rearrange("p t h -> p (t h)"), 2, [P, BT * HEADS, HD]),
                                            ALU.mult).then_inc(kn_ready, 1)

            turns(dve, turn)

        @block.scalar
        def _(act):
            nc.scalar.preload_act_table_set(ACT_TABLES)

            def turn(b, g, stages):
                n = 2 * b + g
                nxt, o = n + 1, 1 - g
                if 2 in stages:
                    act.wait_ge(zT_ps, nxt + 1)
                    nc.scalar.copy(zT[:, o, :], ps_zT[:]).then_inc(zT_ready, 1)
                if 1 in stages:
                    ln1.scale(nc, act, n + 2, g)
                if 4 in stages and g == 0:
                    act.wait_ge(vko_ps, b)
                    nc.scalar.copy(vko[:], ps_vk[:, D:2 * D]).then_inc(vko_ready, 1)
                if 3 in stages:
                    act.wait_ge(qT_ps, n + 1)
                    nc.scalar.copy(qT[:, g, :], ps_qT[:]).then_inc(qT_ready, 1)
                if 4 in stages:
                    ln2.scale(nc, act, n - 2, g)
                if 3 in stages:
                    act.wait_ge(norm_ready, n + 1)
                    nc.scalar.activation(lnn[:, g, :, :], norm[:, g, :, :], ACT.Ln, bias=eps[:, 1:2]).then_inc(lnn_ready, 1)
                    act.wait_ge(lnn_ready, n + 1)
                    nc.scalar.activation(rnorm[:, g, :, :], lnn[:, g, :, :], ACT.Exp, scale=-0.5).then_inc(rnorm_ready, 1)
                if 2 in stages:
                    act.wait_ge(qk_ready, nxt + 1)
                    nc.scalar.activation(e[:, o, :, :], qk[:, o, :, :], ACT.Exp)
                    nc.scalar.activation(m[:, o, :, :], qk[:, o, :, :], ACT.Relu).then_inc(em_ready, 1)

            turns(act, turn)

        @block.gpsimd
        def _(pool):
            def turn(b, g, stages):
                n = 2 * b + g
                if 3 in stages:
                    pool.wait_ge(el_ready, n + 1)
                    nc.gpsimd.tensor_tensor(sq[:, g, :, :], el[:, g, :, 1, :], el[:, g, :, 1, :],
                                            ALU.mult).then_inc(sq_ready, 1)
                if 1 in stages:
                    tiles = bass.ds((n + 2) * BT, BT)
                    pool.wait_ge(z_ready, n + 3)
                    nc.gpsimd.tensor_tensor(zb[:, tiles, :], z[:, g, :, :], bc(rows[:, 0, :], 1, [P, BT, D]),
                                            ALU.add).then_inc(zb_ready, 1)
                    nc.gpsimd.tensor_tensor(x[:, tiles, :], x[:, tiles, :], bc(rows[:, 2, :], 1, [P, BT, D]),
                                            ALU.add).then_inc(beta_added, 1)
                if 4 in stages:
                    k4 = n - 2
                    tiles = bass.ds(k4 * BT, BT)
                    pool.wait_ge(yn_ready, k4 + 1)
                    nc.gpsimd.tensor_tensor(yn[:, g, :, :], yn[:, g, :, :], bc(rows[:, 1, :], 1, [P, BT, D]),
                                            ALU.mult).then_inc(scaled, 1)
                    pool.wait_ge(beta_added, k4 + 1)
                    pool.wait_ge(scaled, k4 + 1)
                    nc.gpsimd.tensor_tensor(x[:, tiles, :], x[:, tiles, :], yn[:, g, :, :],
                                            ALU.add).then_inc(x_done, 1)

            turns(pool, turn)

        @block.tensor
        def _(pe):
            def turn(b, g, stages):
                n = 2 * b + g
                nxt, o = n + 1, 1 - g
                if 2 in stages:
                    pe.wait_ge(z_ready, nxt + 1)
                    for t in range(BT):
                        last = nc.tensor.transpose(ps_zT[:, t * P:(t + 1) * P], z[:, o, t, :], ident[:])
                    last.then_inc(zT_ps, 1)
                    pe.wait_ge(zT_ready, nxt + 1)
                    if 3 in stages:
                        pe.wait_ge(qk_ready, nxt)
                    for t in range(BT):
                        last = nc.tensor.matmul(ps_qkv[:, t, 0:3 * D], zT[:, o, t * P:(t + 1) * P],
                                                w[:].rearrange("p a d -> p (a d)"), start=True, stop=True)
                    last.then_inc(qkv_ps, 1)
                if 4 in stages:
                    if g == 0:
                        pe.wait_ge(vk_ready, b)
                        nc.tensor.matmul(ps_vk[:, D:2 * D], vk[:], wo[:], start=True, stop=True).then_inc(vko_ps, 1)
                        pe.wait_ge(vko_ready, b)
                    if 3 not in stages and g == 1:
                        pe.wait_ge(y_ready, n - 2)
                    for t in range(BT):
                        last = nc.tensor.matmul(ps_o[:, t, :], qT[:, g, t * P:(t + 1) * P], vko[:],
                                                start=True, stop=True)
                    last.then_inc(o_ps, 1)
                if 3 in stages:
                    if 2 not in stages:
                        pe.wait_ge(qT_ready, n)
                    pe.wait_ge(el_ready, n + 1)
                    for t in range(BT):
                        last = nc.tensor.transpose(ps_qT[:, t * P:(t + 1) * P], el[:, g, t, 0, :], ident[:])
                    last.then_inc(qT_ps, 1)
                    pe.wait_ge(kn_ready, n + 1)
                    for t in range(BT):
                        last = nc.tensor.matmul(ps_vk[:, 0:D], v[:, g, t, :], kn[:, g, t, :],
                                                start=(g == 0 and t == 0), stop=(g == 1 and t == BT - 1))
                    if g == 1:
                        last.then_inc(vk_ps, 1)

            turns(pe, turn)


def constants():
    import numpy as np

    f32 = np.float32
    half = HD // 2
    theta = (f32(1.0) / np.power(f32(1250), np.arange(half, dtype=f32) / f32(half))).astype(f32)
    angles = (np.arange(SEQ, dtype=f32)[:, None] * theta[None, :]).astype(f32)
    cos, sin = np.cos(angles).astype(f32), np.sin(angles).astype(f32)

    def table(even, odd):
        pairs = np.stack([even, odd], axis=-1).reshape(SEQ_TILES, P, HD)
        return np.ascontiguousarray(pairs.transpose(1, 0, 2))

    before = np.tril(np.ones((EXPERTS, EXPERTS), f32), -1)
    pick = np.zeros((P, ROUTED + 1, P), f32)
    for c in range(ROUTED):
        for part in range(PARTS):
            for a in range(2):
                pick[part * EXPERTS + 2 * c + a, c, a * INTER:(a + 1) * INTER] = 1
    pick[:, ROUTED, :] = np.eye(P)
    head = np.arange(D) // HD
    bf16 = mybir.dt.np(BF16)
    return {"earlier": np.ascontiguousarray(np.broadcast_to(before, (P, EXPERTS, EXPERTS))).astype(bf16),
            "pick": pick.astype(bf16), "heads": (head[:, None] == head[None, :]).astype(f32),
            "ident": np.eye(P, dtype=f32), "cos": table(cos, cos), "sin": table(-sin, sin)}


def kernel(**inputs):
    import concourse.bacc as bacc
    import numpy as np
    from concourse.bass_utils import run_bass_kernel_spmd as run

    a = {name.split("_", 1)[1]: np.asarray(array) for name, array in inputs.items()}
    c = constants()
    arrays = {
        "x_in": a["attn_a_x"], "w_qkv": a["attn_a_w_qkv"], "b_qkv": a["attn_a_b_qkv"],
        "w_out": a["attn_a_w_out"], "b_out": a["attn_a_b_out"],
        "Wq": a["attn_b_Wq"], "bq": a["attn_b_bq"], "Wk": a["attn_b_Wk"], "bk": a["attn_b_bk"],
        "Wv": a["attn_b_Wv"], "bv": a["attn_b_bv"], "Wo": a["attn_b_Wo"], "bo": a["attn_b_bo"],
        "gamma": a["attn_b_gamma"], "beta": a["attn_b_beta"],
        "gate_t": a["ffn_gate_w"].T, "bias_e": a["ffn_bias_e"],
        "up_t": np.concatenate([a["ffn_up_w"].reshape(EXPERTS * INTER, D), a["ffn_shared_up"]]).T,
        "down_t": np.concatenate([a["ffn_down_w"].transpose(0, 2, 1).reshape(EXPERTS * INTER, D),
                                  a["ffn_shared_down"].T]),
        "ident_in": c["ident"], "cos_in": c["cos"], "sin_in": c["sin"],
        "earlier_in": c["earlier"], "pick_in": c["pick"], "heads_in": c["heads"],
    }
    arrays = {name: np.ascontiguousarray(array) for name, array in arrays.items()}
    nc = bacc.Bacc("TRN2", target_bir_lowering=False, num_devices=1)
    args = {name: nc.dram_tensor(f"in_{name}_dram", array.shape, mybir.dt.from_np(array.dtype),
                                 kind="ExternalInput").ap() for name, array in arrays.items()}
    out = nc.dram_tensor("out_0_dram", (BATCH, SEQ, D), F32, kind="ExternalOutput").ap()
    hybrid_kernel(nc, out=out, **args)
    r = run(nc, [{f"in_{name}_dram": array for name, array in arrays.items()}], core_ids=[0])
    return r.results[0]["out_0_dram"]
```

```python
from contextlib import ExitStack

import concourse.bass as bass
from concourse import mybir

ALU = mybir.AluOpType
ACT = mybir.ActivationFunctionType
F32 = mybir.dt.float32
BF16 = mybir.dt.bfloat16
AX_X = mybir.AxisListType.X

P = 128
BATCH, SEQ, D = 4, 1024, 128
TILES = BATCH * SEQ // P
SEQ_TILES = SEQ // P
HEADS = 16
HD = D // HEADS
BLK = 512
BT = BLK // P
BLOCKS = BATCH * SEQ // BLK
LN_EPS = 1e-5
B_EPS = 1e-6
ACT_TABLES = "natural_log_exp_and_others"

PARTS = 3
STACK = PARTS * PARTS * HD
STACK_K = 96
PAIRS = BATCH * HEADS // 2
HALVES = SEQ // BLK
KV = HD * HD

EXPERTS, GROUPS, TOP_K, TOP_GROUPS = 16, 4, 4, 2
PER_GROUP = EXPERTS // GROUPS
INTER, SHARED = 64, 256
ROUTED = EXPERTS * INTER // P
CHUNKS = ROUTED + SHARED // P
ROUTED_SCALE = 2.5
GATE_COLS = 128
TURN_AT, GATES_AT = 0, 1
ROUTE_PIECES = [0, 0, 2, 1, 2, 2, 1, 3]


class Steps:

    def __init__(self, eng, sem, base=0):
        self.eng, self.sem, self.base, self.n = eng, sem, base, 0

    def then_wait(self, ins):
        self.n += 1
        ins.then_inc(self.sem, 1)
        self.eng.wait_ge(self.sem, self.base + self.n)

    def mark(self, ins):
        self.n += 1
        ins.then_inc(self.sem, 1)

    def wait_apart(self):
        self.eng.wait_ge(self.sem, self.base + self.n)
        self.n += 1
        self.eng.sem_inc(self.sem, 1)


def bc(ap, axis, shape):
    return ap.unsqueeze(axis).to_broadcast(shape)


def row_to_all(ap):
    return ap.unsqueeze(0).to_broadcast([P, ap.shape[0]])


VEC_UNITS = [(0, 1, 0), (0, 1, 1), (0, 4, 1), (1, 3, 0), (1, 3, 1)]
ACT_UNITS = [(u, j, [a for a in range(2) if (u, j, a) not in VEC_UNITS])
             for u in range(HALVES) for j in range(SEQ_TILES)]
ACT_UNITS = [unit for unit in ACT_UNITS if unit[2]]
NA, NV = len(ACT_UNITS), len(VEC_UNITS)
GROUP = 2
S_SLOTS = 2
V_SLOTS = 2
ROTATE_0 = 1 + max(t for t, unit in enumerate(VEC_UNITS) if unit[0] == 0)


def pair_order():
    fixed, head, vec, other = FIX_T, HEAD_T, VEC_T, 0.6
    steps, now = [], 0.0
    for first in range(0, NA, GROUP):
        units = range(first, first + GROUP)
        for n in units:
            now += fixed + head * len(ACT_UNITS[(n + GROUP) % NA][2])
            steps.append((now, 0, "score_act", n + GROUP + S_SLOTS))
        now += fixed + head * sum(len(ACT_UNITS[n][2]) for n in units)
        for n in units:
            steps.append((now, 1, "use_act", n))
    now = 0.0
    for t in range(NV):
        if t == ROTATE_0:
            now += other
            steps.append((now + LATE, 3, "project", 0))
        now += vec
        steps.append((now, 0, "score_vec", t + V_SLOTS))
        steps.append((now + LATE, 2, "use_vec", t))
        if t == 0:
            now += other
            steps.append((now + LATE, 3, "project_before", 1))
        if t in (1, ROTATE_0):
            now += other
    steps.sort()
    return [(kind, n) for _, _, kind, n in steps]


FIX_T, HEAD_T, VEC_T, LATE = 0.17, 0.385, 4.3, 1.0


def hybrid_kernel(nc, x_in, w_qkv, b_qkv, w_out, b_out, Wq, bq, Wk, bk, Wv, bv, Wo, bo, gamma, beta,
                  gate_t, bias_e, up_t, down_t, ident_in, cos_in, sin_in, earlier_in, pick_in,
                  heads_in, out):
    x_dram = x_in.rearrange("b (t p) d -> p (b t) d", p=P)
    out_dram = out.rearrange("b (t p) d -> p (b t) d", p=P)
    scratch = (nc.dram_tensor("qk_scr", [BATCH, PARTS, 2, D, SEQ], BF16).ap(),
               nc.dram_tensor("rq_scr", [BATCH, D, SEQ], F32).ap())

    with ExitStack() as whole:
        def sb(name, shape, dt=F32):
            return whole.enter_context(nc.sbuf_tensor(name, shape, dt))

        x = sb("x", [P, TILES, D])
        ident = sb("ident", [P, P])
        eps = sb("eps", [P, 2])
        ffn = {"gate": sb("gate", [P, GATE_COLS]), "up": sb("up", [P, CHUNKS, P]), "down": sb("down", [P, CHUNKS, D]),
               "bias": sb("bias_e", [P, EXPERTS]),
               "earlier": sb("earlier", [P, EXPERTS, EXPERTS], BF16),
               "pick": sb("pick", [P, ROUTED, P], BF16),
               "identb": sb("identb", [P, P], BF16)}
        att_b = {"w": sb("w_b", [P, 3, D]), "wo": sb("wo_b", [P, D]), "bias": sb("bias_b", [P, 3, D]),
                 "rows": sb("rows_b", [P, 3, D]),
                 "heads": sb("heads", [P, D])}
        later = [(ffn["gate"][:, 0:EXPERTS], gate_t), (ffn["up"][:], up_t.rearrange("d (c i) -> d c i", i=P)),
                 (ffn["down"][:], down_t.rearrange("(c i) d -> i c d", i=P)), (ffn["bias"][:], row_to_all(bias_e)),
                 (ffn["earlier"][:], earlier_in), (ffn["pick"][:], pick_in[:, 0:ROUTED, :]),
                 (ffn["identb"][:], pick_in[:, ROUTED, :]), (att_b["wo"][:], Wo), (att_b["heads"][:], heads_in)]
        for a, (weight, vector) in enumerate(((Wq, bq), (Wk, bk), (Wv, bv))):
            later += [(att_b["w"][:, a, :], weight), (att_b["bias"][:, a, :], row_to_all(vector))]
        for a, vector in enumerate((bo, gamma, beta)):
            later.append((att_b["rows"][:, a, :], row_to_all(vector)))

        with ExitStack() as both:
            rk = both.enter_context(nc.sbuf_tensor("rk", [P, BATCH, HEADS // 2, SEQ_TILES, 2 * HD], F32))
            v = both.enter_context(nc.sbuf_tensor("v", [P, BATCH, HEADS // 2, SEQ_TILES, 2 * HD], F32))
            wo = both.enter_context(nc.sbuf_tensor("wo", [P, HEADS // 2, D], F32))
            stacks = Stacks(nc, both, scratch)
            for h in range(HEADS):
                later.append((wo[(h % 2) * KV:(h % 2 + 1) * KV, h // 2, :],
                              bc(w_out[h * HD:(h + 1) * HD, :], 0, [HD, HD, D])))
            project_a(nc, x_dram, w_qkv, b_qkv, b_out, ident_in, cos_in, sin_in, later, x, ident, eps, rk, v,
                      scratch, stacks, ffn["gate"])
            attend_a(nc, wo, x, rk, v, stacks)
        experts(nc, "f1", ffn, x, ident, eps)
        attend_b(nc, att_b, x, ident, eps)
        experts(nc, "f2", ffn, x, ident, eps, out_dram)


class Stacks:

    LOADS = 16 * (2 * 2 * PARTS + 1)

    def __init__(self, nc, ctx, scratch):
        self.scratch = scratch
        self.q = ctx.enter_context(nc.sbuf_tensor("q_st", [P, 2, 2, SEQ], BF16))
        self.k = ctx.enter_context(nc.sbuf_tensor("k_st", [P, 2, 2, SEQ], BF16))
        self.rq = ctx.enter_context(nc.sbuf_tensor("rq_rep", [P, 2, SEQ], F32))
        self.loaded = [ctx.enter_context(nc.semaphore(f"loaded{s}")) for s in range(2)]

    def load(self, sp, n, s):
        qk_scr, rq_scr = self.scratch
        b, hp = n // (HEADS // 2), n % (HEADS // 2)
        for a in range(2):
            head = bass.ds((2 * hp + a) * HD, HD)
            for r in range(PARTS):
                rows = slice(r * PARTS * HD, (r + 1) * PARTS * HD)
                sp.dma_start(self.q[rows, s, a, :], bc(qk_scr[b, r, 0, head, :], 0, [PARTS, HD, SEQ])
                             ).then_inc(self.loaded[s], 16)
                sp.dma_start(self.k[rows, s, a, :], qk_scr[b, :, 1, head, :]).then_inc(self.loaded[s], 16)
        sp.dma_start(self.rq[:, s, :], bc(rq_scr[b, bass.ds(hp * 2 * HD, 2 * HD), :], 1, [2 * HD, HD, SEQ])
                     ).then_inc(self.loaded[s], 16)


def project_a(nc, x_dram, w_qkv, b_qkv, b_out, ident_in, cos_in, sin_in, later, x, ident, eps, rk, v,
              scratch, stacks, gate):
    qk_scr, rq_scr = scratch
    with ExitStack() as ctx:
        def sb(name, shape, dt=F32):
            return ctx.enter_context(nc.sbuf_tensor(name, shape, dt))

        def sem(name):
            return ctx.enter_context(nc.semaphore(name))

        w = sb("w", [P, 3 * D])
        bias = sb("bias", [P, 3 * D])
        bias_out = sb("bias_out", [P, D])
        cos = sb("cos", [P, SEQ_TILES, HD])
        sin = sb("sin", [P, SEQ_TILES, HD])
        ln = LayerNorm("ln", sb, sem, eps[:, 0:1])
        xn = sb("xn", [P, 2, BT, D])
        xnT = sb("xnT", [P, 2, BLK])
        qk = sb("qk", [P, 2, BT, 2 * D])
        e = sb("e", [P, 2, BT, 2 * D])
        m = sb("m", [P, 2, BT, 2 * D])
        el = sb("el", [P, 2, BT, 2 * D])
        ra = sb("ra", [P, BT, 2 * D])
        rb = sb("rb", [P, 2, BT, 2 * D])
        rq = sb("rq", [P, 2, BT, D])
        rqT = sb("rqT", [P, 2, BLK])
        rest = sb("rest", [P, 2, BLK])
        parts = sb("parts", [P, 2, PARTS, 2, BLK], BF16)

        ps_xT = ctx.enter_context(nc.psum_tensor("ps_xT", [P, BLK], F32))
        ps_qkv = ctx.enter_context(nc.psum_tensor("ps_qkv", [P, BT, 512], F32))
        ps_T = ctx.enter_context(nc.psum_tensor("ps_T", [P, 3, BLK], F32))

        x_loaded = [sem(f"x_loaded{b}") for b in range(BATCH)]
        w_loaded, later_loaded, set_up = sem("w_loaded"), sem("later_loaded"), sem("set_up")
        ln_steps, pool_steps, xn_ready = sem("ln_steps"), sem("pool_steps"), sem("xn_ready")
        xnT_ps, xnT_ready, qkv_ps, qk_ready = sem("xnT_ps"), sem("xnT_ready"), sem("qkv_ps"), sem("qk_ready")
        em_ready, el_ready, rb_ready = sem("em_ready"), sem("el_ready"), sem("rb_ready")
        rot_ready = sem("rot_ready")
        qkT_ps, rqT_ps, rqT_ready = sem("qkT_ps"), sem("rqT_ps"), sem("rqT_ready")
        part0_ready, rest_ready, part1_ready, parts_ready = (
            sem("part0_ready"), sem("rest_ready"), sem("part1_ready"), sem("parts_ready"))
        scratch_written = [sem("scratch_written0"), sem("scratch_written1")]
        WRITES = 16 * 2

        def turns(eng, turn):
            turn(-1, 0, (1,))
            turn(-1, 1, (1, 2))
            with eng.Fori(0, BLOCKS // 2 - 1) as b:
                for g in range(2):
                    turn(b, g, (1, 2, 3))
            turn(BLOCKS // 2 - 1, 0, (2, 3))
            turn(BLOCKS // 2 - 1, 1, (3,))

        block = ctx.enter_context(nc.Block())

        @block.sync
        def _(sp):
            for b in range(BATCH):
                tiles = slice(b * SEQ_TILES, (b + 1) * SEQ_TILES)
                sp.dma_start(x[:, tiles, :], x_dram[:, tiles, :]).then_inc(x_loaded[b], 16)
                if b == 0:
                    for dst, src in ((ident[:], ident_in), (w[:], w_qkv), (bias[:], row_to_all(b_qkv)),
                                     (bias_out[:], row_to_all(b_out)), (cos[:], cos_in), (sin[:], sin_in)):
                        sp.dma_start(dst, src).then_inc(w_loaded, 16)
            for dst, src in later:
                sp.dma_start(dst, src).then_inc(later_loaded, 16)
            for g in range(2):
                sp.sem_inc(scratch_written[g], 16)

            def write(b):
                for g in range(2):
                    sp.wait_ge(parts_ready, 2 * b + g + 1)
                    sp.wait_ge(rqT_ready, 2 * b + g + 1)
                    tok = slice(g * BLK, (g + 1) * BLK)
                    sp.dma_start(qk_scr[b, :, :, :, tok].rearrange("s a d n -> d (s a) n"),
                                 parts[:, g, :, :, :].rearrange("d s a n -> d (s a) n")).then_inc(scratch_written[g], 16)
                    sp.dma_start(rq_scr[b, :, tok], rqT[:, g, :]).then_inc(scratch_written[g], 16)

            with sp.Fori(0, BATCH - 1) as b:
                write(b)
            for g in range(2):
                sp.wait_ge(scratch_written[g], WRITES * (BATCH - 1) + 16)
            sp.wait_ge(set_up, 1)
            for s in range(2):
                stacks.load(sp, s, s)
            write(BATCH - 1)
            for g in range(2):
                sp.wait_ge(scratch_written[g], WRITES * BATCH + 16)
            sp.wait_ge(later_loaded, 16 * len(later))

        @block.vector
        def _(dve):
            nc.vector.memset(eps[:, 0:1], LN_EPS)
            nc.vector.memset(eps[:, 1:2], B_EPS)
            nc.vector.memset(gate[:, EXPERTS:GATE_COLS], 0.0)
            nc.vector.memset(stacks.q[64:STACK_K, :, :, :], 0.0)
            nc.vector.memset(stacks.k[64:STACK_K, :, :, :], 0.0).then_inc(set_up, 1)
            dve.sem_inc(rest_ready, 1)
            flat = "p t f -> p (t f)"

            def bias_qkv(b, g):
                n = 2 * b + g
                dve.wait_ge(qkv_ps, n + 1)
                nc.vector.tensor_tensor(
                    v[:, b, :, g * BT:(g + 1) * BT, :].rearrange("p h t f -> p t h f"),
                    ps_qkv[:, :, 2 * D:3 * D].rearrange("p t (h f) -> p t h f", f=2 * HD),
                    bc(bias[:, 2 * D:3 * D].rearrange("p (h f) -> p h f", f=2 * HD), 1,
                       [P, BT, HEADS // 2, 2 * HD]), ALU.add)
                nc.vector.tensor_tensor(qk[:, g, :, :], ps_qkv[:, :, 0:2 * D],
                                        bc(bias[:, 0:2 * D], 1, [P, BT, 2 * D]), ALU.add).then_inc(qk_ready, 1)

            def elu_and_sines(b, g):
                n = 2 * b + g
                dve.wait_ge(em_ready, n + 1)
                nc.vector.scalar_tensor_tensor(
                    out=el[:, g, :, :].rearrange(flat), in0=e[:, g, :, :].rearrange(flat), scalar=1.0,
                    in1=m[:, g, :, :].rearrange(flat), op0=ALU.min, op1=ALU.add).then_inc(el_ready, 1)
                dve.wait_ge(el_ready, n + 1)
                ev = el[:, g, :, :].rearrange("p t (h f two) -> p t h f two", two=2, f=HD // 2)
                rv = rb[:, g, :, :].rearrange("p t (h f two) -> p t h f two", two=2, f=HD // 2)
                sv = sin[:, g * BT:(g + 1) * BT, :].rearrange("p t (f two) -> p t f two", two=2)
                for a in range(2):
                    last = nc.vector.tensor_tensor(
                        rv[:, :, :, :, a], ev[:, :, :, :, 1 - a],
                        bc(sv[:, :, :, a], 2, [P, BT, 2 * HEADS, HD // 2]), ALU.mult)
                last.then_inc(rb_ready, 1)

            def split(b, g):
                n = 2 * b + g
                dve.wait_ge(part0_ready, n + 1)
                nc.vector.tensor_tensor(rest[:], ps_T[:, 0:2, :], parts[:, g, 0, :, :],
                                        ALU.subtract).then_inc(rest_ready, 1)
                dve.wait_ge(rest_ready, n + 2)
                nc.vector.tensor_copy(parts[:, g, 1, :, :], rest[:]).then_inc(part1_ready, 1)
                dve.wait_ge(part1_ready, n + 1)
                nc.vector.tensor_tensor(parts[:, g, 2, :, :], rest[:], parts[:, g, 1, :, :],
                                        ALU.subtract).then_inc(parts_ready, 1)

            def turn(b, g, stages):
                if 1 in stages:
                    n = 2 * b + 2 + g
                    steps = Steps(dve, ln_steps, n * LayerNorm.STEPS)
                    tile = lambda t: x[:, n * BT + t, :]
                    ln.statistics(nc, dve, steps, n, g, tile)
                if 3 in stages:
                    elu_and_sines(b, g)
                if 1 in stages:
                    ln.normalize(nc, dve, steps, n, g, lambda t: xn[:, g, t, :], tile).then_inc(xn_ready, 1)
                if 2 in stages:
                    if g:
                        bias_qkv(b + 1, 0)
                    else:
                        bias_qkv(b, 1)
                if 3 in stages:
                    split(b, g)

            for b in range(BATCH):
                dve.wait_ge(x_loaded[b], 16)
            dve.wait_ge(w_loaded, 16 * 6)
            turns(dve, turn)

        @block.scalar
        def _(act):
            nc.scalar.preload_act_table_set(ACT_TABLES)
            act.wait_ge(set_up, 1)

            def turn(b, g, stages):
                if 2 in stages:
                    n, o = 2 * b + g + 1, 1 - g
                    act.wait_ge(xnT_ps, n + 1)
                    nc.scalar.copy(xnT[:, o, :], ps_xT[:]).then_inc(xnT_ready, 1)
                if 1 in stages:
                    ln.scale(nc, act, 2 * b + g + 2, g)
                if 3 in stages:
                    n = 2 * b + g
                    act.wait_ge(qkT_ps, n + 1)
                    act.wait_ge(scratch_written[g], WRITES * b + 16)
                    nc.scalar.copy(parts[:, g, 0, :, :], ps_T[:, 0:2, :]).then_inc(part0_ready, 1)
                if 2 in stages:
                    n, o = 2 * b + g + 1, 1 - g
                    act.wait_ge(qk_ready, n + 1)
                    nc.scalar.activation(e[:, o, :, :], qk[:, o, :, :], ACT.Exp)
                    nc.scalar.activation(m[:, o, :, :], qk[:, o, :, :], ACT.Relu).then_inc(em_ready, 1)
                if 3 in stages:
                    n = 2 * b + g
                    act.wait_ge(rqT_ps, n + 1)
                    nc.scalar.copy(rqT[:, g, :], ps_T[:, 2, :]).then_inc(rqT_ready, 1)

            turns(act, turn)

        @block.gpsimd
        def _(pool):
            pool.wait_ge(w_loaded, 16 * 6)

            def turn(b, g, stages):
                if 3 in stages:
                    n = 2 * b + g
                    pool.wait_ge(el_ready, n + 1)
                    nc.gpsimd.tensor_tensor(
                        ra[:].rearrange("p t (h f) -> p t h f", f=HD),
                        el[:, g, :, :].rearrange("p t (h f) -> p t h f", f=HD),
                        bc(cos[:, g * BT:(g + 1) * BT, :], 2, [P, BT, 2 * HEADS, HD]),
                        ALU.mult).then_inc(pool_steps, 1)
                    pool.wait_ge(pool_steps, n + 1)
                    pool.wait_ge(rb_ready, n + 1)
                    nc.gpsimd.tensor_tensor(
                        rk[:, b, :, g * BT:(g + 1) * BT, :].rearrange("p h t f -> p t h f"),
                        ra[:, :, D:2 * D].rearrange("p t (h f) -> p t h f", f=2 * HD),
                        rb[:, g, :, D:2 * D].rearrange("p t (h f) -> p t h f", f=2 * HD),
                        ALU.add)
                    nc.gpsimd.tensor_tensor(rq[:, g, :, :], ra[:, :, 0:D], rb[:, g, :, 0:D],
                                            ALU.add).then_inc(rot_ready, 1)
                    pool.wait_ge(rot_ready, n + 1)
                if 1 in stages:
                    n = 2 * b + g + 2
                    pool.wait_ge(xn_ready, n + 1)
                    nc.gpsimd.tensor_tensor(x[:, bass.ds(n * BT, BT), :], x[:, bass.ds(n * BT, BT), :],
                                            bc(bias_out[:], 1, [P, BT, D]), ALU.add)

            turns(pool, turn)

        @block.tensor
        def _(pe):
            pe.wait_ge(w_loaded, 16 * 6)

            def turn(b, g, stages):
                if 2 in stages:
                    n, o = 2 * b + g + 1, 1 - g
                    pe.wait_ge(xn_ready, n + 1)
                    for t in range(BT):
                        last = nc.tensor.transpose(ps_xT[:, t * P:(t + 1) * P], xn[:, o, t, :], ident[:])
                    last.then_inc(xnT_ps, 1)
                if 2 in stages:
                    n, o = 2 * b + g + 1, 1 - g
                    pe.wait_ge(xnT_ready, n + 1)
                    if 3 in stages:
                        pe.wait_ge(qk_ready, n)
                    for t in range(BT):
                        last = nc.tensor.matmul(ps_qkv[:, t, 0:3 * D], xnT[:, o, t * P:(t + 1) * P], w[:],
                                                start=True, stop=True)
                    last.then_inc(qkv_ps, 1)
                if 3 in stages:
                    n = 2 * b + g
                    pe.wait_ge(el_ready, n + 1)
                    pe.wait_ge(rest_ready, n + 1)
                    for a in range(2):
                        for t in range(BT):
                            last = nc.tensor.transpose(ps_T[:, a, t * P:(t + 1) * P], el[:, g, t, a * D:(a + 1) * D],
                                                       ident[:])
                    last.then_inc(qkT_ps, 1)
                if 3 in stages:
                    if 2 not in stages:
                        pe.wait_ge(rqT_ready, 2 * b + g)
                    pe.wait_ge(rot_ready, 2 * b + g + 1)
                    for t in range(BT):
                        last = nc.tensor.transpose(ps_T[:, 2, t * P:(t + 1) * P], rq[:, g, t, :], ident[:])
                    last.then_inc(rqT_ps, 1)

            turns(pe, turn)


def attend_a(nc, wo, x, rk, v, stacks):
    with ExitStack() as ctx:
        def sb(name, shape, dt=F32):
            return ctx.enter_context(nc.sbuf_tensor(name, shape, dt))

        def sem(name):
            return ctx.enter_context(nc.semaphore(name))

        q_st, k_st, rq_rep, loaded, LOADS = stacks.q, stacks.k, stacks.rq, stacks.loaded, Stacks.LOADS
        kv = sb("kv", [P, 2, 2, SEQ_TILES, KV])
        r_act = sb("r_act", [P, 2 * NA, BLK])
        r_vec = sb("r_vec", [P, NV, BLK])
        gq = sb("gq", [P, HALVES, BLK])

        ps_act = ctx.enter_context(nc.psum_tensor("ps_act", [P, S_SLOTS, 2, BLK], F32))
        ps_vec = ctx.enter_context(nc.psum_tensor("ps_vec", [P, V_SLOTS, BLK], F32))
        ps_g = ctx.enter_context(nc.psum_tensor("ps_g", [P, HALVES, BLK], F32))

        act_scores, ln_done, act_ready = sem("act_scores"), sem("ln_done"), sem("act_ready")
        vec_scores, vec_ready = sem("vec_scores"), sem("vec_ready")
        kv_ready = sem("kv_ready")
        g_ready, gq_ready, y_ready, x_added = sem("g_ready"), sem("gq_ready"), sem("y_ready"), sem("x_added")

        def pairs(eng, pair):
            pair(0, 0, True, False)
            pair(0, 1, False, False)
            with eng.Fori(1, PAIRS // 2 - 1) as i:
                for s in range(2):
                    pair(i, s, False, False)
            pair(PAIRS // 2 - 1, 0, False, False)
            pair(PAIRS // 2 - 1, 1, False, True)

        block = ctx.enter_context(nc.Block())

        @block.sync
        def _(sp):
            with sp.Fori(0, PAIRS // 2 - 1) as i:
                for s in range(2):
                    sp.wait_ge(gq_ready, HALVES * (2 * i + s + 1))
                    stacks.load(sp, 2 * i + s + 2, s)

        @block.gpsimd
        def _(pool):
            def products(n, s):
                b, hp = n // (HEADS // 2), n % (HEADS // 2)
                for a in range(2):
                    last = nc.gpsimd.tensor_tensor(
                        kv[:, s, a, :, :].rearrange("p t (c d) -> p t c d", d=HD),
                        bc(rk[:, b, hp, :, a * HD:(a + 1) * HD], 3, [P, SEQ_TILES, HD, HD]),
                        bc(v[:, b, hp, :, a * HD:(a + 1) * HD], 2, [P, SEQ_TILES, HD, HD]), ALU.mult)
                last.then_inc(kv_ready, 1)

            for s in range(2):
                products(s, s)
            with pool.Fori(0, PAIRS // 2 - 1) as i:
                for s in range(2):
                    pool.wait_ge(g_ready, HALVES * (2 * i + s + 1))
                    products(2 * i + s + 2, s)

        @block.tensor
        def _(pe):
            def scores(out, s, a, u, j):
                return nc.tensor.matmul(out, k_st[0:STACK_K, s, a, j * P:(j + 1) * P],
                                        q_st[0:STACK_K, s, a, u * BLK:(u + 1) * BLK], start=True, stop=True)

            def score_act(i, s, c, first=False):
                s, c = s + c // NA, c % NA
                u, j, heads = ACT_UNITS[c]
                count = (2 * i + s) * NA + c
                s = s % 2
                if not first:
                    pe.wait_ge(ln_done, count - S_SLOTS + 1)
                for a in heads:
                    last = scores(ps_act[:, (s * NA + c) % S_SLOTS, a, :], s, a, u, j)
                last.then_inc(act_scores, 1)

            def score_vec(i, s, t, first=False):
                s, t = s + t // NV, t % NV
                u, j, a = VEC_UNITS[t]
                count = (2 * i + s) * NV + t
                s = s % 2
                if not first:
                    pe.wait_ge(vec_ready, count - V_SLOTS + 1)
                scores(ps_vec[:, (s * NV + t) % V_SLOTS, :], s, a, u, j).then_inc(vec_scores, 1)

            def pair(i, s, first, last_pair):
                n = 2 * i + s
                opened = set()
                left = {(u, a): SEQ_TILES for u in range(HALVES) for a in range(2)}
                next_loaded = False

                def use(u, j, a, r):
                    if u not in [half for half, _ in opened]:
                        pe.wait_ge(x_added, HALVES * n + u + 1)
                    ins = nc.tensor.matmul(ps_g[a * KV:(a + 1) * KV, u, :], kv[:, s, a, j, :], r,
                                           start=(u, a) not in opened, stop=left[u, a] == 1)
                    opened.add((u, a))
                    left[u, a] -= 1
                    if left[u, 0] == 0 and left[u, 1] == 0:
                        ins.then_inc(g_ready, 1)

                pe.wait_ge(kv_ready, n + 1)
                for kind, c in pair_order():
                    if kind in ("score_act", "score_vec"):
                        own = c < (NA if kind == "score_act" else NV)
                        if not own and last_pair:
                            continue
                        if not own and not next_loaded:
                            pe.wait_ge(loaded[(s + 1) % 2], LOADS * (i + 1 + (s + 1) // 2))
                            next_loaded = True
                        (score_act if kind == "score_act" else score_vec)(i, s, c)
                    elif kind == "project":
                        project(n, c)
                    elif kind == "project_before":
                        if not first:
                            project(n - 1, c)
                    elif kind == "use_act":
                        u, j, heads = ACT_UNITS[c]
                        pe.wait_ge(act_ready, n * (NA // GROUP) + c // GROUP + 1)
                        for a in heads:
                            use(u, j, a, r_act[:, 2 * c + a, :])
                    elif kind == "use_vec":
                        u, j, a = VEC_UNITS[c]
                        pe.wait_ge(vec_ready, n * NV + c + 1)
                        use(u, j, a, r_vec[:, c, :])

            def project(n, u):
                pe.wait_ge(gq_ready, HALVES * n + u + 1)
                for t in range(BT):
                    last = nc.tensor.matmul(ps_g[:, u, t * P:(t + 1) * P], gq[:, u, t * P:(t + 1) * P],
                                            wo[:, n % (HEADS // 2), :], start=True, stop=True)
                last.then_inc(y_ready, 1)

            pe.wait_ge(loaded[0], LOADS)
            for c in range(S_SLOTS):
                score_act(0, 0, c, first=True)
            for c in range(V_SLOTS):
                score_vec(0, 0, c, first=True)
            for c in range(S_SLOTS, S_SLOTS + GROUP):
                score_act(0, 0, c)
            pairs(pe, pair)
            project(PAIRS - 1, 1)

        @block.scalar
        def _(act):
            nc.scalar.preload_act_table_set(ACT_TABLES)

            def ln(n, s, c):
                n, s, c = n + c // NA, (s + c // NA) % 2, c % NA
                heads = ACT_UNITS[c][2]
                act.wait_ge(act_scores, n * NA + c + 1)
                nc.scalar.activation(r_act[:, 2 * c + heads[0]:2 * c + heads[-1] + 1, :],
                                     ps_act[:, (s * NA + c) % S_SLOTS, heads[0]:heads[-1] + 1, :],
                                     ACT.Ln).then_inc(ln_done, 1)

            def pair(i, s, first, last_pair):
                n = 2 * i + s
                if first:
                    for c in range(GROUP):
                        ln(n, s, c)
                for k in range(NA // GROUP):
                    units = range(k * GROUP, (k + 1) * GROUP)
                    for c in units:
                        if c + GROUP < NA or not last_pair:
                            ln(n, s, c + GROUP)
                    rows = [2 * c + a for c in units for a in ACT_UNITS[c][2]]
                    assert rows == list(range(rows[0], rows[-1] + 1))
                    r = r_act[:, rows[0]:rows[-1] + 1, :]
                    act.wait_ge(ln_done, n * NA + units[-1] + 1)
                    nc.scalar.activation(r, r, ACT.Exp, scale=-1.0).then_inc(act_ready, 1)

            pairs(act, pair)

        @block.vector
        def _(dve):
            dve.sem_inc(x_added, HALVES)

            def rotate(n, s, u):
                dve.wait_ge(g_ready, HALVES * n + u + 1)
                nc.vector.tensor_tensor(gq[:, u, :], ps_g[:, u, :], rq_rep[:, s, u * BLK:(u + 1) * BLK],
                                        ALU.mult).then_inc(gq_ready, 1)

            def add(n, u):
                dve.wait_ge(y_ready, HALVES * n + u + 1)
                tiles = x[:, bass.ds((n // (HEADS // 2)) * SEQ_TILES + u * BT, BT), :]
                nc.vector.tensor_tensor(tiles, ps_g[:, u, :].rearrange("p (t d) -> p t d", d=D), tiles,
                                        ALU.add).then_inc(x_added, 1)

            def pair(i, s, first, last_pair):
                n = 2 * i + s
                for t in range(NV):
                    if t == ROTATE_0:
                        rotate(n, s, 0)
                    dve.wait_ge(vec_scores, n * NV + t + 1)
                    nc.vector.reciprocal(r_vec[:, t, :], ps_vec[:, (s * NV + t) % V_SLOTS, :]).then_inc(vec_ready, 1)
                    if t == 0 and not first:
                        rotate(n - 1, 1 - s, 1)
                    if t == 1 and not first:
                        add(n - 1, 1)
                    if t == ROTATE_0:
                        add(n, 0)

            pairs(dve, pair)
            rotate(PAIRS - 1, 1, 1)
            add(PAIRS - 1, 1)


class LayerNorm:

    STEPS = BT + 6

    def __init__(self, name, sb, sem, eps, eps_value=LN_EPS):
        self.stats = sb(name + "_stats", [P, BT, 6])
        self.mv = sb(name + "_mv", [P, 2, BT, 2])
        self.lnv = sb(name + "_lnv", [P, 2, BT])
        self.rstd = sb(name + "_rstd", [P, 2, BT])
        self.newton = sb(name + "_newton", [P, 3, BT])
        self.eps, self.eps_value = eps, eps_value
        self.stats_ready, self.ln_ready, self.rstd_ready = (
            sem(name + "_stats_ready"), sem(name + "_ln_ready"), sem(name + "_rstd_ready"))

    def statistics(self, nc, dve, steps, n, g, tile):
        for t in range(BT):
            steps.mark(nc.vector.bn_stats(self.stats[:, t, :], tile(t)))
        steps.wait_apart()
        for t in range(BT):
            last = nc.vector.bn_aggr(self.mv[:, g, t, :], self.stats[:, t, :])
        last.then_inc(self.stats_ready, 1)
        dve.wait_ge(self.stats_ready, n + 1)

    def scale(self, nc, act, n, g):
        act.wait_ge(self.stats_ready, n + 1)
        nc.scalar.activation(self.lnv[:, g, :], self.mv[:, g, :, 1], ACT.Ln, bias=self.eps).then_inc(self.ln_ready, 1)
        act.wait_ge(self.ln_ready, n + 1)
        nc.scalar.activation(self.rstd[:, g, :], self.lnv[:, g, :], ACT.Exp, scale=-0.5).then_inc(self.rstd_ready, 1)

    def normalize(self, nc, dve, steps, n, g, dst, tile):
        V, (half, t1, r), r0 = nc.vector, (self.newton[:, a, :] for a in range(3)), self.rstd[:, g, :]
        steps.then_wait(V.tensor_scalar(half, self.mv[:, g, :, 1], self.eps_value, -0.5, ALU.add, ALU.mult))
        dve.wait_ge(self.rstd_ready, n + 1)
        steps.then_wait(V.tensor_tensor(t1, half, r0, ALU.mult))
        steps.then_wait(V.tensor_tensor(half, t1, r0, ALU.mult))
        steps.then_wait(V.tensor_scalar(t1, half, 1.5, None, ALU.add))
        steps.then_wait(V.tensor_tensor(r, t1, r0, ALU.mult))
        for t in range(BT):
            last = V.tensor_scalar(dst(t), tile(t), self.mv[:, g, t, 0:1], self.newton[:, 2, t:t + 1],
                                   ALU.subtract, ALU.mult)
        return last


def experts(nc, name, weights, x, ident, eps, out_dram=None):
    with ExitStack() as ctx:
        def sb(n, shape, dt=F32):
            return ctx.enter_context(nc.sbuf_tensor(f"{name}_{n}", shape, dt))

        def sem(n):
            return ctx.enter_context(nc.semaphore(f"{name}_{n}"))

        def ps(n, shape, dt=F32):
            return ctx.enter_context(nc.psum_tensor(f"{name}_{n}", shape, dt))

        E, G, RANKED = EXPERTS, GROUPS, STACK_K
        SLOTS, R_SLOTS, LAG = 2, 5, 3
        gate, up, down, bias, earlier, pick, identb = (
            weights[n] for n in ("gate", "up", "down", "bias", "earlier", "pick", "identb"))
        ln = LayerNorm(name + "_ln", lambda n, shape: sb(n, shape), sem, eps[:, 0:1])
        xn = sb("xn", [P, 2, BT, D])
        xnT = sb("xnT", [P, 2, BLK])
        ex = sb("ex", [P, BT, E])
        one_ex = sb("one_ex", [P, BT, E])
        score = sb("score", [P, BT, E])
        biased = sb("biased", [P, BT, E])
        sums = sb("sums", [P, BT * G, 6])
        group = sb("group", [P, BT, G])
        g_more = sb("g_more", [P, BT, G, G], BF16)
        g_same = sb("g_same", [P, BT, G, G], BF16)
        g_rank = sb("g_rank", [P, BT, G])
        g_in = sb("g_in", [P, BT * G])
        masked = sb("masked", [P, BT, E])
        more = sb("more", [P, BT, E, E], BF16)
        same = sb("same", [P, BT, E, E], BF16)
        rank = sb("rank", [P, BT * E])
        wsel = sb("wsel", [P, BT * E])
        total = sb("total", [P, BT])
        inv = sb("inv", [P, BT])
        weight = sb("weight", [P, BT, E])
        wrest = sb("wrest", [P, BT, E])
        wparts = sb("wparts", [P, BT, RANKED], BF16)
        wT = sb("wT", [P, BLK], BF16)
        r = sb("r", [P, R_SLOTS, BLK])
        rw = sb("rw", [P, SLOTS, BLK])
        h = sb("h", [P, 2, CHUNKS, BLK])

        ps_x = ps("ps_x", [P, BLK])
        ps_wT = ps("ps_wT", [P, 2 * BLK], BF16)
        ps_u = ps("ps_u", [P, SLOTS, BLK])
        ps_w = ps("ps_w", [P, SLOTS, BLK])
        ps_y = ps("ps_y", [P, 2, BT, D])

        set_up = sem("set_up")
        ln_steps, route_steps = sem("ln_steps"), sem("route_steps")
        xn_ready, xT_ps, xnT_ready = sem("xn_ready"), sem("xT_ps"), sem("xnT_ready")
        gate_ps, ex_ready, wparts_ready, wT_ps, wT_ready = (
            sem("gate_ps"), sem("ex_ready"), sem("wparts_ready"), sem("wT_ps"), sem("wT_ready"))
        u_ps, w_ps, r_ready, rw_ready, h_ready = sem("u_ps"), sem("w_ps"), sem("r_ready"), sem("rw_ready"), sem("h_ready")
        y_ready, x_ready, stored = sem("y_ready"), sem("x_ready"), sem("stored")

        def blocks(eng, main):
            main(0, 0, True, 2)
            main(1, 1, False, 2)
            with eng.Fori(1, BLOCKS // 2 - 1) as i:
                for g in range(2):
                    main(2 * i + g, g, False, 2)
            main(BLOCKS - 2, 0, False, 1)
            main(BLOCKS - 1, 1, False, 0)

        block = ctx.enter_context(nc.Block())

        @block.sync
        def _(sp):
            if out_dram is not None:
                with sp.Fori(0, BLOCKS) as n:
                    sp.wait_ge(x_ready, n + 1)
                    sp.dma_start(out_dram[:, bass.ds(n * BT, BT), :],
                                 x[:, bass.ds(n * BT, BT), :]).then_inc(stored, 16)
                sp.wait_ge(stored, 16 * BLOCKS)

        @block.vector
        def _(dve):
            nc.vector.memset(wparts[:], 0.0).then_inc(set_up, 1)
            dve.wait_ge(set_up, 1)
            t3, t4 = "p t e -> p (t e)", "p (t g) e -> p t g e"
            dve.sem_inc(r_ready, SLOTS)
            dve.sem_inc(rw_ready, SLOTS)
            dve.sem_inc(h_ready, R_SLOTS)
            ROUTE_STEPS = 28

            def statistics(n, g):
                steps = Steps(dve, ln_steps, n * LayerNorm.STEPS)
                ln.statistics(nc, dve, steps, n, g, lambda t: x[:, n * BT + t, :])
                return steps

            def normalize(steps, n, g):
                ln.normalize(nc, dve, steps, n, g, lambda t: xn[:, g, t, :],
                             lambda t: x[:, n * BT + t, :]).then_inc(xn_ready, 1)

            def route(n):
                s = Steps(dve, route_steps, n * ROUTE_STEPS)
                V = nc.vector
                dve.wait_ge(ex_ready, n + 1)
                s.then_wait(V.tensor_scalar(one_ex[:], ex[:], 1.0, None, ALU.add))
                s.then_wait(V.reciprocal(score[:], one_ex[:]))
                s.then_wait(V.tensor_tensor(biased[:], score[:], bc(bias[:], 1, [P, BT, E]), ALU.add))
                yield
                four = biased[:].rearrange("p t (g e) -> p (t g) e", e=PER_GROUP)
                s.mark(V.tensor_tensor(sums[:, :, 0:3], four[:, :, 0:3], four[:, :, 1:4], ALU.add))
                s.mark(V.tensor_tensor(sums[:, :, 3:5], four[:, :, 0:2], four[:, :, 2:4], ALU.add))
                s.then_wait(V.tensor_tensor(sums[:, :, 5:6], four[:, :, 0:1], four[:, :, 3:4], ALU.add))
                s.then_wait(V.tensor_reduce(group[:].rearrange("p t g -> p (t g)"), sums[:], AX_X, ALU.max))
                yield
                sh = [P, BT, G, G]
                s.mark(V.tensor_tensor(g_more[:], bc(group[:], 2, sh), bc(group[:], 3, sh), ALU.is_gt))
                s.then_wait(V.tensor_tensor(g_same[:], bc(group[:], 2, sh), bc(group[:], 3, sh), ALU.is_equal))
                s.then_wait(V.tensor_tensor(g_same[:], g_same[:], bc(earlier[:, 0:G, 0:G], 1, sh), ALU.mult))
                s.then_wait(V.tensor_tensor(g_more[:], g_more[:], g_same[:], ALU.add))
                yield
                s.then_wait(V.tensor_reduce(g_rank[:], g_more[:], AX_X, ALU.add))
                s.then_wait(V.tensor_scalar(g_in[:], g_rank[:].rearrange("p t g -> p (t g)"), float(TOP_GROUPS), None,
                                            ALU.is_lt))
                s.then_wait(V.tensor_tensor(masked[:].rearrange("p t (g e) -> p (t g) e", e=PER_GROUP), four,
                                            bc(g_in[:], 2, [P, BT * G, PER_GROUP]), ALU.mult))
                yield
                sh = [P, BT, E, E]
                s.mark(V.tensor_tensor(more[:], bc(masked[:], 2, sh), bc(masked[:], 3, sh), ALU.is_gt))
                yield
                s.then_wait(V.tensor_tensor(same[:], bc(masked[:], 2, sh), bc(masked[:], 3, sh), ALU.is_equal))
                yield
                s.then_wait(V.tensor_tensor(same[:], same[:], bc(earlier[:], 1, sh), ALU.mult))
                s.then_wait(V.tensor_tensor(more[:], more[:], same[:], ALU.add))
                yield
                s.then_wait(V.tensor_reduce(rank[:].rearrange("p (t e) -> p t e", e=E), more[:], AX_X, ALU.add))
                s.then_wait(V.scalar_tensor_tensor(out=wsel[:], in0=rank[:], scalar=float(TOP_K),
                                                   in1=score[:].rearrange(t3), op0=ALU.is_lt, op1=ALU.mult))
                chosen = wsel[:].rearrange("p (t e) -> p t e", e=E)
                s.then_wait(V.tensor_reduce(total[:], chosen, AX_X, ALU.add))
                yield
                s.then_wait(V.tensor_scalar(inv[:], total[:], 1e-20, None, ALU.add))
                s.then_wait(V.reciprocal(total[:], inv[:]))
                s.then_wait(V.tensor_scalar(inv[:], total[:], ROUTED_SCALE, None, ALU.mult))
                s.then_wait(V.tensor_tensor(weight[:], chosen, bc(inv[:], 2, [P, BT, E]), ALU.mult))
                s.then_wait(V.tensor_copy(wparts[:, :, 0:E], weight[:]))
                yield
                s.then_wait(V.tensor_tensor(wrest[:], weight[:], wparts[:, :, 0:E], ALU.subtract))
                s.then_wait(V.tensor_copy(wparts[:, :, E:2 * E], wrest[:]))
                V.tensor_tensor(wparts[:, :, 2 * E:3 * E], wrest[:], wparts[:, :, E:2 * E],
                                ALU.subtract).then_inc(wparts_ready, 1)
                assert s.n == ROUTE_STEPS, s.n
                yield

            def add(n, g):
                dve.wait_ge(y_ready, n + 1)
                tiles = x[:, bass.ds(n * BT, BT), :]
                nc.vector.tensor_tensor(tiles, ps_y[:, g, :, :], tiles, ALU.add).then_inc(x_ready, 1)

            def main(n, g, first, ahead):
                routing = route(n + 1) if ahead else iter(())
                for c in range(ROUTED):
                    dve.wait_ge(r_ready, SLOTS + CHUNKS * n + c + 1)
                    dve.wait_ge(w_ps, ROUTED * n + c + 1)
                    before = c - SLOTS if c >= SLOTS else ROUTED + c - SLOTS - CHUNKS
                    dve.wait_ge(h_ready, R_SLOTS + CHUNKS * n + before + 1)
                    nc.vector.tensor_tensor(rw[:, c % SLOTS, :], r[:, c % R_SLOTS, :], ps_w[:, c % SLOTS, :],
                                            ALU.mult).then_inc(rw_ready, 1)
                    for _ in range(ROUTE_PIECES[c]):
                        next(routing, None)
                    if c == LAG and not first:
                        add(n - 1, 1 - g)
                    if c == 0 and ahead == 2:
                        steps = statistics(n + 2, g)
                    if c == 1 and ahead == 2:
                        normalize(steps, n + 2, g)
                assert next(routing, None) is None

            normalize(statistics(0, 0), 0, 0)
            normalize(statistics(1, 1), 1, 1)
            for _ in route(0):
                pass
            blocks(dve, main)
            add(BLOCKS - 1, 1)

        @block.scalar
        def _(act):
            nc.scalar.preload_act_table_set(ACT_TABLES)

            def turn(n, g):
                act.wait_ge(xT_ps, n + 1)
                nc.scalar.copy(xnT[:, g, :], ps_x[:]).then_inc(xnT_ready, 1)

            def exp_gate(n):
                act.wait_ge(gate_ps, n + 1)
                nc.scalar.activation(ex[:], ps_x[:].rearrange("p (t e) -> p t e", e=GATE_COLS)[:, :, 0:E], ACT.Exp,
                                     scale=-1.0).then_inc(ex_ready, 1)

            def turn_weights(n):
                act.wait_ge(wT_ps, n + 1)
                nc.scalar.copy(wT[0:RANKED, :], ps_wT[0:RANKED, 0:BLK]).then_inc(wT_ready, 1)

            def main(n, g, first, ahead):
                for c in range(CHUNKS):
                    act.wait_ge(u_ps, CHUNKS * n + c + 1)
                    act.wait_ge(h_ready, CHUNKS * n + c + 1)
                    nc.scalar.activation(r[:, c % R_SLOTS, :], ps_u[:, c % SLOTS, :], ACT.Relu).then_inc(r_ready, 1)
                    if c == TURN_AT and ahead:
                        turn(n + 1, 1 - g)
                    if c == 1 and ahead == 2:
                        ln.scale(nc, act, n + 2, g)
                    if c == GATES_AT and ahead:
                        exp_gate(n + 1)
                if ahead:
                    turn_weights(n + 1)

            ln.scale(nc, act, 0, 0)
            ln.scale(nc, act, 1, 1)
            turn(0, 0)
            exp_gate(0)
            turn_weights(0)
            blocks(act, main)

        @block.gpsimd
        def _(pool):
            def main(n, g, first, ahead):
                for c in range(CHUNKS):
                    slot = r[:, c % R_SLOTS, :]
                    if c < ROUTED:
                        pool.wait_ge(rw_ready, SLOTS + ROUTED * n + c + 1)
                        other = rw[:, c % SLOTS, :]
                    else:
                        pool.wait_ge(r_ready, SLOTS + CHUNKS * n + c + 1)
                        other = slot
                    nc.gpsimd.tensor_tensor(h[:, g, c, :], slot, other, ALU.mult).then_inc(h_ready, 1)

            blocks(pool, main)

        @block.tensor
        def _(pe):
            pe.wait_ge(set_up, 1)

            def turn(n, g):
                pe.wait_ge(xn_ready, n + 1)
                for t in range(BT):
                    last = nc.tensor.transpose(ps_x[:, t * P:(t + 1) * P], xn[:, g, t, :], ident[:])
                last.then_inc(xT_ps, 1)

            def gates(n, g):
                pe.wait_ge(xnT_ready, n + 1)
                for t in range(BT):
                    last = nc.tensor.matmul(ps_x[:, t * GATE_COLS:(t + 1) * GATE_COLS],
                                            xnT[:, g, t * P:(t + 1) * P], gate[:], start=True, stop=True)
                last.then_inc(gate_ps, 1)

            def turn_weights(n):
                pe.wait_ge(wparts_ready, n + 1)
                for t in range(BT):
                    last = nc.tensor.transpose(ps_wT[0:RANKED, t * P:(t + 1) * P], wparts[:, t, :], identb[:])
                last.then_inc(wT_ps, 1)

            def into_y(n, g, c):
                pe.wait_ge(h_ready, R_SLOTS + CHUNKS * n + c + 1)
                for t in range(BT):
                    last = nc.tensor.matmul(ps_y[:, g, t, :], h[:, g, c, t * P:(t + 1) * P], down[:, c, :],
                                            start=(c == 0 and t == 0), stop=(c == CHUNKS - 1),
                                            skip_group_check=True)
                if c == CHUNKS - 1:
                    last.then_inc(y_ready, 1)

            def main(n, g, first, ahead):
                for c in range(CHUNKS):
                    pe.wait_ge(r_ready, CHUNKS * n + c + 1)
                    nc.tensor.matmul(ps_u[:, c % SLOTS, :], up[:, c, :], xnT[:, g, :],
                                     start=True, stop=True).then_inc(u_ps, 1)
                    if c == 0:
                        pe.wait_ge(wT_ready, n + 1)
                    if c < ROUTED:
                        pe.wait_ge(rw_ready, ROUTED * n + c + 1)
                        nc.tensor.matmul(ps_w[:, c % SLOTS, :], pick[0:RANKED, c, :], wT[0:RANKED, :],
                                         start=True, stop=True).then_inc(w_ps, 1)
                    if c == TURN_AT and ahead:
                        turn(n + 1, 1 - g)
                    if c == GATES_AT and ahead:
                        gates(n + 1, 1 - g)
                    if c >= LAG:
                        into_y(n, g, c - LAG)
                    elif not first:
                        into_y(n - 1, 1 - g, CHUNKS - LAG + c)
                if ahead:
                    turn_weights(n + 1)

            turn(0, 0)
            gates(0, 0)
            turn_weights(0)
            blocks(pe, main)
            for c in range(CHUNKS - LAG, CHUNKS):
                into_y(BLOCKS - 1, 1, c)


def attend_b(nc, weights, x, ident, eps):
    with ExitStack() as ctx:
        def sb(n, shape, dt=F32):
            return ctx.enter_context(nc.sbuf_tensor("b_" + n, shape, dt))

        def sem(n):
            return ctx.enter_context(nc.semaphore("b_" + n))

        def ps(n, shape, dt=F32):
            return ctx.enter_context(nc.psum_tensor("b_" + n, shape, dt))

        w, wo, bias, rows, heads = (weights[n] for n in ("w", "wo", "bias", "rows", "heads"))
        ln1 = LayerNorm("ln1", lambda n, shape: sb(n, shape), sem, eps[:, 0:1])
        ln2 = LayerNorm("ln2", lambda n, shape: sb(n, shape), sem, eps[:, 1:2], B_EPS)
        z = sb("z", [P, 2, BT, D])
        zb = sb("zb", [P, TILES, D])
        zT = sb("zT", [P, 2, BLK])
        qk = sb("qk", [P, 2, BT, 2 * D])
        v = sb("v", [P, 2, BT, D])
        e = sb("e", [P, 2, BT, 2 * D])
        m = sb("m", [P, 2, BT, 2 * D])
        el = sb("el", [P, 2, BT, 2, D])
        sq = sb("sq", [P, 2, BT, D])
        norm = sb("norm", [P, 2, BT, HEADS])
        lnn = sb("lnn", [P, 2, BT, HEADS])
        rnorm = sb("rnorm", [P, 2, BT, HEADS])
        kn = sb("kn", [P, 2, BT, D])
        qT = sb("qT", [P, 2, BLK])
        vk = sb("vk", [P, D])
        vko = sb("vko", [P, D])
        y = sb("y", [P, 2, BT, D])
        yn = sb("yn", [P, 2, BT, D])

        ps_zT = ps("ps_zT", [P, BLK])
        ps_qT = ps("ps_qT", [P, BLK])
        ps_qkv = ps("ps_qkv", [P, BT, 512])
        ps_vk = ps("ps_vk", [P, 512])
        ps_o = ps("ps_o", [P, BT, D])

        ln1_steps, ln2_steps = sem("ln1_steps"), sem("ln2_steps")
        z_ready, zb_ready, zT_ps, zT_ready, qkv_ps, qk_ready, em_ready, el_ready, qT_ps, qT_ready = (
            sem(n) for n in ("z_ready", "zb_ready", "zT_ps", "zT_ready", "qkv_ps", "qk_ready", "em_ready",
                             "el_ready", "qT_ps", "qT_ready"))
        sq_ready, norm_ready, lnn_ready, rnorm_ready, kn_ready, vk_ps, vk_ready, vko_ps, vko_ready = (
            sem(n) for n in ("sq_ready", "norm_ready", "lnn_ready", "rnorm_ready", "kn_ready", "vk_ps", "vk_ready",
                             "vko_ps", "vko_ready"))
        o_ps, y_ready, yn_ready, beta_added, scaled, x_done = (
            sem(n) for n in ("o_ps", "y_ready", "yn_ready", "beta_added", "scaled", "x_done"))

        def turns(eng, turn):
            turn(-1, 0, (1,))
            turn(-1, 1, (1, 2))
            turn(0, 0, (1, 2, 3))
            turn(0, 1, (1, 2, 3))
            with eng.Fori(1, BATCH - 1) as b:
                for g in range(2):
                    turn(b, g, (1, 2, 3, 4))
            turn(BATCH - 1, 0, (2, 3, 4))
            turn(BATCH - 1, 1, (3, 4))
            turn(BATCH, 0, (4,))
            turn(BATCH, 1, (4,))

        def per_head(ap):
            return ap.rearrange("p t (h f) -> p (t h) f", f=HD)

        block = ctx.enter_context(nc.Block())

        @block.vector
        def _(dve):
            flat = "p t f -> p (t f)"

            def turn(b, g, stages):
                n = 2 * b + g
                nxt, o = n + 1, 1 - g
                if 1 in stages:
                    k1 = n + 2
                    steps1 = Steps(dve, ln1_steps, k1 * LayerNorm.STEPS)
                    xt = lambda t: x[:, k1 * BT + t, :]
                    ln1.statistics(nc, dve, steps1, k1, g, xt)
                if 3 in stages:
                    dve.wait_ge(em_ready, n + 1)
                    nc.vector.scalar_tensor_tensor(
                        out=el[:, g, :, :, :].rearrange("p t a d -> p (t a d)"), in0=e[:, g, :, :].rearrange(flat),
                        scalar=1.0, in1=m[:, g, :, :].rearrange(flat), op0=ALU.min,
                        op1=ALU.add).then_inc(el_ready, 1)
                if 4 in stages and g == 0:
                    dve.wait_ge(vk_ps, b)
                    nc.vector.tensor_tensor(vk[:], ps_vk[:, 0:D], heads[:], ALU.mult).then_inc(vk_ready, 1)
                if 1 in stages:
                    if 3 in stages:
                        dve.wait_ge(zb_ready, n + 1)
                    ln1.normalize(nc, dve, steps1, k1, g, lambda t: z[:, g, t, :], xt).then_inc(z_ready, 1)
                if 4 in stages:
                    k4 = n - 2
                    dve.wait_ge(o_ps, k4 + 1)
                    dve.wait_ge(zb_ready, k4 + 1)
                    nc.vector.tensor_tensor(y[:, g, :, :], zb[:, bass.ds(k4 * BT, BT), :], ps_o[:],
                                            ALU.add).then_inc(y_ready, 1)
                    dve.wait_ge(y_ready, k4 + 1)
                    steps2 = Steps(dve, ln2_steps, k4 * LayerNorm.STEPS)
                    yt = lambda t: y[:, g, t, :]
                    ln2.statistics(nc, dve, steps2, k4, g, yt)
                if 3 in stages:
                    dve.wait_ge(sq_ready, n + 1)
                    nc.vector.tensor_reduce(norm[:, g, :, :].rearrange("p t h -> p (t h)"), per_head(sq[:, g, :, :]),
                                            AX_X, ALU.add).then_inc(norm_ready, 1)
                if 2 in stages:
                    dve.wait_ge(qkv_ps, nxt + 1)
                    nc.vector.tensor_tensor(v[:, o, :, :], ps_qkv[:, :, 2 * D:3 * D],
                                            bc(bias[:, 2, :], 1, [P, BT, D]), ALU.add)
                    nc.vector.tensor_tensor(qk[:, o, :, :], ps_qkv[:, :, 0:2 * D],
                                            bc(bias[:, 0:2, :].rearrange("p a d -> p (a d)"), 1, [P, BT, 2 * D]),
                                            ALU.add).then_inc(qk_ready, 1)
                if 4 in stages:
                    if 3 not in stages:
                        dve.wait_ge(x_done, k4 - 1)
                    ln2.normalize(nc, dve, steps2, k4, g, lambda t: yn[:, g, t, :], yt).then_inc(yn_ready, 1)
                if 3 in stages:
                    dve.wait_ge(rnorm_ready, n + 1)
                    nc.vector.tensor_tensor(kn[:, g, :, :].rearrange("p t (h f) -> p (t h) f", f=HD),
                                            el[:, g, :, 1, :].rearrange("p t (h f) -> p t h f", f=HD),
                                            bc(rnorm[:, g, :, :].rearrange("p t h -> p (t h)"), 2, [P, BT * HEADS, HD]),
                                            ALU.mult).then_inc(kn_ready, 1)

            turns(dve, turn)

        @block.scalar
        def _(act):
            nc.scalar.preload_act_table_set(ACT_TABLES)

            def turn(b, g, stages):
                n = 2 * b + g
                nxt, o = n + 1, 1 - g
                if 2 in stages:
                    act.wait_ge(zT_ps, nxt + 1)
                    nc.scalar.copy(zT[:, o, :], ps_zT[:]).then_inc(zT_ready, 1)
                if 1 in stages:
                    ln1.scale(nc, act, n + 2, g)
                if 4 in stages and g == 0:
                    act.wait_ge(vko_ps, b)
                    nc.scalar.copy(vko[:], ps_vk[:, D:2 * D]).then_inc(vko_ready, 1)
                if 3 in stages:
                    act.wait_ge(qT_ps, n + 1)
                    nc.scalar.copy(qT[:, g, :], ps_qT[:]).then_inc(qT_ready, 1)
                if 4 in stages:
                    ln2.scale(nc, act, n - 2, g)
                if 3 in stages:
                    act.wait_ge(norm_ready, n + 1)
                    nc.scalar.activation(lnn[:, g, :, :], norm[:, g, :, :], ACT.Ln, bias=eps[:, 1:2]).then_inc(lnn_ready, 1)
                    act.wait_ge(lnn_ready, n + 1)
                    nc.scalar.activation(rnorm[:, g, :, :], lnn[:, g, :, :], ACT.Exp, scale=-0.5).then_inc(rnorm_ready, 1)
                if 2 in stages:
                    act.wait_ge(qk_ready, nxt + 1)
                    nc.scalar.activation(e[:, o, :, :], qk[:, o, :, :], ACT.Exp)
                    nc.scalar.activation(m[:, o, :, :], qk[:, o, :, :], ACT.Relu).then_inc(em_ready, 1)

            turns(act, turn)

        @block.gpsimd
        def _(pool):
            def turn(b, g, stages):
                n = 2 * b + g
                if 3 in stages:
                    pool.wait_ge(el_ready, n + 1)
                    nc.gpsimd.tensor_tensor(sq[:, g, :, :], el[:, g, :, 1, :], el[:, g, :, 1, :],
                                            ALU.mult).then_inc(sq_ready, 1)
                if 1 in stages:
                    tiles = bass.ds((n + 2) * BT, BT)
                    pool.wait_ge(z_ready, n + 3)
                    nc.gpsimd.tensor_tensor(zb[:, tiles, :], z[:, g, :, :], bc(rows[:, 0, :], 1, [P, BT, D]),
                                            ALU.add).then_inc(zb_ready, 1)
                    nc.gpsimd.tensor_tensor(x[:, tiles, :], x[:, tiles, :], bc(rows[:, 2, :], 1, [P, BT, D]),
                                            ALU.add).then_inc(beta_added, 1)
                if 4 in stages:
                    k4 = n - 2
                    tiles = bass.ds(k4 * BT, BT)
                    pool.wait_ge(yn_ready, k4 + 1)
                    nc.gpsimd.tensor_tensor(yn[:, g, :, :], yn[:, g, :, :], bc(rows[:, 1, :], 1, [P, BT, D]),
                                            ALU.mult).then_inc(scaled, 1)
                    pool.wait_ge(beta_added, k4 + 1)
                    pool.wait_ge(scaled, k4 + 1)
                    nc.gpsimd.tensor_tensor(x[:, tiles, :], x[:, tiles, :], yn[:, g, :, :],
                                            ALU.add).then_inc(x_done, 1)

            turns(pool, turn)

        @block.tensor
        def _(pe):
            def turn(b, g, stages):
                n = 2 * b + g
                nxt, o = n + 1, 1 - g
                if 2 in stages:
                    pe.wait_ge(z_ready, nxt + 1)
                    for t in range(BT):
                        last = nc.tensor.transpose(ps_zT[:, t * P:(t + 1) * P], z[:, o, t, :], ident[:])
                    last.then_inc(zT_ps, 1)
                    pe.wait_ge(zT_ready, nxt + 1)
                    if 3 in stages:
                        pe.wait_ge(qk_ready, nxt)
                    for t in range(BT):
                        last = nc.tensor.matmul(ps_qkv[:, t, 0:3 * D], zT[:, o, t * P:(t + 1) * P],
                                                w[:].rearrange("p a d -> p (a d)"), start=True, stop=True)
                    last.then_inc(qkv_ps, 1)
                if 4 in stages:
                    if g == 0:
                        pe.wait_ge(vk_ready, b)
                        nc.tensor.matmul(ps_vk[:, D:2 * D], vk[:], wo[:], start=True, stop=True).then_inc(vko_ps, 1)
                        pe.wait_ge(vko_ready, b)
                    if 3 not in stages and g == 1:
                        pe.wait_ge(y_ready, n - 2)
                    for t in range(BT):
                        last = nc.tensor.matmul(ps_o[:, t, :], qT[:, g, t * P:(t + 1) * P], vko[:],
                                                start=True, stop=True)
                    last.then_inc(o_ps, 1)
                if 3 in stages:
                    if 2 not in stages:
                        pe.wait_ge(qT_ready, n)
                    pe.wait_ge(el_ready, n + 1)
                    for t in range(BT):
                        last = nc.tensor.transpose(ps_qT[:, t * P:(t + 1) * P], el[:, g, t, 0, :], ident[:])
                    last.then_inc(qT_ps, 1)
                    pe.wait_ge(kn_ready, n + 1)
                    for t in range(BT):
                        last = nc.tensor.matmul(ps_vk[:, 0:D], v[:, g, t, :], kn[:, g, t, :],
                                                start=(g == 0 and t == 0), stop=(g == 1 and t == BT - 1))
                    if g == 1:
                        last.then_inc(vk_ps, 1)

            turns(pe, turn)


def constants():
    import numpy as np

    f32 = np.float32
    half = HD // 2
    theta = (f32(1.0) / np.power(f32(1250), np.arange(half, dtype=f32) / f32(half))).astype(f32)
    angles = (np.arange(SEQ, dtype=f32)[:, None] * theta[None, :]).astype(f32)
    cos, sin = np.cos(angles).astype(f32), np.sin(angles).astype(f32)

    def table(even, odd):
        pairs = np.stack([even, odd], axis=-1).reshape(SEQ_TILES, P, HD)
        return np.ascontiguousarray(pairs.transpose(1, 0, 2))

    before = np.tril(np.ones((EXPERTS, EXPERTS), f32), -1)
    pick = np.zeros((P, ROUTED + 1, P), f32)
    for c in range(ROUTED):
        for part in range(PARTS):
            for a in range(2):
                pick[part * EXPERTS + 2 * c + a, c, a * INTER:(a + 1) * INTER] = 1
    pick[:, ROUTED, :] = np.eye(P)
    head = np.arange(D) // HD
    bf16 = mybir.dt.np(BF16)
    return {"earlier": np.ascontiguousarray(np.broadcast_to(before, (P, EXPERTS, EXPERTS))).astype(bf16),
            "pick": pick.astype(bf16), "heads": (head[:, None] == head[None, :]).astype(f32),
            "ident": np.eye(P, dtype=f32), "cos": table(cos, cos), "sin": table(-sin, sin)}


def kernel(**inputs):
    import concourse.bacc as bacc
    import numpy as np
    from concourse.bass_utils import run_bass_kernel_spmd as run

    a = {name.split("_", 1)[1]: np.asarray(array) for name, array in inputs.items()}
    c = constants()
    arrays = {
        "x_in": a["attn_a_x"], "w_qkv": a["attn_a_w_qkv"], "b_qkv": a["attn_a_b_qkv"],
        "w_out": a["attn_a_w_out"], "b_out": a["attn_a_b_out"],
        "Wq": a["attn_b_Wq"], "bq": a["attn_b_bq"], "Wk": a["attn_b_Wk"], "bk": a["attn_b_bk"],
        "Wv": a["attn_b_Wv"], "bv": a["attn_b_bv"], "Wo": a["attn_b_Wo"], "bo": a["attn_b_bo"],
        "gamma": a["attn_b_gamma"], "beta": a["attn_b_beta"],
        "gate_t": a["ffn_gate_w"].T, "bias_e": a["ffn_bias_e"],
        "up_t": np.concatenate([a["ffn_up_w"].reshape(EXPERTS * INTER, D), a["ffn_shared_up"]]).T,
        "down_t": np.concatenate([a["ffn_down_w"].transpose(0, 2, 1).reshape(EXPERTS * INTER, D),
                                  a["ffn_shared_down"].T]),
        "ident_in": c["ident"], "cos_in": c["cos"], "sin_in": c["sin"],
        "earlier_in": c["earlier"], "pick_in": c["pick"], "heads_in": c["heads"],
    }
    arrays = {name: np.ascontiguousarray(array) for name, array in arrays.items()}
    nc = bacc.Bacc("TRN2", target_bir_lowering=False, num_devices=1)
    args = {name: nc.dram_tensor(f"in_{name}_dram", array.shape, mybir.dt.from_np(array.dtype),
                                 kind="ExternalInput").ap() for name, array in arrays.items()}
    out = nc.dram_tensor("out_0_dram", (BATCH, SEQ, D), F32, kind="ExternalOutput").ap()
    hybrid_kernel(nc, out=out, **args)
    r = run(nc, [{f"in_{name}_dram": array for name, array in arrays.items()}], core_ids=[0])
    return r.results[0]["out_0_dram"]
```
